# Optimizing a Trainium2 kernel written in Bass

```python
import numpy as np
import jax
import jax.numpy as jnp

def _softmax(x, axis=-1):
    return jax.nn.softmax(x, axis=axis)

def _gelu(x):
    return jax.nn.gelu(x, approximate=True)

def _silu(x):
    return jax.nn.silu(x)

def _sigmoid(x):
    return jax.nn.sigmoid(x)

def _layernorm(x, axis=-1, eps=1e-05):
    m = jnp.mean(x, axis=axis, keepdims=True)
    v = jnp.var(x, axis=axis, keepdims=True)
    return (x - m) / jnp.sqrt(v + eps)

def _scatter_add(tgt, idx, src, axis=0):
    return tgt.at[idx].add(src)

def _segment_sum(src, seg, n):
    return jax.ops.segment_sum(src, seg, n)
kernel_name = 'mk_gnn_resnorm_d4_gnn_r16_6b7445'

def setup_inputs(seed: int=0):
    np.random.seed(seed)
    _w = jnp.asarray

    def _rec_inputs():
        import jax
        import jax.numpy as jnp
        _gk = jax.random.key(seed)
        x = -0.000202 + 1 * jax.random.normal(jax.random.fold_in(_gk, 1), (3125, 128), jnp.float32)
        _s = jax.random.randint(jax.random.fold_in(_gk, 2), (50000,), 0, 3125, jnp.int32)
        _d = jax.random.randint(jax.random.fold_in(_gk, 3), (50000,), 0, 3125, jnp.int32)
        _loop = jnp.arange(3125, dtype=jnp.int32)
        src = jnp.concatenate([_s, _d, _loop])
        dst = jnp.concatenate([_d, _s, _loop])
        _o = jnp.argsort(dst, stable=True)
        src = src[_o]
        dst = dst[_o]
        edge_attr_128 = 2.93046e-05 + 1.00006 * jax.random.normal(jax.random.fold_in(_gk, 12), (103125, 128), jnp.float32)
        edge_type_4 = jax.random.randint(jax.random.fold_in(_gk, 14), (103125,), 0, 4, jnp.int32)
        edge_weight = jax.random.uniform(jax.random.fold_in(_gk, 15), (103125,), jnp.float32, 0.0, 0.999998)
        return (x, src, dst, edge_attr_128, edge_type_4, edge_weight)
    x, src, dst, edge_attr_128, edge_type_4, edge_weight = _rec_inputs()

    def _L0_gnn_setup():
        import jax, jax.numpy as jnp
        import numpy as np
        NUM_USERS = 3125
        EMBED_DIM = 128
        NUM_EDGES = 50000
        key = jax.random.key(seed)
        k1, k2, k3, k4, k5 = jax.random.split(key, 5)
        user_emb = jax.random.normal(k1, (NUM_USERS, EMBED_DIM), dtype=jnp.float32)
        limit = float(np.sqrt(6.0 / (EMBED_DIM + EMBED_DIM)))
        social_weight = jax.random.uniform(k2, (EMBED_DIM, EMBED_DIM), dtype=jnp.float32, minval=-limit, maxval=limit)
        rows = jax.random.randint(k3, (NUM_EDGES,), 0, NUM_USERS)
        cols = jax.random.randint(k4, (NUM_EDGES,), 0, NUM_USERS)
        vals = jax.random.uniform(k5, (NUM_EDGES,), dtype=jnp.float32)
        return {'user_emb': user_emb, 'social_weight': social_weight, 'rows': rows, 'cols': cols, 'vals': vals}
    _L0_gnn_all = _L0_gnn_setup()
    _L0_gnn_in = {k: v for k, v in _L0_gnn_all.items() if k in ('social_weight',)}
    del _L0_gnn_all

    def _L1_gnn_setup():
        import jax, jax.numpy as jnp
        import numpy as np
        N = 6250
        E = 100000
        D = 128
        G = 128
        K = 4
        STEPS = 3

        def _gru_cell(a, h, W_ih, b_ih, W_hh, b_hh):
            gi = a @ W_ih.T + b_ih
            gh = h @ W_hh.T + b_hh
            ir, iz, in_ = jnp.split(gi, 3, axis=1)
            hr, hz, hn = jnp.split(gh, 3, axis=1)
            r = jax.nn.sigmoid(ir + hr)
            z = jax.nn.sigmoid(iz + hz)
            n = jnp.tanh(in_ + r * hn)
            return (1.0 - z) * n + z * h
        key = jax.random.key(seed)
        ks = jax.random.split(key, 16)
        s = 0.05
        return {'features': jax.random.normal(ks[0], (N, D), jnp.float32), 'src': jax.random.randint(ks[1], (E,), 0, N, jnp.int32), 'dst': jax.random.randint(ks[2], (E,), 0, N, jnp.int32), 'etypes': jax.random.randint(ks[3], (E,), 0, K, jnp.int32), 'W_et': jax.random.normal(ks[4], (K, D, D), jnp.float32) * s, 'b_et': jax.random.normal(ks[5], (K, D), jnp.float32) * s, 'W_ih': jax.random.normal(ks[6], (3 * D, D), jnp.float32) * s, 'b_ih': jax.random.normal(ks[7], (3 * D,), jnp.float32) * s, 'W_hh': jax.random.normal(ks[8], (3 * D, D), jnp.float32) * s, 'b_hh': jax.random.normal(ks[9], (3 * D,), jnp.float32) * s, 'i_w': jax.random.normal(ks[10], (G, D + D), jnp.float32) * s, 'i_b': jax.random.normal(ks[11], (G,), jnp.float32) * s, 'j_w': jax.random.normal(ks[12], (G, D), jnp.float32) * s, 'j_b': jax.random.normal(ks[13], (G,), jnp.float32) * s}
    _L1_gnn_all = _L1_gnn_setup()
    _L1_gnn_in = {k: v for k, v in _L1_gnn_all.items() if k in ('W_et', 'b_et', 'W_ih', 'b_ih', 'W_hh', 'b_hh', 'i_w', 'i_b', 'j_w', 'j_b')}
    del _L1_gnn_all

    def _L2_gnn_setup():
        import jax, jax.numpy as jnp
        import numpy as np
        N_NODES = 6250
        N_EDGES = 100000
        D = 128

        def mean_agg(x, src, dst, n):
            s = jax.ops.segment_sum(x[src], dst, num_segments=n)
            deg = jax.ops.segment_sum(jnp.ones(src.shape[0], x.dtype), dst, num_segments=n)
            return s / jnp.maximum(deg, 1.0)[:, None]

        def gin_layer(x, Wa, ba, Wb, bb):
            h = x @ Wa.T + ba
            h = h @ Wb.T + bb
            return jax.nn.relu(h)
        key = jax.random.key(seed)
        ks = jax.random.split(key, 8)
        sc = 1.0 / np.sqrt(D)
        return {'features': jax.random.normal(ks[0], (N_NODES, D), jnp.float32), 'src': jax.random.randint(ks[1], (N_EDGES,), 0, N_NODES, jnp.int32), 'dst': jax.random.randint(ks[2], (N_EDGES,), 0, N_NODES, jnp.int32), 'W1a': jax.random.normal(ks[3], (D, D), jnp.float32) * sc, 'b1a': jnp.zeros((D,), jnp.float32), 'W1b': jax.random.normal(ks[4], (D, D), jnp.float32) * sc, 'b1b': jnp.zeros((D,), jnp.float32), 'W2a': jax.random.normal(ks[5], (D, D), jnp.float32) * sc, 'b2a': jnp.zeros((D,), jnp.float32), 'W2b': jax.random.normal(ks[6], (D, D), jnp.float32) * sc, 'b2b': jnp.zeros((D,), jnp.float32)}
    _L2_gnn_all = _L2_gnn_setup()
    _L2_gnn_in = {k: v for k, v in _L2_gnn_all.items() if k in ('W1a', 'b1a', 'W1b', 'b1b', 'W2a', 'b2a', 'W2b', 'b2b')}
    del _L2_gnn_all

    def _L3_gnn_setup():
        import jax, jax.numpy as jnp
        import numpy as np
        N_NODES = 625
        D = 128
        N_EDGES = 40000
        key = jax.random.key(seed)
        ks = jax.random.split(key, 14)
        x = jax.random.normal(ks[0], (N_NODES, D), dtype=jnp.float32)
        edge_index = jax.random.randint(ks[1], (2, N_EDGES), 0, N_NODES, dtype=jnp.int64)
        edge_attr = jax.random.normal(ks[2], (N_EDGES, D), dtype=jnp.float32)
        s = 1.0 / np.sqrt(D)

        def lin(kw, kb):
            W = jax.random.uniform(kw, (D, D), dtype=jnp.float32, minval=-s, maxval=s)
            b = jax.random.uniform(kb, (D,), dtype=jnp.float32, minval=-s, maxval=s)
            return (W, b)
        WA, bA = lin(ks[3], ks[4])
        WB, bB = lin(ks[5], ks[6])
        WC, bC = lin(ks[7], ks[8])
        WE, bE = lin(ks[9], ks[10])
        Wres, bres = lin(ks[11], ks[12])
        return {'x': x, 'edge_index': edge_index, 'edge_attr': edge_attr, 'WA': WA, 'bA': bA, 'WB': WB, 'bB': bB, 'WC': WC, 'bC': bC, 'WE': WE, 'bE': bE, 'Wres': Wres, 'bres': bres}
    _L3_gnn_all = _L3_gnn_setup()
    _L3_gnn_in = {k: v for k, v in _L3_gnn_all.items() if k in ('WA', 'bA', 'WB', 'bB', 'WC', 'bC', 'WE', 'bE', 'Wres', 'bres')}
    del _L3_gnn_all
    return {'x': x, 'src': src, 'dst': dst, 'edge_attr_128': edge_attr_128, 'edge_type_4': edge_type_4, 'edge_weight': edge_weight, 'L0_gnn_social_weight': _L0_gnn_in['social_weight'], 'L1_gnn_W_et': _L1_gnn_in['W_et'], 'L1_gnn_b_et': _L1_gnn_in['b_et'], 'L1_gnn_W_ih': _L1_gnn_in['W_ih'], 'L1_gnn_b_ih': _L1_gnn_in['b_ih'], 'L1_gnn_W_hh': _L1_gnn_in['W_hh'], 'L1_gnn_b_hh': _L1_gnn_in['b_hh'], 'L1_gnn_i_w': _L1_gnn_in['i_w'], 'L1_gnn_i_b': _L1_gnn_in['i_b'], 'L1_gnn_j_w': _L1_gnn_in['j_w'], 'L1_gnn_j_b': _L1_gnn_in['j_b'], 'L2_gnn_W1a': _L2_gnn_in['W1a'], 'L2_gnn_b1a': _L2_gnn_in['b1a'], 'L2_gnn_W1b': _L2_gnn_in['W1b'], 'L2_gnn_b1b': _L2_gnn_in['b1b'], 'L2_gnn_W2a': _L2_gnn_in['W2a'], 'L2_gnn_b2a': _L2_gnn_in['b2a'], 'L2_gnn_W2b': _L2_gnn_in['W2b'], 'L2_gnn_b2b': _L2_gnn_in['b2b'], 'L3_gnn_WA': _L3_gnn_in['WA'], 'L3_gnn_bA': _L3_gnn_in['bA'], 'L3_gnn_WB': _L3_gnn_in['WB'], 'L3_gnn_bB': _L3_gnn_in['bB'], 'L3_gnn_WC': _L3_gnn_in['WC'], 'L3_gnn_bC': _L3_gnn_in['bC'], 'L3_gnn_WE': _L3_gnn_in['WE'], 'L3_gnn_bE': _L3_gnn_in['bE'], 'L3_gnn_Wres': _L3_gnn_in['Wres'], 'L3_gnn_bres': _L3_gnn_in['bres']}

def reference(x, src, dst, edge_attr_128, edge_type_4, edge_weight, L0_gnn_social_weight, L1_gnn_W_et, L1_gnn_b_et, L1_gnn_W_ih, L1_gnn_b_ih, L1_gnn_W_hh, L1_gnn_b_hh, L1_gnn_i_w, L1_gnn_i_b, L1_gnn_j_w, L1_gnn_j_b, L2_gnn_W1a, L2_gnn_b1a, L2_gnn_W1b, L2_gnn_b1b, L2_gnn_W2a, L2_gnn_b2a, L2_gnn_W2b, L2_gnn_b2b, L3_gnn_WA, L3_gnn_bA, L3_gnn_WB, L3_gnn_bB, L3_gnn_WC, L3_gnn_bC, L3_gnn_WE, L3_gnn_bE, L3_gnn_Wres, L3_gnn_bres):
    import jax
    import jax.numpy as jnp

    def _L0_gnn_ref(user_emb, social_weight, rows, cols, vals):
        import jax, jax.numpy as jnp
        import numpy as np
        NUM_USERS = 3125
        EMBED_DIM = 128
        NUM_EDGES = 50000
        weighted = jnp.matmul(user_emb, social_weight)
        gathered = weighted[cols] * vals[:, None]
        neighbor = jax.ops.segment_sum(gathered, rows, num_segments=user_emb.shape[0])
        return user_emb + neighbor

    def _L1_gnn_ref(features, src, dst, etypes, W_et, b_et, W_ih, b_ih, W_hh, b_hh, i_w, i_b, j_w, j_b):
        import jax, jax.numpy as jnp
        import numpy as np
        N = 6250
        E = 100000
        D = 128
        G = 128
        K = 4
        STEPS = 3

        def _gru_cell(a, h, W_ih, b_ih, W_hh, b_hh):
            gi = a @ W_ih.T + b_ih
            gh = h @ W_hh.T + b_hh
            ir, iz, in_ = jnp.split(gi, 3, axis=1)
            hr, hz, hn = jnp.split(gh, 3, axis=1)
            r = jax.nn.sigmoid(ir + hr)
            z = jax.nn.sigmoid(iz + hz)
            n = jnp.tanh(in_ + r * hn)
            return (1.0 - z) * n + z * h
        n_nodes = features.shape[0]
        h = features
        for _ in range(STEPS):
            t = jnp.einsum('nd,kod->kno', h, W_et) + b_et[:, None, :]
            msg = t[etypes, src]
            a = jax.ops.segment_sum(msg, dst, num_segments=n_nodes)
            h = _gru_cell(a, h, W_ih, b_ih, W_hh, b_hh)
        gate = jax.nn.sigmoid(jnp.concatenate([h, features], axis=1) @ i_w.T + i_b)
        return gate * (h @ j_w.T + j_b)

    def _L2_gnn_ref(features, src, dst, W1a, b1a, W1b, b1b, W2a, b2a, W2b, b2b):
        import jax, jax.numpy as jnp
        import numpy as np
        N_NODES = 6250
        N_EDGES = 100000
        D = 128

        def mean_agg(x, src, dst, n):
            s = jax.ops.segment_sum(x[src], dst, num_segments=n)
            deg = jax.ops.segment_sum(jnp.ones(src.shape[0], x.dtype), dst, num_segments=n)
            return s / jnp.maximum(deg, 1.0)[:, None]

        def gin_layer(x, Wa, ba, Wb, bb):
            h = x @ Wa.T + ba
            h = h @ Wb.T + bb
            return jax.nn.relu(h)
        n = features.shape[0]
        h = features + mean_agg(features, src, dst, n)
        h = gin_layer(h, W1a, b1a, W1b, b1b)
        h = jax.nn.relu(h)
        h2 = h + mean_agg(h, src, dst, n)
        out = gin_layer(h2, W2a, b2a, W2b, b2b)
        return out

    def _L3_gnn_ref(x, edge_index, edge_attr, WA, bA, WB, bB, WC, bC, WE, bE, Wres, bres):
        import jax, jax.numpy as jnp
        import numpy as np
        N_NODES = 625
        D = 128
        N_EDGES = 40000
        row, col = (edge_index[0], edge_index[1])
        Bx = x @ WB + bB
        Cx = x @ WC + bC
        Ax = x @ WA + bA
        m = Bx[row] + Cx[col] + (edge_attr @ WE + bE)
        m = jax.nn.sigmoid(m) * Ax[row]
        agg = jax.ops.segment_sum(m, col, num_segments=x.shape[0])
        return jax.nn.relu(agg + (x @ Wres + bres))
    edge_index = jnp.stack([src, dst])
    x = _layernorm(x + _L0_gnn_ref(x, L0_gnn_social_weight, src, dst, edge_weight), axis=-1)
    x = _layernorm(x + _L1_gnn_ref(x, src, dst, edge_type_4, L1_gnn_W_et, L1_gnn_b_et, L1_gnn_W_ih, L1_gnn_b_ih, L1_gnn_W_hh, L1_gnn_b_hh, L1_gnn_i_w, L1_gnn_i_b, L1_gnn_j_w, L1_gnn_j_b), axis=-1)
    x = _layernorm(x + _L2_gnn_ref(x, src, dst, L2_gnn_W1a, L2_gnn_b1a, L2_gnn_W1b, L2_gnn_b1b, L2_gnn_W2a, L2_gnn_b2a, L2_gnn_W2b, L2_gnn_b2b), axis=-1)
    x = _layernorm(x + _L3_gnn_ref(x, edge_index, edge_attr_128, L3_gnn_WA, L3_gnn_bA, L3_gnn_WB, L3_gnn_bB, L3_gnn_WC, L3_gnn_bC, L3_gnn_WE, L3_gnn_bE, L3_gnn_Wres, L3_gnn_bres), axis=-1)
    return x

_drawn_inputs = setup_inputs


def setup_inputs(seed=0):
    import zlib

    import numpy as np

    out = dict(_drawn_inputs(seed))
    spreads = {'L2_gnn_b1a': (0.0, 0.1),
     'L2_gnn_b1b': (0.0, 0.1),
     'L2_gnn_b2a': (0.0, 0.1),
     'L2_gnn_b2b': (0.0, 0.1)}
    factors = {'L1_gnn_b_ih': 2.747, 'L1_gnn_b_hh': 3.522, 'L1_gnn_i_b': 7.68, 'L3_gnn_bres': 4.948}
    for name, (base, spread) in spreads.items():
        noise = np.random.default_rng([zlib.crc32(name.encode()), seed]).standard_normal(out[name].shape)
        drawn = base * np.exp(spread * noise) if base else spread * noise
        out[name] = jnp.asarray(drawn.astype(out[name].dtype))
    for name, factor in factors.items():
        out[name] = (out[name] * factor).astype(out[name].dtype)
    return out
```

```python
from contextlib import ExitStack

import numpy as np
import concourse.bass as bass
from concourse import mybir

F32 = mybir.dt.float32
I32 = mybir.dt.int32
BF16 = mybir.dt.bfloat16
ALU = mybir.AluOpType
ACT = mybir.ActivationFunctionType
AX = mybir.AxisListType
RMAX = bass.bass_isa.ReduceOp.max

N, D, E, K = 3125, 128, 103125, 4
P = 128
TN = 125
NT = N // TN
W = 34
WIN = W * P
RMAXN = -(-E // WIN)
NTAB = (RMAXN + 1) * NT
RING = W // 2
NCH = 8
CH = 392
NP = NCH * CH
BR, BC = 33, 25
BIG = float(E + 1)
EPS = 1e-5
PRE_LAG, MUL_LAG, S_LAG = 2, 3, 5

WNAMES = ["w0"] + [f"wet{k}" for k in range(K)] + ["ih_r", "ih_z", "ih_n", "hh_r", "hh_z", "hh_n", "iw_h", "iw_f", "jw",
          "w1a", "w1b", "w2a", "w2b", "wb", "wa", "wc", "we", "wres"]
BNAMES = ["bih_r", "bih_z", "bih_n", "bhh_r", "bhh_z", "bhh_n", "ib", "jb", "b1a", "b1b", "b2a", "b2b", "bres"]
RNAMES = [f"bet{k}" for k in range(K)] + ["zero", "ba", "bb", "bc", "be"]


class Shared:
    pass


class Sems:

    def __init__(self, nc, ctx):
        self.nc, self.ctx, self.by_name = nc, ctx, {}

    def __call__(self, name):
        if name not in self.by_name:
            self.by_name[name] = self.ctx.enter_context(self.nc.semaphore(name))
        return self.by_name[name]

    def clear(self):
        nums = [s.num for s in self.by_name.values()]
        self.nc.sync.sem_clear(range(min(nums), max(nums) + 1))
        self.nc.all_engine_barrier()


def setup_phase(nc, g, sem):
    loaded, blocks_in = sem("loaded"), sem("blocks_in")
    made, chain, reduced = sem("made"), sem("chain"), sem("reduced")
    n_iota = 6
    with nc.Block() as block:
        @block.sync
        def _(sp):
            sp.dma_start(g.dblk[0:TN, :], g.dst.rearrange("(p f) -> p f", p=TN)).then_inc(blocks_in, 16)
            sp.dma_start(g.w[:, :], g.d_w).then_inc(loaded, 16)
            sp.dma_start(g.b[:, :], g.d_b).then_inc(loaded, 16)
            sp.dma_start(g.brow[:, :], g.d_brow.broadcast_to((P, len(RNAMES) * D))).then_inc(loaded, 16)
            sp.dma_start(g.X[:, :], g.d_xT).then_inc(loaded, 16)
            sp.wait_ge(loaded, 64)

        @block.gpsimd
        def _(pool):
            io = dict(allow_small_or_imprecise_dtypes=True)
            pool.iota(g.iota1[:, :], [[1, TN]], base=1, channel_multiplier=0, **io).then_inc(made, 1)
            pool.iota(g.eidx[:, :], [[P, W]], base=0, channel_multiplier=1, **io).then_inc(made, 1)
            pool.iota(g.ident[:, :], [[1, P]], base=0, channel_multiplier=-1, **io).then_inc(made, 1)
            pool.iota(g.blk[:, :], [[BC, BR]], base=0, channel_multiplier=BR * BC, **io).then_inc(made, 1)
            pool.iota(g.dtlo[:, :], [[TN, NT]], base=0, channel_multiplier=0, **io).then_inc(made, 1)
            pool.iota(g.rnd[:, :], [[WIN, RMAXN + 1]], base=0, channel_multiplier=0, **io).then_inc(made, 1)
            pool.wait_ge(reduced, 1)
            pool.partition_all_reduce(g.red[:, :], g.part[:, :], P, RMAX).then_inc(reduced, 1)

        @block.vector
        def _(dve):
            n = [0]

            def link(ins):
                n[0] += 1
                ins.then_inc(chain, 1)
                dve.wait_ge(chain, n[0])

            dve.memset(g.onesd[:, :], 1.0 / D)
            dve.memset(g.ones[:, :], 1.0)
            dve.memset(g.epst[:, :], EPS)
            dve.memset(g.rdeg[:, :], 0.0)
            link(dve.memset(g.part[:, :], 0.0))
            dve.wait_ge(loaded, 64)
            bsum = g.brow[:, (K + 2) * D:(K + 3) * D]
            link(dve.tensor_tensor(bsum, bsum, g.brow[:, (K + 3) * D:(K + 4) * D], ALU.add))
            link(dve.tensor_tensor(bsum, bsum, g.brow[:, (K + 4) * D:(K + 5) * D], ALU.add))
            dve.wait_ge(made, n_iota)
            link(dve.tensor_scalar(g.ident[:, :], g.ident[:, :], 0.0, None, ALU.is_equal))
            dve.wait_ge(blocks_in, 16)
            dv = g.dblk[0:TN, :].rearrange("p (a b) -> p a b", b=BC)
            dve.tensor_reduce(g.bmax[0:TN, :], dv, AX.X, ALU.max)
            link(dve.tensor_reduce(g.bmin[0:TN, :], dv, AX.X, ALU.min))
            shape = [TN, NT, BR]
            lo = g.dtlo[0:TN, :].unsqueeze(2).broadcast_to(shape)
            bmin = g.bmin[0:TN, :].unsqueeze(1).broadcast_to(shape)
            bmax = g.bmax[0:TN, :].unsqueeze(1).broadcast_to(shape)
            blk = g.blk[0:TN, :].unsqueeze(1).broadcast_to(shape)
            ov, c2 = g.ov[0:TN, :, :], g.c2[0:TN, :, :]
            link(dve.tensor_scalar(g.bmin[0:TN, :], g.bmin[0:TN, :], float(TN - 1), None, ALU.subtract))
            link(dve.tensor_tensor(ov, bmin, lo, ALU.is_le))
            link(dve.tensor_tensor(c2, bmax, lo, ALU.is_ge))
            link(dve.tensor_tensor(ov, ov, c2, ALU.mult))
            link(dve.tensor_tensor(c2, ov, blk, ALU.mult))
            link(dve.scalar_tensor_tensor(out=ov, in0=ov, scalar=BIG, in1=c2, op0=ALU.mult, op1=ALU.subtract))
            link(dve.tensor_reduce(g.part[0:TN, 0:NT], ov, AX.X, ALU.max))
            link(dve.tensor_scalar(ov, ov, 0.0, float(BC), ALU.is_gt, ALU.mult))
            link(dve.tensor_tensor(c2, c2, ov, ALU.add))
            dve.tensor_reduce(g.part[0:TN, NT:2 * NT], c2, AX.X, ALU.max).then_inc(reduced, 1)
            dve.wait_ge(reduced, 2)
            neg, hi = g.red[:, 0:NT], g.red[:, NT:2 * NT]
            link(dve.tensor_scalar(g.lo[:, :], neg, -1.0, BIG, ALU.mult, ALU.add))
            link(dve.tensor_tensor(hi, hi, g.lo[:, :], ALU.subtract))
            link(dve.tensor_reduce(g.span[:, :], hi, AX.X, ALU.max))
            link(dve.tensor_scalar(g.span[:, :], g.span[:, :], 0.5, 1.0 / WIN, ALU.subtract, ALU.mult))
            link(dve.tensor_scalar(g.span[:, :], g.span[:, :], 0.5, 1.0, ALU.add, ALU.max))
            link(dve.tensor_copy(g.rounds[:, :], g.span[:, :]))
            sh = [P, RMAXN + 1, NT]
            link(dve.tensor_tensor(g.wfirst[:, :, :], g.lo[:, :].unsqueeze(1).broadcast_to(sh),
                                   g.rnd[:, :].unsqueeze(2).broadcast_to(sh), ALU.add))
            link(dve.tensor_scalar(g.c3[:, :, :], g.wfirst[:, :, :], float(E - WIN), None, ALU.min))
            link(dve.tensor_tensor(g.wfirst[:, :, :], g.wfirst[:, :, :], g.c3[:, :, :], ALU.subtract))
            link(dve.tensor_copy(g.wstart[:, :, :], g.c3[:, :, :]))
            link(dve.tensor_scalar(g.c3[:, 0, :], g.dtlo[:, :], -1.0, 1.0, ALU.mult, ALU.add))
            link(dve.tensor_copy(g.wnode[:, :, :], g.c3[:, 0, :].unsqueeze(1).broadcast_to(sh)))


ET = -(-E // P)
SG, SR = 26, 13
NB, BW = 7, 448
assert ET % SG == 0 and SG % SR == 0 and NB * BW == NP


def scatter_phase(nc, g, sem):
    edges_in, made, idx_now, turn, rows_used, split_done, onehot_done, tile_added, chain, taken, zeroed = (
        sem(s) for s in ("edges_in", "made", "idx_now", "turn", "rows_used", "split_done", "onehot_done",
                         "tile_added", "chain", "taken", "zeroed"))
    src_i = g.S3[:, 0:ET].bitcast(I32)
    dst_i = g.S3[:, ET:2 * ET].bitcast(I32)
    src_f, wgt = g.S3[:, 2 * ET:3 * ET], g.H[:, 0:ET]
    nodes = g.H[:, ET:ET + NP // 2].bitcast(mybir.dt.int16)
    oh = [t[:, 0:NP // 2].bitcast(BF16) for t in (g.S1, g.S2)]
    h1, h2, h3 = (g.attr[:, 0, k * P:(k + 1) * P].bitcast(BF16).rearrange("p (u f) -> p u f", u=2) for k in range(3))
    rest = g.attr[:, 0, 3 * P:5 * P].rearrange("p (u f) -> p u f", u=2)
    zero = g.attr[:, 0, 5 * P:5 * P + BW // 2].bitcast(BF16)
    with nc.Block() as block:
        @block.sync
        def _(sp):
            sp.dma_start(dst_i, g.dst_pt).then_inc(edges_in, 16)
            sp.dma_start(src_i, g.src_pt).then_inc(edges_in, 16)
            sp.dma_start(wgt, g.ewt_pt).then_inc(edges_in, 16)

        @block.gpsimd
        def _(pool):
            pool.iota(nodes, [[1, NP]], base=0, channel_multiplier=0,
                      allow_small_or_imprecise_dtypes=True).then_inc(made, 1)
            pool.wait_ge(edges_in, 48)
            with pool.Fori(0, ET // SG) as i:
                for h in range(SG // SR):
                    pool.wait_ge(rows_used, i * SG + h * SR + 1)
                    pool.sem_inc(turn)
                    pool.tensor_copy(g.gnow[:, h * SR:(h + 1) * SR], dst_i[:, bass.ds(i * SG + h * SR, SR)]).then_inc(idx_now, 1)
                    pool.wait_ge(idx_now, i * 2 + h + 1)
                    pool.sem_inc(turn)
                    for u in range(SR):
                        pool.wait_ge(rows_used, i * SG + h * SR + u + 2)
                        pool.sem_inc(turn)
                        pool.indirect_dma_start(g.rows[:, u, 0:D], None, g.x,
                                                bass.IndirectOffsetOnAxis(g.gnow[:, h * SR + u:h * SR + u + 1], 0)
                                                ).then_inc(g.rows_in[u], 16)

        @block.vector
        def _(dve):
            dve.sem_inc(rows_used, SR + 1)
            dve.memset(zero, 0.0).then_inc(zeroed, 1)
            dve.wait_ge(edges_in, 48)
            dve.tensor_copy(src_f, src_i).then_inc(chain, 1)
            dve.wait_ge(chain, 1)
            dve.wait_ge(made, 1)
            with dve.Fori(0, ET // SG) as i:
                for u in range(SG):
                    t = i * SG + u
                    w = wgt[:, bass.ds(t, 1)]
                    b = u % 2
                    dve.wait_ge(tile_added, t + 1)
                    dve.tensor_scalar(oh[b], nodes, src_f[:, bass.ds(t, 1)], None, ALU.is_equal
                                      ).then_inc(onehot_done, 1)
                    dve.wait_ge(g.rows_in[u % SR], (i * 2 + u // SR + 1) * 16)
                    row = g.rows[:, u % SR, 0:D]
                    dve.tensor_scalar(h1[:, b, :], row, w, None, ALU.mult).then_inc(chain, 1)
                    dve.wait_ge(chain, t * 3 + 2)
                    dve.scalar_tensor_tensor(out=rest[:, b, :], in0=row, scalar=w, in1=h1[:, b, :], op0=ALU.mult,
                                             op1=ALU.subtract).then_inc(chain, 1)
                    dve.wait_ge(chain, t * 3 + 3)
                    dve.sem_inc(rows_used)
                    dve.tensor_scalar(h2[:, b, :], rest[:, b, :], 1.0, None, ALU.mult).then_inc(chain, 1)
                    dve.wait_ge(chain, t * 3 + 4)
                    dve.tensor_tensor(h3[:, b, :], rest[:, b, :], h2[:, b, :], ALU.subtract).then_inc(split_done, 1)
            dve.wait_ge(tile_added, ET + 3)
            for c in range(NB):
                dve.tensor_copy(g.acc[:, c * BW:(c + 1) * BW], g.ps[:, c, 0:BW]).then_inc(taken, 1)

        @block.tensor
        def _(pe):
            pe.sem_inc(tile_added, 2)
            pe.wait_ge(zeroed, 1)
            for c in range(NB):
                pe.matmul(g.ps[:, c, 0:BW], zero[:, 0:P], zero, start=True, stop=False, skip_group_check=True)
            with pe.Fori(0, ET // SG) as i:
                for u in range(SG):
                    t = i * SG + u
                    b = u % 2
                    pe.wait_ge(onehot_done, t + 1)
                    pe.wait_ge(split_done, t + 1)
                    for part in (h1, h2, h3):
                        for c in range(NB):
                            mm = pe.matmul(g.ps[:, c, 0:BW], part[:, b, :], oh[b][:, c * BW:(c + 1) * BW],
                                           start=False, stop=False, skip_group_check=True)
                    mm.then_inc(tile_added, 1)
            for c in range(NB):
                mm = pe.matmul(g.ps[:, c, 0:BW], zero[:, 0:P], zero, start=False, stop=True, skip_group_check=True)
            mm.then_inc(tile_added, 1)


def edge_phase(nc, g, sem, kind, table, width, before, deg=False):
    L1, L3 = kind == "L1", kind == "L3"
    raw_in, conv_done, metaT_done, idx_done = sem("raw_in"), sem("conv_done"), sem("metaT_done"), sem("idx_done")
    rows_in = g.rows_in
    attr_in = [sem(f"attr_in{i}") for i in range(2)]
    idx_now, sp_turn = sem("idx_now"), sem("sp_turn")
    turn, tile_added, onehot_done, acc_done, chain = (
        sem("turn"), sem("tile_added"), sem("onehot_done"), sem("acc_done"), sem("chain"))
    ohT_ps, ohT_done, edge_ps, pre_ps, pre_done, sig_done, msg_done = (
        sem("ohT_ps"), sem("ohT_done"), sem("edge_ps"), sem("pre_ps"), sem("pre_done"), sem("sig_done"),
        sem("msg_done"))
    CR = RING + 1
    n_meta = 3 if L1 else 2
    rows_done = msg_done if L3 else tile_added

    def old(w, ring):
        return w - ring + 1 if w >= ring else 0

    wstart = g.wstart[:, :, :].rearrange("p a b -> p (a b)")
    wfirst = g.wfirst[:, :, :].rearrange("p a b -> p (a b)")
    wnode = g.wnode[:, :, :].rearrange("p a b -> p (a b)")

    with nc.Block() as block:
        @block.sync
        def _(sp):
            rounds = sp.value_load(g.rounds[0:1, 0:1], min_val=1, max_val=RMAXN)

            def load_meta(gi, at):
                def win(t):
                    return t[bass.ds(at, WIN)].rearrange("(w p) -> w p", p=P)
                sp.wait_ge(conv_done, gi + 1)
                sp.sem_inc(sp_turn)
                sp.dma_start(g.rawi[0:W, :], win(g.dst)).then_inc(raw_in, 16)
                sp.dma_start(g.rawi[W:2 * W, :], win(g.src)).then_inc(raw_in, 16)
                if L1:
                    sp.dma_start(g.rawi[2 * W:3 * W, :], win(g.ety)).then_inc(raw_in, 16)

            with sp.Fori(0, rounds * NT) as gi:
                at = sp.value_load(wstart[0:1, bass.ds(gi, 1)], min_val=0, max_val=E - WIN)
                load_meta(gi, at)
                if L3:
                    for half in range(2):
                        sp.wait_ge(edge_ps, gi * W + half * RING + 1)
                        sp.sem_inc(sp_turn)
                        sp.dma_start(g.attr[:, half, :],
                                     g.d_attrT[:, bass.ds(at + half * RING * P, RING * P)]).then_inc(attr_in[half], 16)
            last = sp.snap(rounds * NT)
            at = sp.value_load(wstart[0:1, bass.ds(last, 1)], min_val=0, max_val=E - WIN)
            load_meta(last, at)

        @block.gpsimd
        def _(pool):
            rounds = pool.value_load(g.rounds[0:1, 0:1], min_val=1, max_val=RMAXN)
            groups = [0, 4, 8, 12, RING, RING + 4, RING + 8, RING + 12, W]
            with pool.Fori(0, rounds * NT) as gi:
                par = pool.snap((gi % 2) * W)
                pool.wait_ge(idx_done, gi + 1)
                pool.sem_inc(turn)
                for a, b in zip(groups, groups[1:]):
                    pool.wait_ge(rows_done, gi * W + b + 1)
                    pool.sem_inc(turn)
                    if a % RING == 0:
                        half = a // RING
                        pool.tensor_copy(g.gnow[:, a:a + RING], g.gidx[:, bass.ds(par + a, RING)]).then_inc(idx_now, 1)
                        pool.wait_ge(idx_now, gi * 2 + half + 1)
                        pool.sem_inc(turn)
                    for w in range(a, b):
                        pool.indirect_dma_start(g.rows[:, w % RING, 0:width], None, table,
                                                bass.IndirectOffsetOnAxis(g.gnow[:, w:w + 1], 0)
                                                ).then_inc(rows_in[w % RING], 16)

        @block.tensor
        def _(pe):
            rounds = pe.value_load(g.rounds[0:1, 0:1], min_val=1, max_val=RMAXN)
            base = pe.snap(rounds * (NT * 2 * 16 * before))

            def transpose_meta(gi):
                pe.wait_ge(conv_done, gi + 2)
                pe.transpose(g.ps[:, 6, 0:n_meta * W], g.meta[0:n_meta * W, :],
                             g.ident[0:n_meta * W, 0:n_meta * W]).then_inc(metaT_done, 1)

            def add_up(gi, w, rows):
                if w == 0:
                    pe.wait_ge(acc_done, gi + 1)
                mm = pe.matmul(g.ps[:, 0, 0:TN], rows, g.oh[:, w % RING, :], start=(w == 0), stop=(w == W - 1))
                if deg:
                    mm = pe.matmul(g.ps[:, 1, 0:TN], g.ones[:, :], g.oh[:, w % RING, :],
                                   start=(w == 0), stop=(w == W - 1))
                mm.then_inc(tile_added, 1)

            pe.sem_inc(metaT_done)
            pe.sem_inc(edge_ps, CR)
            pe.sem_inc(tile_added, CR)
            pe.sem_inc(pre_ps, 2)
            transpose_meta(0)
            with pe.Fori(0, rounds) as r:
                with pe.Fori(0, NT) as dt:
                    gi = pe.snap(r * NT + dt)
                    for w in range(W + (S_LAG if L3 else 0)):
                        if w == W // 2 - 1:
                            transpose_meta(gi + 1)
                        if not L3:
                            pe.wait_ge(onehot_done, gi * W + w + 1)
                            pe.wait_ge(rows_in[w % RING], (gi * 2 + w // RING + 1) * 16 + base + g.rows_base[w % RING])
                            add_up(gi, w, g.rows[:, w % RING, 0:D])
                            continue
                        if w < W:
                            pe.wait_ge(onehot_done, gi * W + w + 1)
                            pe.wait_ge(ohT_done, gi * W + w + 1)
                            pe.transpose(g.ps[0:TN, 2 + w % 2, 0:P], g.oh[:, w % RING, :],
                                         g.ident[:, :]).then_inc(ohT_ps, 1)
                            if w % RING == 0:
                                pe.wait_ge(attr_in[w // RING], (gi + 1) * 16)
                            pe.wait_ge(pre_done, gi * W + w + 1)
                            pe.matmul(g.ps[:, 4 + w % 2, 0:D],
                                      g.attr[:, w // RING, (w % RING) * P:(w % RING + 1) * P],
                                      g.wt("we"), start=True, stop=False).then_inc(edge_ps, 1)
                        if 1 <= w <= W:
                            u = w - 1
                            pe.wait_ge(ohT_done, gi * W + u + 3)
                            pe.matmul(g.ps[:, 4 + u % 2, 0:D], g.ohT[0:TN, u % 2, :],
                                      g.C[0:TN, bass.ds(dt * D, D)], start=False, stop=True).then_inc(pre_ps, 1)
                        if w >= S_LAG:
                            u = w - S_LAG
                            pe.wait_ge(msg_done, gi * W + u + 1 + CR)
                            add_up(gi, u, g.msg[:, u % 4, :])

        @block.vector
        def _(dve):
            rounds = dve.value_load(g.rounds[0:1, 0:1], min_val=1, max_val=RMAXN)
            base = dve.snap(rounds * (NT * 2 * 16 * before))
            links = 4 if L1 else 3

            def prepare(gi):
                made = [0]

                def link(ins):
                    made[0] += 1
                    ins.then_inc(chain, 1)
                    dve.wait_ge(chain, gi * links + made[0])

                par = dve.snap((gi % 2) * W)
                ints = 3 * W if L1 else 2 * W
                dve.wait_ge(raw_in, (gi + 1) * 16 * n_meta)
                dve.tensor_copy(g.meta[0:ints, :], g.rawi[0:ints, :]).then_inc(conv_done, 1)
                link(dve.tensor_scalar(g.mask[:, :], g.eidx[:, :], wfirst[:, bass.ds(gi, 1)], None, ALU.is_ge))
                dve.wait_ge(metaT_done, gi + 2)
                m = g.ps[:, 6, :]
                link(dve.scalar_tensor_tensor(out=g.dcol[:, bass.ds(par, W)], in0=m[:, 0:W],
                                              scalar=wnode[:, bass.ds(gi, 1)], in1=g.mask[:, :],
                                              op0=ALU.add, op1=ALU.mult))
                if L1:
                    link(dve.tensor_scalar(g.tmpw[:, :], m[:, 2 * W:3 * W], float(N), None, ALU.mult))
                    link(dve.tensor_tensor(g.gidx[:, bass.ds(par, W)], g.tmpw[:, :], m[:, W:2 * W], ALU.add))
                else:
                    link(dve.tensor_scalar(g.gidx[:, bass.ds(par, W)], m[:, W:2 * W], 1.0, None, ALU.mult))
                assert made[0] == links
                dve.sem_inc(idx_done)

            dve.sem_inc(conv_done)
            dve.sem_inc(acc_done)
            dve.sem_inc(pre_done, 2)
            dve.sem_inc(msg_done, CR)
            dve.memset(g.acc[:, :], 0.0).then_inc(acc_done, 1)
            dve.wait_ge(acc_done, 2)
            prepare(0)
            with dve.Fori(0, rounds) as r:
                with dve.Fori(0, NT) as dt:
                    gi = dve.snap(r * NT + dt)
                    par = dve.snap((gi % 2) * W)
                    for w in range(W + (MUL_LAG if L3 else 0)):
                        if w == W // 2 - 1:
                            prepare(gi + 1)
                        if w < W:
                            dve.wait_ge(tile_added, gi * W + w + 2)
                            dc = g.dcol[:, bass.ds(par + w, 1)]
                            dve.tensor_scalar(g.oh[:, w % RING, :], g.iota1[:, :], dc, None, ALU.is_equal
                                              ).then_inc(onehot_done, 1)
                        if L3 and PRE_LAG <= w < W + PRE_LAG:
                            u = w - PRE_LAG
                            dve.wait_ge(pre_ps, gi * W + u + 3)
                            dve.wait_ge(rows_in[u % RING], (gi * 2 + u // RING + 1) * 16 + base + g.rows_base[u % RING])
                            dve.wait_ge(sig_done, gi * W + old(u, 4) + 1)
                            dve.tensor_tensor(g.pre[:, u % 4, :], g.ps[:, 4 + u % 2, 0:D], g.rows[:, u % RING, 0:D],
                                              ALU.add).then_inc(pre_done, 1)
                        if L3 and w >= MUL_LAG:
                            u = w - MUL_LAG
                            dve.wait_ge(sig_done, gi * W + u + 2)
                            dve.wait_ge(tile_added, gi * W + old(u, 4) + CR)
                            dve.tensor_tensor(g.msg[:, u % 4, :], g.sig[:, u % 4, :], g.rows[:, u % RING, D:2 * D],
                                              ALU.mult).then_inc(msg_done, 1)
                    dve.wait_ge(tile_added, gi * W + W + CR)
                    dve.wait_ge(acc_done, gi + 2)
                    a = g.acc[:, bass.ds(dt * TN, TN)]
                    if deg:
                        q = g.rdeg[:, bass.ds(dt * TN, TN)]
                        dve.tensor_tensor(q, q, g.ps[:, 1, 0:TN], ALU.add)
                    dve.tensor_tensor(a, a, g.ps[:, 0, 0:TN], ALU.add).then_inc(acc_done, 1)

        @block.scalar
        def _(act):
            if not L3:
                return
            rounds = act.value_load(g.rounds[0:1, 0:1], min_val=1, max_val=RMAXN)
            act.sem_inc(ohT_done, 2)
            act.sem_inc(sig_done)
            with act.Fori(0, rounds * NT) as gi:
                for w in range(W + PRE_LAG):
                    if w < W:
                        act.wait_ge(pre_ps, gi * W + w + 1)
                        act.wait_ge(ohT_ps, gi * W + w + 1)
                        act.activation(g.ohT[0:TN, w % 2, :], g.ps[0:TN, 2 + w % 2, 0:P], ACT.Copy
                                       ).then_inc(ohT_done, 1)
                    if w >= PRE_LAG:
                        u = w - PRE_LAG
                        act.wait_ge(msg_done, gi * W + old(u, 4) + CR)
                        act.wait_ge(pre_done, gi * W + u + 3)
                        act.activation(g.sig[:, u % 4, :], g.pre[:, u % 4, :], ACT.Sigmoid).then_inc(sig_done, 1)


TU = 5


def table_phase(nc, g, sem, feats, rhs, bias, M, dest, cpart=False):
    tile_copied, row_ps, rows_done, row_out = sem("tile_copied"), sem("row_ps"), sem("rows_done"), [
        sem(f"row_out{u}") for u in range(TU)]
    sp_turn = sem("sp_turn")
    MD = M - D if cpart else M
    with nc.Block() as block:
        @block.vector
        def _(dve):
            dve.sem_inc(rows_done, TU + 1)
            with dve.Fori(0, NT // TU) as i:
                for u in range(TU):
                    dve.wait_ge(row_ps, i * TU + u + 1)
                    dve.tensor_scalar(g.lt[:, u, :], feats[:, bass.ds(i * TU * TN + u * TN, TN)], 1.0, None,
                                      ALU.mult).then_inc(tile_copied, 1)
                for u in range(TU):
                    dve.wait_ge(row_ps, i * TU + u + 1 + TU)
                    dve.wait_ge(row_out[u], i * 16 + 1)
                    if cpart:
                        dve.tensor_tensor(g.C[0:TN, bass.ds(i * TU * D + u * D, D)], g.ps[0:TN, u, MD:M],
                                          bias[0:TN, MD:M], ALU.add)
                    dve.tensor_tensor(g.rowbuf[0:TN, u, 0:MD], g.ps[0:TN, u, 0:MD], bias[0:TN, 0:MD],
                                      ALU.add).then_inc(rows_done, 1)

        @block.tensor
        def _(pe):
            pe.sem_inc(row_ps, TU)
            with pe.Fori(0, NT // TU) as i:
                for u in range(TU):
                    pe.wait_ge(rows_done, i * TU + u + 2)
                    pe.wait_ge(tile_copied, i * TU + u + 1)
                    pe.matmul(g.ps[0:TN, u, 0:M], g.lt[:, u, :], rhs, start=True, stop=True).then_inc(row_ps, 1)

        @block.sync
        def _(sp):
            for u in range(TU):
                sp.sem_inc(row_out[u])
            with sp.Fori(0, NT // TU) as i:
                for u in range(TU):
                    sp.wait_ge(rows_done, i * TU + u + 2 + TU)
                    sp.sem_inc(sp_turn)
                    sp.dma_start(dest(bass.ds(i * TU * TN + u * TN, TN)), g.rowbuf[0:TN, u, 0:MD]
                                 ).then_inc(row_out[u], 16)
            for u in range(TU):
                sp.wait_ge(row_out[u], NT // TU * 16 + 1)


def cols(t, c):
    return t[:, c * CH:(c + 1) * CH]


def bank(g, b):
    return g.ps[:, b, 0:CH]


class Norm:

    def __init__(self, g, sem):
        self.g = g
        (self.ready, self.mean_ps, self.centred, self.squared, self.var_ps, self.root_done, self.recip_done,
         self.x_done) = (sem(s) for s in ("ln_ready", "ln_mean_ps", "ln_centred", "ln_squared", "ln_var_ps",
                                          "ln_root", "ln_recip", "ln_x"))

    def tensor(self, pe):
        g = self.g
        for c in range(NCH):
            pe.wait_ge(self.ready, c + 1)
            pe.matmul(bank(g, c), g.onesd[:, :], cols(g.S3, c), start=True, stop=True).then_inc(self.mean_ps, 1)
        for c in range(NCH):
            pe.wait_ge(self.squared, c + 1)
            pe.matmul(bank(g, c), g.onesd[:, :], cols(g.S2, c), start=True, stop=True).then_inc(self.var_ps, 1)

    def vector(self, dve):
        g = self.g
        for c in range(NCH):
            dve.wait_ge(self.mean_ps, c + 1)
            dve.tensor_tensor(cols(g.S3, c), cols(g.S3, c), bank(g, c), ALU.subtract).then_inc(self.centred, 1)
        for c in range(NCH):
            dve.wait_ge(self.root_done, c + 1)
            dve.reciprocal(cols(g.S1, c), cols(g.S1, c)).then_inc(self.recip_done, 1)
            if c:
                dve.wait_ge(self.recip_done, c)
                dve.tensor_tensor(cols(g.X, c - 1), cols(g.S3, c - 1), cols(g.S1, c - 1), ALU.mult
                                  ).then_inc(self.x_done, 1)
        dve.wait_ge(self.recip_done, NCH)
        dve.tensor_tensor(cols(g.X, NCH - 1), cols(g.S3, NCH - 1), cols(g.S1, NCH - 1), ALU.mult
                          ).then_inc(self.x_done, 1)

    def scalar(self, act):
        g = self.g
        for c in range(NCH):
            act.wait_ge(self.centred, c + 1)
            act.activation(cols(g.S2, c), cols(g.S3, c), ACT.Square).then_inc(self.squared, 1)
        for c in range(NCH):
            act.wait_ge(self.var_ps, c + 1)
            act.activation(cols(g.S1, c), bank(g, c), ACT.Sqrt, bias=g.epst[:, 0:1]).then_inc(self.root_done, 1)


def first_node_phase(nc, g, sem):
    y_ps, h_done = sem("y_ps"), sem("h_done")
    norm = Norm(g, sem)
    with nc.Block() as block:
        @block.tensor
        def _(pe):
            for c in range(NCH):
                pe.matmul(bank(g, c), g.wt("w0"), cols(g.acc, c), start=True, stop=True).then_inc(y_ps, 1)
            norm.tensor(pe)

        @block.vector
        def _(dve):
            for c in range(NCH):
                dve.wait_ge(y_ps, c + 1)
                dve.scalar_tensor_tensor(out=cols(g.S3, c), in0=cols(g.X, c), scalar=2.0, in1=bank(g, c),
                                         op0=ALU.mult, op1=ALU.add).then_inc(norm.ready, 1)
            norm.vector(dve)

        @block.scalar
        def _(act):
            norm.scalar(act)
            for c in range(NCH):
                act.wait_ge(norm.x_done, c + 1)
                act.activation(cols(g.H, c), cols(g.X, c), ACT.Copy).then_inc(h_done, 1)


def gru_phase(nc, g, sem):
    bias_done, gates_ps, r_done, z_done, rn_done, pre_done, n_done, diff_done, prod_done, h_done = (
        sem(s) for s in ("gru_bias", "gates_ps", "r_done", "z_done", "rn_done", "npre_done", "n_done", "diff_done",
                         "prod_done", "h_done"))
    with nc.Block() as block:
        @block.tensor
        def _(pe):
            for c in range(NCH):
                b = 4 * (c % 2)
                if c >= 2:
                    pe.wait_ge(z_done, c - 1)
                    pe.wait_ge(pre_done, c - 1)
                for k, (wi, wh) in enumerate((("ih_r", "hh_r"), ("ih_z", "hh_z"))):
                    pe.matmul(bank(g, b + k), g.wt(wi), cols(g.acc, c), start=True, stop=False)
                    pe.matmul(bank(g, b + k), g.wt(wh), cols(g.H, c), start=False, stop=True)
                pe.matmul(bank(g, b + 2), g.wt("ih_n"), cols(g.acc, c), start=True, stop=True)
                pe.matmul(bank(g, b + 3), g.wt("hh_n"), cols(g.H, c), start=True, stop=True).then_inc(gates_ps, 1)

        @block.scalar
        def _(act):
            act.wait_ge(bias_done, 2)
            for c in range(NCH + 1):
                if c < NCH:
                    b = 4 * (c % 2)
                    act.wait_ge(gates_ps, c + 1)
                    act.activation(cols(g.S1, c), bank(g, b), ACT.Sigmoid, bias=g.bsum[:, 0:1]).then_inc(r_done, 1)
                    act.activation(cols(g.S2, c), bank(g, b + 1), ACT.Sigmoid, bias=g.bsum[:, 1:2]).then_inc(z_done, 1)
                if c:
                    act.wait_ge(pre_done, c)
                    act.activation(cols(g.S3, c - 1), cols(g.S3, c - 1), ACT.Tanh).then_inc(n_done, 1)

        @block.vector
        def _(dve):
            dve.tensor_tensor(g.bsum[:, 0:1], g.bt("bih_r"), g.bt("bhh_r"), ALU.add).then_inc(bias_done, 1)
            dve.tensor_tensor(g.bsum[:, 1:2], g.bt("bih_z"), g.bt("bhh_z"), ALU.add).then_inc(bias_done, 1)
            for c in range(NCH + 1):
                if c < NCH:
                    b = 4 * (c % 2)
                    dve.wait_ge(r_done, c + 1)
                    dve.scalar_tensor_tensor(out=cols(g.S1, c), in0=bank(g, b + 3), scalar=g.bt("bhh_n"),
                                             in1=cols(g.S1, c), op0=ALU.add, op1=ALU.mult).then_inc(rn_done, 1)
                    dve.wait_ge(rn_done, c + 1)
                    dve.scalar_tensor_tensor(out=cols(g.S3, c), in0=bank(g, b + 2), scalar=g.bt("bih_n"),
                                             in1=cols(g.S1, c), op0=ALU.add, op1=ALU.add).then_inc(pre_done, 1)
                if c:
                    p = c - 1
                    dve.wait_ge(n_done, c)
                    dve.tensor_tensor(cols(g.S1, p), cols(g.H, p), cols(g.S3, p), ALU.subtract).then_inc(diff_done, 1)
                    dve.wait_ge(diff_done, c)
                    dve.wait_ge(z_done, c)
                    dve.tensor_tensor(cols(g.S2, p), cols(g.S2, p), cols(g.S1, p), ALU.mult).then_inc(prod_done, 1)
                    dve.wait_ge(prod_done, c)
                    dve.tensor_tensor(cols(g.H, p), cols(g.S3, p), cols(g.S2, p), ALU.add).then_inc(h_done, 1)


def gate_phase(nc, g, sem):
    out_ps, gate_done, prod_done = sem("out_ps"), sem("gate_done"), sem("prod_done")
    norm = Norm(g, sem)
    with nc.Block() as block:
        @block.tensor
        def _(pe):
            for c in range(NCH):
                b = 2 * (c % 4)
                if c >= 4:
                    pe.wait_ge(prod_done, c - 3)
                pe.matmul(bank(g, b), g.wt("iw_h"), cols(g.H, c), start=True, stop=False)
                pe.matmul(bank(g, b), g.wt("iw_f"), cols(g.X, c), start=False, stop=True)
                pe.matmul(bank(g, b + 1), g.wt("jw"), cols(g.H, c), start=True, stop=True).then_inc(out_ps, 1)
            pe.wait_ge(prod_done, NCH)
            norm.tensor(pe)

        @block.scalar
        def _(act):
            for c in range(NCH):
                act.wait_ge(out_ps, c + 1)
                act.activation(cols(g.S1, c), bank(g, 2 * (c % 4)), ACT.Sigmoid, bias=g.bt("ib")).then_inc(gate_done, 1)
            norm.scalar(act)

        @block.vector
        def _(dve):
            for c in range(NCH):
                dve.wait_ge(gate_done, c + 1)
                dve.scalar_tensor_tensor(out=cols(g.S2, c), in0=bank(g, 2 * (c % 4) + 1), scalar=g.bt("jb"),
                                         in1=cols(g.S1, c), op0=ALU.add, op1=ALU.mult).then_inc(prod_done, 1)
                dve.wait_ge(prod_done, c + 1)
                dve.tensor_tensor(cols(g.S3, c), cols(g.X, c), cols(g.S2, c), ALU.add).then_inc(norm.ready, 1)
            norm.vector(dve)


def gin_phase(nc, g, sem, first):
    deg_max, deg_done, mean_done, in_done, a_ps, a_done, b_ps, b_done = (
        sem(s) for s in ("deg_max", "deg_done", "mean_done", "in_done", "a_ps", "a_done", "b_ps", "b_done"))
    norm = None if first else Norm(g, sem)
    wa, wb, ba, bb = ("w1a", "w1b", "b1a", "b1b") if first else ("w2a", "w2b", "b2a", "b2b")
    f = g.X if first else g.H
    with nc.Block() as block:
        @block.tensor
        def _(pe):
            for c in range(NCH):
                pe.wait_ge(in_done, c + 1)
                pe.matmul(bank(g, c), g.wt(wa), cols(g.S1, c), start=True, stop=True).then_inc(a_ps, 1)
            for c in range(NCH):
                pe.wait_ge(a_done, c + 1)
                pe.matmul(bank(g, c), g.wt(wb), cols(g.S2, c), start=True, stop=True).then_inc(b_ps, 1)
            if not first:
                norm.tensor(pe)

        @block.scalar
        def _(act):
            for c in range(NCH):
                act.wait_ge(a_ps, c + 1)
                act.activation(cols(g.S2, c), bank(g, c), ACT.Identity, bias=g.bt(ba)).then_inc(a_done, 1)
            for c in range(NCH):
                act.wait_ge(b_ps, c + 1)
                act.activation(cols(g.H, c), bank(g, c), ACT.Relu, bias=g.bt(bb)).then_inc(b_done, 1)
            if not first:
                norm.scalar(act)

        @block.vector
        def _(dve):
            if first:
                for c in range(NCH):
                    dve.tensor_scalar(cols(g.rdeg, c), cols(g.rdeg, c), 1.0, None, ALU.max).then_inc(deg_max, 1)
                for c in range(NCH):
                    dve.wait_ge(deg_max, c + 1)
                    dve.reciprocal(cols(g.rdeg, c), cols(g.rdeg, c)).then_inc(deg_done, 1)
            for c in range(NCH):
                if first:
                    dve.wait_ge(deg_done, c + 1)
                dve.tensor_tensor(cols(g.S1, c), cols(g.acc, c), cols(g.rdeg, c), ALU.mult).then_inc(mean_done, 1)
                dve.wait_ge(mean_done, c + 1)
                dve.tensor_tensor(cols(g.S1, c), cols(g.S1, c), cols(f, c), ALU.add).then_inc(in_done, 1)
            if not first:
                for c in range(NCH):
                    dve.wait_ge(b_done, c + 1)
                    dve.tensor_tensor(cols(g.S3, c), cols(g.X, c), cols(g.H, c), ALU.add).then_inc(norm.ready, 1)
                norm.vector(dve)


def last_node_phase(nc, g, sem):
    res_ps, sum_done, relu_done, stored = sem("res_ps"), sem("sum_done"), sem("relu_done"), sem("stored")
    norm = Norm(g, sem)
    with nc.Block() as block:
        @block.tensor
        def _(pe):
            for c in range(NCH):
                pe.matmul(bank(g, c), g.wt("wres"), cols(g.X, c), start=True, stop=True).then_inc(res_ps, 1)
            norm.tensor(pe)

        @block.scalar
        def _(act):
            for c in range(NCH):
                act.wait_ge(sum_done, c + 1)
                act.activation(cols(g.S2, c), cols(g.S1, c), ACT.Relu, bias=g.bt("bres")).then_inc(relu_done, 1)
            norm.scalar(act)

        @block.vector
        def _(dve):
            for c in range(NCH):
                dve.wait_ge(res_ps, c + 1)
                dve.tensor_tensor(cols(g.S1, c), cols(g.acc, c), bank(g, c), ALU.add).then_inc(sum_done, 1)
            for c in range(NCH):
                dve.wait_ge(relu_done, c + 1)
                dve.tensor_tensor(cols(g.S3, c), cols(g.X, c), cols(g.S2, c), ALU.add).then_inc(norm.ready, 1)
            norm.vector(dve)

        @block.sync
        def _(sp):
            sp.wait_ge(norm.x_done, NCH)
            sp.dma_start(g.out, g.X[:, :]).then_inc(stored, 16)
            sp.wait_ge(stored, 16)


def build(nc, d, out):
    g = Shared()
    with ExitStack() as ctx:
        def sb(name, shape, dt=F32):
            return ctx.enter_context(nc.sbuf_tensor(name, shape, dt))

        g.x, g.src, g.dst, g.ety = d["x"], d["src"], d["dst"], d["etype"]
        g.src_pt, g.dst_pt, g.ewt_pt = d["src_pt"], d["dst_pt"], d["eweight_pt"]
        g.d_attrT, g.d_w, g.d_b, g.d_brow, g.d_xT, g.out = d["attrT"], d["w"], d["b"], d["brow"], d["xT"], out
        t_types = nc.dram_tensor("t_types", (K * N, D), F32, kind="Internal").ap()
        t_feats = nc.dram_tensor("t_feats", (N, D), F32, kind="Internal").ap()
        t_gated = nc.dram_tensor("t_gated", (N, 2 * D), F32, kind="Internal").ap()

        g.X, g.H, g.acc, g.rdeg = sb("X", [P, NP]), sb("H", [P, NP]), sb("acc", [P, NP]), sb("rdeg", [P, NP])
        g.S1, g.S2, g.S3 = sb("S1", [P, NP]), sb("S2", [P, NP]), sb("S3", [P, NP])
        g.w, g.b, g.brow = sb("w", [P, len(WNAMES) * D]), sb("b", [P, len(BNAMES)]), sb("brow", [P, len(RNAMES) * D])
        g.wt = lambda n: g.w[:, WNAMES.index(n) * D:(WNAMES.index(n) + 1) * D]
        g.bt = lambda n: g.b[:, BNAMES.index(n):BNAMES.index(n) + 1]
        g.bsum, g.epst = sb("bsum", [P, 2]), sb("epst", [P, 1])
        g.ident, g.ones, g.onesd = sb("ident", [P, P]), sb("ones", [P, P]), sb("onesd", [P, P])
        g.iota1, g.eidx = sb("iota1", [P, TN]), sb("eidx", [P, W])
        shape = [P, RMAXN + 1, NT]
        g.wstart, g.wfirst, g.wnode = sb("wstart", shape, I32), sb("wfirst", shape), sb("wnode", shape)
        g.rounds = sb("rounds", [P, 1], I32)
        g.rawi, g.meta, g.mask, g.tmpw = sb("rawi", [P, P], I32), sb("meta", [P, P]), sb("mask", [P, W]), sb("tmpw", [P, W])
        g.dcol, g.gidx = sb("dcol", [P, 2 * W]), sb("gidx", [P, 2 * W], I32)
        g.gnow = sb("gnow", [P, W], I32)
        g.rows, g.oh, g.ohT = sb("rows", [P, RING, 2 * D]), sb("oh", [P, RING, TN]), sb("ohT", [P, 2, P])
        g.attr, g.C = sb("attr", [P, 2, RING * P]), sb("C", [P, NT * D])
        g.pre, g.sig, g.msg = sb("pre", [P, 4, D]), sb("sig", [P, 4, D]), sb("msg", [P, 4, D])
        g.lt = sb("lt", [P, TU, TN])
        g.rowbuf = g.rows[:, 0:2 * TU, :].rearrange("p (u h) d -> p u (h d)", h=2)
        g.dblk = sb("dblk", [P, BR * BC], I32)
        g.ov = g.S1[:, 0:NT * BR].rearrange("p (a b) -> p a b", b=BR)
        g.c2 = g.S2[:, 0:NT * BR].rearrange("p (a b) -> p a b", b=BR)
        g.c3 = g.S3[:, 0:(RMAXN + 1) * NT].rearrange("p (a b) -> p a b", b=NT)
        g.blk, g.bmin, g.bmax = sb("blk", [P, BR]), sb("bmin", [P, BR]), sb("bmax", [P, BR])
        g.dtlo, g.rnd = sb("dtlo", [P, NT]), sb("rnd", [P, RMAXN + 1])
        g.part, g.red, g.lo, g.span = sb("part", [P, 2 * NT]), sb("red", [P, 2 * NT]), sb("lo", [P, NT]), sb("span", [P, 1])
        g.ps = ctx.enter_context(nc.psum_tensor("ps", [P, 8, 512], F32))
        g.rows_in = [ctx.enter_context(nc.semaphore(f"rows_in{i}")) for i in range(RING)]
        sem = Sems(nc, ctx)
        g.rows_base = [ET // SR * 16 if i < SR else 0 for i in range(RING)]

        setup_phase(nc, g, sem)
        sem.clear()
        scatter_phase(nc, g, sem)
        sem.clear()
        first_node_phase(nc, g, sem)
        sem.clear()
        types = t_types.rearrange("(k n) f -> n k f", k=K)
        for step in range(3):
            table_phase(nc, g, sem, g.H, g.w[:, D:(1 + K) * D], g.brow, K * D, lambda n: types[n, :, :])
            sem.clear()
            edge_phase(nc, g, sem, "L1", t_types, D, step, deg=(step == 0))
            sem.clear()
            gru_phase(nc, g, sem)
            sem.clear()
        gate_phase(nc, g, sem)
        sem.clear()
        zero_row = g.brow[:, K * D:(K + 1) * D]
        for first in (True, False):
            table_phase(nc, g, sem, g.X if first else g.H, g.ident[:, :], zero_row, D, lambda n: t_feats[n, :])
            sem.clear()
            edge_phase(nc, g, sem, "L2", t_feats, D, 3 if first else 4)
            sem.clear()
            gin_phase(nc, g, sem, first)
            sem.clear()
        w0 = WNAMES.index("wb") * D
        table_phase(nc, g, sem, g.X, g.w[:, w0:w0 + 3 * D], g.brow[:, K * D:(K + 3) * D], 3 * D,
                    lambda n: t_gated[n, :], cpart=True)
        sem.clear()
        edge_phase(nc, g, sem, "L3", t_gated, 2 * D, 5)
        sem.clear()
        last_node_phase(nc, g, sem)


def kernel(**inputs):
    import concourse.bacc as bacc
    from concourse.bass_utils import run_bass_kernel_spmd

    a = {k: np.asarray(v) for k, v in inputs.items()}
    wih, whh, wet, iw = a["L1_gnn_W_ih"], a["L1_gnn_W_hh"], a["L1_gnn_W_et"], a["L1_gnn_i_w"]
    blocks = [a["L0_gnn_social_weight"]] + [wet[k].T for k in range(K)]
    blocks += [wih[i * D:(i + 1) * D].T for i in range(3)] + [whh[i * D:(i + 1) * D].T for i in range(3)]
    blocks += [iw[:, :D].T, iw[:, D:].T, a["L1_gnn_j_w"].T]
    blocks += [a[f"L2_gnn_W{n}"].T for n in ("1a", "1b", "2a", "2b")]
    blocks += [a[f"L3_gnn_W{n}"] for n in ("B", "A", "C", "E", "res")]
    columns = [a["L1_gnn_b_ih"].reshape(3, D), a["L1_gnn_b_hh"].reshape(3, D), a["L1_gnn_i_b"][None],
               a["L1_gnn_j_b"][None]] + [a[f"L2_gnn_b{n}"][None] for n in ("1a", "1b", "2a", "2b")]
    columns += [a["L3_gnn_bres"][None]]
    rows = [a["L1_gnn_b_et"].reshape(-1), np.zeros(D, np.float32)] + [a[f"L3_gnn_b{n}"] for n in ("A", "B", "C", "E")]
    pad = lambda v: np.pad(v, (0, ET * P - E)).reshape(P, ET)
    xT = np.zeros((D, NP), np.float32)
    xT[:, :N] = a["x"].T
    arrays = {
        "x": a["x"], "xT": xT, "src": a["src"], "dst": a["dst"], "etype": a["edge_type_4"],
        "src_pt": pad(a["src"]), "dst_pt": pad(a["dst"]), "eweight_pt": pad(a["edge_weight"]),
        "attrT": np.ascontiguousarray(a["edge_attr_128"].T), "w": np.concatenate(blocks, axis=1),
        "b": np.ascontiguousarray(np.concatenate(columns, axis=0).T), "brow": np.concatenate(rows)[None],
    }
    nc = bacc.Bacc("TRN2", target_bir_lowering=False, num_devices=1)
    d = {k: nc.dram_tensor("in_" + k, v.shape, mybir.dt.from_np(v.dtype), kind="ExternalInput").ap()
         for k, v in arrays.items()}
    out = nc.dram_tensor("out_x", (D, NP), F32, kind="ExternalOutput").ap()
    build(nc, d, out)
    r = run_bass_kernel_spmd(nc, [{"in_" + k: v for k, v in arrays.items()}], core_ids=[0])
    return np.ascontiguousarray(r.results[0]["out_x"][:, :N].T)
```

```python
from contextlib import ExitStack

import numpy as np
import concourse.bass as bass
from concourse import mybir

F32 = mybir.dt.float32
I32 = mybir.dt.int32
BF16 = mybir.dt.bfloat16
F16 = mybir.dt.float16
ALU = mybir.AluOpType
ACT = mybir.ActivationFunctionType
AX = mybir.AxisListType
RMAX = bass.bass_isa.ReduceOp.max

N, D, E, K = 3125, 128, 103125, 4
P = 128
TN = 125
NT = N // TN
W = 34
WIN = W * P
RMAXN = -(-E // WIN)
NTAB = (RMAXN + 1) * NT
RING = W // 2
NCH = 8
CH = 392
NP = NCH * CH
BR, BC = 33, 25
BIG = float(E + 1)
EPS = 1e-5
PRE_LAG, MUL_LAG, S_LAG = 2, 3, 5

WNAMES = ["w0"] + [f"wet{k}" for k in range(K)] + ["ih_r", "ih_z", "ih_n", "hh_r", "hh_z", "hh_n", "iw_h", "iw_f", "jw",
          "w1a", "w1b", "w2a", "w2b", "wb", "wa", "wc", "we", "wres"]
BNAMES = ["bih_r", "bih_z", "bih_n", "bhh_r", "bhh_z", "bhh_n", "ib", "jb", "b1a", "b1b", "b2a", "b2b", "bres"]
RNAMES = [f"bet{k}" for k in range(K)] + ["zero", "ba", "bb", "bc", "be"]


class Shared:
    pass


class Sems:

    def __init__(self, nc, ctx):
        self.nc, self.ctx, self.by_name = nc, ctx, {}

    def __call__(self, name):
        if name not in self.by_name:
            self.by_name[name] = self.ctx.enter_context(self.nc.semaphore(name))
        return self.by_name[name]

    def clear(self):
        nums = [s.num for s in self.by_name.values()]
        self.nc.sync.sem_clear(range(min(nums), max(nums) + 1))
        self.nc.all_engine_barrier()


def setup_phase(nc, g, sem):
    loaded, blocks_in = sem("loaded"), sem("blocks_in")
    made, chain, reduced = sem("made"), sem("chain"), sem("reduced")
    n_iota = 6
    with nc.Block() as block:
        @block.sync
        def _(sp):
            sp.dma_start(g.dblk[0:TN, :], g.dst.rearrange("(p f) -> p f", p=TN)).then_inc(blocks_in, 16)
            sp.dma_start(g.w[:, :], g.d_w).then_inc(loaded, 16)
            sp.dma_start(g.b[:, :], g.d_b).then_inc(loaded, 16)
            sp.dma_start(g.brow[:, :], g.d_brow.broadcast_to((P, len(RNAMES) * D))).then_inc(loaded, 16)
            sp.dma_start(g.X[:, :], g.d_xT).then_inc(loaded, 16)
            sp.wait_ge(loaded, 64)

        @block.gpsimd
        def _(pool):
            io = dict(allow_small_or_imprecise_dtypes=True)
            pool.iota(g.iota1[:, :], [[1, TN]], base=1, channel_multiplier=0, **io).then_inc(made, 1)
            pool.iota(g.eidx[:, :], [[P, W]], base=0, channel_multiplier=1, **io).then_inc(made, 1)
            pool.iota(g.ident[:, :], [[1, P]], base=0, channel_multiplier=-1, **io).then_inc(made, 1)
            pool.iota(g.blk[:, :], [[BC, BR]], base=0, channel_multiplier=BR * BC, **io).then_inc(made, 1)
            pool.iota(g.dtlo[:, :], [[TN, NT]], base=0, channel_multiplier=0, **io).then_inc(made, 1)
            pool.iota(g.rnd[:, :], [[WIN, RMAXN + 1]], base=0, channel_multiplier=0, **io).then_inc(made, 1)
            pool.wait_ge(reduced, 1)
            pool.partition_all_reduce(g.red[:, :], g.part[:, :], P, RMAX).then_inc(reduced, 1)

        @block.vector
        def _(dve):
            n = [0]

            def link(ins):
                n[0] += 1
                ins.then_inc(chain, 1)
                dve.wait_ge(chain, n[0])

            dve.memset(g.onesd[:, :], 1.0 / D)
            dve.memset(g.ones[:, :], 1.0)
            dve.memset(g.ones16[:, :], 1.0)
            dve.memset(g.epst[:, :], EPS)
            dve.memset(g.rdeg[:, :], 0.0)
            link(dve.memset(g.part[:, :], 0.0))
            dve.wait_ge(loaded, 64)
            bsum = g.brow[:, (K + 2) * D:(K + 3) * D]
            link(dve.tensor_tensor(bsum, bsum, g.brow[:, (K + 3) * D:(K + 4) * D], ALU.add))
            link(dve.tensor_tensor(bsum, bsum, g.brow[:, (K + 4) * D:(K + 5) * D], ALU.add))
            dve.wait_ge(made, n_iota)
            link(dve.tensor_scalar(g.ident[:, :], g.ident[:, :], 0.0, None, ALU.is_equal))
            dve.wait_ge(blocks_in, 16)
            dv = g.dblk[0:TN, :].rearrange("p (a b) -> p a b", b=BC)
            dve.tensor_reduce(g.bmax[0:TN, :], dv, AX.X, ALU.max)
            link(dve.tensor_reduce(g.bmin[0:TN, :], dv, AX.X, ALU.min))
            shape = [TN, NT, BR]
            lo = g.dtlo[0:TN, :].unsqueeze(2).broadcast_to(shape)
            bmin = g.bmin[0:TN, :].unsqueeze(1).broadcast_to(shape)
            bmax = g.bmax[0:TN, :].unsqueeze(1).broadcast_to(shape)
            blk = g.blk[0:TN, :].unsqueeze(1).broadcast_to(shape)
            ov, c2 = g.ov[0:TN, :, :], g.c2[0:TN, :, :]
            link(dve.tensor_scalar(g.bmin[0:TN, :], g.bmin[0:TN, :], float(TN - 1), None, ALU.subtract))
            link(dve.tensor_tensor(ov, bmin, lo, ALU.is_le))
            link(dve.tensor_tensor(c2, bmax, lo, ALU.is_ge))
            link(dve.tensor_tensor(ov, ov, c2, ALU.mult))
            link(dve.tensor_tensor(c2, ov, blk, ALU.mult))
            link(dve.scalar_tensor_tensor(out=ov, in0=ov, scalar=BIG, in1=c2, op0=ALU.mult, op1=ALU.subtract))
            link(dve.tensor_reduce(g.part[0:TN, 0:NT], ov, AX.X, ALU.max))
            link(dve.tensor_scalar(ov, ov, 0.0, float(BC), ALU.is_gt, ALU.mult))
            link(dve.tensor_tensor(c2, c2, ov, ALU.add))
            dve.tensor_reduce(g.part[0:TN, NT:2 * NT], c2, AX.X, ALU.max).then_inc(reduced, 1)
            dve.wait_ge(reduced, 2)
            neg, hi = g.red[:, 0:NT], g.red[:, NT:2 * NT]
            link(dve.tensor_scalar(g.lo[:, :], neg, -1.0, BIG, ALU.mult, ALU.add))
            link(dve.tensor_tensor(hi, hi, g.lo[:, :], ALU.subtract))
            link(dve.tensor_reduce(g.span[:, :], hi, AX.X, ALU.max))
            link(dve.tensor_scalar(g.span[:, :], g.span[:, :], 0.5, 1.0 / WIN, ALU.subtract, ALU.mult))
            link(dve.tensor_scalar(g.span[:, :], g.span[:, :], 0.5, 1.0, ALU.add, ALU.max))
            link(dve.tensor_copy(g.rounds[:, :], g.span[:, :]))
            sh = [P, RMAXN + 1, NT]
            link(dve.tensor_tensor(g.wfirst[:, :, :], g.lo[:, :].unsqueeze(1).broadcast_to(sh),
                                   g.rnd[:, :].unsqueeze(2).broadcast_to(sh), ALU.add))
            link(dve.tensor_scalar(g.c3[:, :, :], g.wfirst[:, :, :], float(E - WIN), None, ALU.min))
            link(dve.tensor_tensor(g.wfirst[:, :, :], g.wfirst[:, :, :], g.c3[:, :, :], ALU.subtract))
            link(dve.tensor_copy(g.wstart[:, :, :], g.c3[:, :, :]))
            link(dve.tensor_scalar(g.c3[:, 0, :], g.dtlo[:, :], -1.0, 1.0, ALU.mult, ALU.add))
            link(dve.tensor_copy(g.wnode[:, :, :], g.c3[:, 0, :].unsqueeze(1).broadcast_to(sh)))


NB_S = 2 * NT + 1
OHR = 4


def sort_phase(nc, g, sem):
    made, raw_in, conv_done, metaT_done, chain, ends_done, offs_ps, lo_done, perm_ps, unpacked, reduced = (
        sem(s) for s in ("made", "raw_in", "conv_done", "metaT_done", "chain", "ends_done", "offs_ps", "lo_done",
                         "perm_ps", "unpacked", "reduced"))
    sp_turn = sem("sp_turn")
    wstart = g.wstart[:, 0, :]
    wfirst, wnode = g.wfirst[:, 0, :], g.wnode[:, 0, :]
    oh = g.S1[:, 0:NT * W // 2].bitcast(BF16).rearrange("p (b w) -> p b w", w=W)
    pos = g.S2[:, 0:NT * W + 1]
    val = g.S3[:, 0:NT * W].rearrange("p (b w) -> p b w", w=W)
    ohlo = g.S1[:, 512:512 + OHR * P].rearrange("p (u f) -> p u f", u=OHR)
    rhs = g.S1[:, 1024:1024 + OHR * 2 * NB_S].rearrange("p (u f) -> p u f", u=OHR)
    names = ["mask", "dc", "valid", "code", "stile", "sloc", "packed", "weight", "bucket", "rank", "q", "low", "own",
             "slot", "third", "over", "overmax"]
    f = {n: g.wk[:, i * W:(i + 1) * W] for i, n in enumerate(names)}
    with nc.Block() as block:
        @block.sync
        def _(sp):
            with sp.Fori(0, NT) as gi:
                at = sp.value_load(wstart[0:1, bass.ds(gi, 1)], min_val=0, max_val=E - WIN)
                sp.wait_ge(conv_done, gi + 1)
                sp.sem_inc(sp_turn)
                sp.wait_ge(metaT_done, gi + 1)
                sp.sem_inc(sp_turn)
                for i, t in enumerate((g.dst, g.src, g.ety)):
                    sp.dma_start(g.rawi[i * W:(i + 1) * W, :],
                                 t[bass.ds(at, WIN)].rearrange("(w p) -> w p", p=P)).then_inc(raw_in, 16)
                sp.dma_start(g.raww[0:W, :], g.ewt[bass.ds(at, WIN)].rearrange("(w p) -> w p", p=P)).then_inc(raw_in, 16)

        @block.gpsimd
        def _(pool):
            io = dict(allow_small_or_imprecise_dtypes=True)
            pool.iota(g.diff[:, :], [[1, P]], base=0, channel_multiplier=-1, **io).then_inc(made, 1)
            pool.iota(g.iotaf[:, :], [[1, P]], base=1, channel_multiplier=0, **io).then_inc(made, 1)
            pool.iota(g.iotah[:, :], [[1, 512]], base=1, channel_multiplier=0, **io).then_inc(made, 1)
            pool.wait_ge(reduced, 1)
            pool.partition_all_reduce(g.flags[:, 1:2], g.flags[:, 0:1], P, RMAX).then_inc(reduced, 1)

        @block.tensor
        def _(pe):
            pe.sem_inc(metaT_done)
            pe.wait_ge(made, 8)
            with pe.Fori(0, NT) as gi:
                pe.wait_ge(raw_in, (gi + 1) * 64)
                pe.wait_ge(conv_done, gi + 2)
                pe.transpose(g.ps[:, 5, 0:3 * W], g.raww[0:3 * W, :], g.ident[0:3 * W, 0:3 * W])
                pe.transpose(g.ps[:, 6, 0:3 * W], g.meta[0:3 * W, :], g.ident[0:3 * W, 0:3 * W]).then_inc(metaT_done, 1)
                pe.wait_ge(ends_done, gi + 1)
                pe.matmul(g.ps[:, 7, 0:NT], g.before[:, :], pos[:, W:NT * W + 1:W], start=True, stop=False)
                pe.matmul(g.ps[:, 7, 0:NT], g.nbefore[:, :], pos[:, 0:NT * W:W], start=False, stop=True).then_inc(offs_ps, 1)
                for w in range(W):
                    if w == 0:
                        pe.wait_ge(unpacked, gi + 1)
                    pe.wait_ge(lo_done, gi * W + w + 1)
                    pe.matmul(g.ps[:, 0, 0:2 * NB_S], ohlo[:, w % OHR, :], rhs[:, w % OHR, :],
                              start=(w == 0), stop=(w == W - 1)).then_inc(perm_ps, 1)

        @block.vector
        def _(dve):
            links = 27
            n = [0]

            def link0(ins):
                n[0] += 1
                ins.then_inc(reduced, 1)
                dve.wait_ge(reduced, n[0])

            dve.sem_inc(unpacked)
            dve.wait_ge(made, 3)
            dve.tensor_scalar(g.before[:, :], g.diff[:, :], 0.0, None, ALU.is_gt).then_inc(made, 1)
            dve.tensor_scalar(g.nbefore[:, :], g.diff[:, :], 0.0, -1.0, ALU.is_ge, ALU.mult).then_inc(made, 1)
            dve.memset(g.raww[:, :], 0.0).then_inc(made, 1)
            dve.memset(pos[:, 0:1], 0.0).then_inc(made, 1)
            dve.memset(f["overmax"], 0.0).then_inc(made, 1)
            dve.wait_ge(made, 8)
            dve.sem_inc(conv_done)
            with dve.Fori(0, NT) as gi:
                made_n = [0]

                def link(ins):
                    made_n[0] += 1
                    ins.then_inc(chain, 1)
                    dve.wait_ge(chain, gi * links + made_n[0])

                dve.wait_ge(raw_in, (gi + 1) * 64)
                dve.tensor_copy(g.meta[0:3 * W, :], g.rawi[0:3 * W, :]).then_inc(conv_done, 1)
                link(dve.tensor_scalar(f["mask"], g.eidx[:, :], wfirst[:, bass.ds(gi, 1)], None, ALU.is_ge))
                dve.wait_ge(metaT_done, gi + 2)
                m = g.ps[:, 6, :]
                m_dst, m_src, m_type = m[:, 0:W], m[:, W:2 * W], m[:, 2 * W:3 * W]
                link(dve.scalar_tensor_tensor(out=f["dc"], in0=m_dst, scalar=wnode[:, bass.ds(gi, 1)], in1=f["mask"],
                                              op0=ALU.add, op1=ALU.mult))
                dve.tensor_copy(f["weight"], g.ps[:, 5, 0:W])
                dve.tensor_scalar(g.wi[:, 0:W], m_src, float(TN // 2), 1.0 / TN, ALU.subtract, ALU.mult)
                dve.scalar_tensor_tensor(out=f["code"], in0=m_type, scalar=float(TN), in1=f["dc"], op0=ALU.mult, op1=ALU.add)
                link(dve.tensor_scalar(f["valid"], f["dc"], 1.0, None, ALU.is_ge))
                link(dve.scalar_tensor_tensor(out=f["valid"], in0=f["dc"], scalar=float(TN), in1=f["valid"],
                                              op0=ALU.is_le, op1=ALU.mult))
                link(dve.tensor_copy(f["stile"], g.wi[:, 0:W]))
                dve.scalar_tensor_tensor(out=f["bucket"], in0=f["stile"], scalar=1.0, in1=f["valid"], op0=ALU.add, op1=ALU.mult)
                link(dve.scalar_tensor_tensor(out=f["sloc"], in0=f["stile"], scalar=-float(TN), in1=m_src,
                                              op0=ALU.mult, op1=ALU.add))
                link(dve.scalar_tensor_tensor(out=f["packed"], in0=f["sloc"], scalar=512.0, in1=f["code"],
                                              op0=ALU.mult, op1=ALU.add))
                link(dve.tensor_scalar(f["packed"], f["packed"], 512.0, None, ALU.add))
                sh = [P, NT, W]
                link(dve.tensor_tensor(oh, f["bucket"].unsqueeze(1).broadcast_to(sh),
                                       g.iotaf[:, 0:NT].unsqueeze(2).broadcast_to(sh), ALU.is_equal))
                ohf = g.S1[:, 0:NT * W // 2].bitcast(BF16)
                link(dve.tensor_tensor_scan(pos[:, 1:NT * W + 1], ohf, ohf, 0.0, ALU.add, ALU.max))
                dve.sem_inc(ends_done)
                dve.wait_ge(offs_ps, gi + 1)
                posv = pos[:, 1:NT * W + 1].rearrange("p (b w) -> p b w", w=W)
                link(dve.tensor_tensor(val, posv, g.ps[:, 7, 0:NT].unsqueeze(2).broadcast_to(sh), ALU.add))
                link(dve.tensor_tensor(val, val, oh, ALU.mult))
                link(dve.tensor_reduce(f["rank"], val.rearrange("p b w -> p w b"), AX.X, ALU.add))
                link(dve.tensor_scalar(g.wi[:, 0:W], f["rank"], 64.5, 1.0 / P, ALU.subtract, ALU.mult))
                link(dve.tensor_copy(f["q"], g.wi[:, 0:W]))
                dve.scalar_tensor_tensor(out=f["low"], in0=f["q"], scalar=-float(P), in1=f["rank"], op0=ALU.mult, op1=ALU.add)
                dve.tensor_scalar(f["own"], f["bucket"], g.iotaf[:, bass.ds(gi, 1)], None, ALU.is_equal)
                link(dve.scalar_tensor_tensor(out=f["slot"], in0=f["stile"], scalar=2.0, in1=f["q"], op0=ALU.mult, op1=ALU.add))
                dve.scalar_tensor_tensor(out=f["third"], in0=f["q"], scalar=2.0, in1=f["own"], op0=ALU.is_ge, op1=ALU.mult)
                dve.tensor_tensor(f["over"], f["q"], f["own"], ALU.subtract)
                link(dve.scalar_tensor_tensor(out=f["slot"], in0=f["slot"], scalar=1.0, in1=f["valid"], op0=ALU.add, op1=ALU.mult))
                link(dve.tensor_tensor(f["overmax"], f["overmax"], f["over"], ALU.max))
                link(dve.scalar_tensor_tensor(out=f["over"], in0=f["slot"], scalar=float(NB_S), in1=f["third"],
                                              op0=ALU.subtract, op1=ALU.mult))
                link(dve.tensor_tensor(f["slot"], f["slot"], f["over"], ALU.subtract))
                for w in range(W):
                    u = w % OHR
                    if w >= OHR:
                        dve.wait_ge(perm_ps, gi * W + w - OHR + 1)
                    dve.tensor_scalar(ohlo[:, u, :], g.iotaf[:, :], f["low"][:, w:w + 1], None, ALU.is_equal)
                    for i, what in enumerate(("packed", "weight")):
                        ins = dve.tensor_scalar(rhs[:, u, i * NB_S:(i + 1) * NB_S], g.iotaf[:, 0:NB_S],
                                                f["slot"][:, w:w + 1], f[what][:, w:w + 1], ALU.is_equal, ALU.mult)
                    ins.then_inc(lo_done, 1)
                dve.wait_ge(perm_ps, gi * W + W)
                pk, at = g.ps[:, 0, 0:NB_S], bass.ds(gi * NB_S, NB_S)
                wi, t1, t2 = g.wi[:, 0:NB_S], g.wk2[:, 0:NB_S], g.wk2[:, NB_S:2 * NB_S]
                dve.tensor_scalar(g.t_w[:, at], g.ps[:, 0, NB_S:2 * NB_S], 1.0, None, ALU.mult)
                link(dve.tensor_scalar(wi, pk, 255.5, 1.0 / 512, ALU.subtract, ALU.mult))
                link(dve.tensor_copy(t1, wi))
                link(dve.tensor_scalar(g.t_src[:, at], t1, 1.0, None, ALU.mult))
                link(dve.scalar_tensor_tensor(out=t2, in0=t1, scalar=-512.0, in1=pk, op0=ALU.mult, op1=ALU.add))
                dve.tensor_scalar(g.t_code[:, at], t2, 1.0, None, ALU.mult)
                dve.sem_inc(unpacked)
                link(dve.tensor_scalar(wi, t2, 63.0, 1.0 / TN, ALU.subtract, ALU.mult))
                link(dve.tensor_copy(t1, wi))
                link(dve.scalar_tensor_tensor(out=g.t_dst[:, at], in0=t1, scalar=-float(TN), in1=t2,
                                              op0=ALU.mult, op1=ALU.add))
                assert made_n[0] == links, made_n
            link0(dve.tensor_reduce(g.flags[:, 0:1], f["overmax"], AX.X, ALU.max))
            dve.wait_ge(reduced, 2)
            n[0] += 1
            link0(dve.tensor_copy(g.flags[:, 2:3], g.rounds[:, :]))
            link0(dve.tensor_scalar(g.flags[:, 3:4], g.flags[:, 1:2], 1.5, None, ALU.is_ge))
            link0(dve.scalar_tensor_tensor(out=g.flags[:, 4:5], in0=g.flags[:, 2:3], scalar=1.5, in1=g.flags[:, 3:4],
                                           op0=ALU.is_ge, op1=ALU.max))
            link0(dve.tensor_scalar(g.flags[:, 5:6], g.flags[:, 4:5], -1.0, 1.0, ALU.mult, ALU.add))
            link0(dve.tensor_tensor(g.flags[:, 6:7], g.flags[:, 4:5], g.flags[:, 2:3], ALU.mult))
            link0(dve.tensor_copy(g.path[:, :], g.flags[:, 4:7]))


def on_path(g, eng, path):
    if path == "both":
        return ExitStack()
    at = 1 if path == "dense" else 0
    return eng.If(eng.value_load(g.path[0:1, at:at + 1], min_val=0, max_val=1))


def group_of(b):
    return b // 4, b % 4


NBL = NT + 1
NGR = -(-NBL // 4)
TAKE = 20


def dense_weighted_phase(nc, g, sem):
    made, slots_used, mat_done, y_ps, added, x_in, x_copied, sp_turn, chain = (
        sem(s) for s in ("made", "slots_used", "mat_done", "y_ps", "added", "x_in", "x_copied", "sp_turn",
                         "chain"))
    ohd = g.S1[:, 0:OHR * P].rearrange("p (u f) -> p u f", u=OHR)
    ohs = g.S1[:, 512:512 + OHR * P].rearrange("p (u f) -> p u f", u=OHR)
    mat = g.S2[:, 0:1024].rearrange("p (u f) -> p u f", u=2)
    xnext, xcur = g.S3[0:TN, 0:P], g.S3[0:TN, P:2 * P]
    with nc.Block() as block:
        @block.sync
        def _(sp):
            with on_path(g, sp, "dense"):
                sp.sem_inc(x_copied)
                with sp.Fori(0, NT) as dt:
                    sp.wait_ge(x_copied, dt + 1)
                    sp.sem_inc(sp_turn)
                    sp.dma_start(xnext, g.x[bass.ds(dt * TN, TN), :]).then_inc(x_in, 16)

        @block.vector
        def _(dve):
            with on_path(g, dve, "dense"):
                dve.memset(g.acc[:, :], 0.0).then_inc(added, 1)
                dve.wait_ge(added, 1)
                dve.sem_inc(added, 2)
                with dve.Fori(0, NT) as dt:
                    def take(gr):
                        dve.wait_ge(y_ps, dt * NGR + gr + 2)
                        ps = g.ps[:, 4 + gr % 2, :]
                        if gr < NGR - 1:
                            a = g.acc[:, gr * 4 * TN:(gr + 1) * 4 * TN]
                            dve.wait_ge(added, dt * (NGR + 1) + gr + 3)
                            dve.tensor_tensor(a, a, ps[:, 0:4 * TN], ALU.add).then_inc(added, 1)
                            return
                        a = g.acc[:, (NT - 1) * TN:NT * TN]
                        dve.wait_ge(added, dt * (NGR + 1) + NGR + 2)
                        dve.tensor_tensor(a, a, ps[:, 0:TN], ALU.add).then_inc(added, 1)
                        dve.wait_ge(added, dt * (NGR + 1) + NGR + 3)
                        a = g.acc[:, bass.ds(dt * TN, TN)]
                        dve.tensor_tensor(a, a, ps[:, TN:2 * TN], ALU.add).then_inc(added, 1)

                    for t in range(NB_S):
                        u = t % OHR
                        at = bass.ds(dt * NB_S + t, 1)
                        dve.wait_ge(slots_used, dt * NB_S + t + 1)
                        dve.tensor_scalar(ohd[:, u, 0:TN], g.iotaf[:, 0:TN], g.t_dst[:, at], None, ALU.is_equal)
                        dve.tensor_scalar(ohs[:, u, 0:TN], g.iotaf[:, 0:TN], g.t_src[:, at], g.t_w[:, at],
                                          ALU.is_equal, ALU.mult).then_inc(made, 1)
                        if t >= TAKE and (t - TAKE) % 8 == 0:
                            take((t - TAKE) // 8)
                    for gr in range((NB_S - 1 - TAKE) // 8 + 1, NGR):
                        take(gr)

        @block.tensor
        def _(pe):
            with on_path(g, pe, "dense"):
                pe.sem_inc(slots_used, OHR)
                with pe.Fori(0, NT) as dt:
                    def times_x(gr):
                        if gr == 0:
                            pe.wait_ge(x_copied, dt + 2)
                        n = 4 * TN if gr < NGR - 1 else 2 * TN
                        pe.wait_ge(mat_done, dt * NGR + gr + 3)
                        pe.wait_ge(added, dt * (NGR + 1) + (3, 1)[gr] if gr < 2 else dt * (NGR + 1) + gr + 2)
                        pe.matmul(g.ps[:, 4 + gr % 2, 0:n], xcur, mat[0:TN, gr % 2, 0:n], start=True, stop=True
                                  ).then_inc(y_ps, 1)

                    for b in range(NBL):
                        gr, c = group_of(b)
                        if c == 0:
                            pe.wait_ge(mat_done, dt * NGR + max(gr + 1, 2))
                        ts = range(2 * b, min(2 * b + 2, NB_S))
                        for t in ts:
                            pe.wait_ge(made, dt * NB_S + t + 1)
                            mm = pe.matmul(g.ps[0:TN, gr % 2, c * TN:(c + 1) * TN], ohd[:, t % OHR, 0:TN],
                                           ohs[:, t % OHR, 0:TN], start=(t == ts[0]), stop=(t == ts[-1]))
                            mm.then_inc(slots_used, 1)
                        if c == 1 and gr:
                            times_x(gr - 1)
                    times_x(NGR - 1)

        @block.scalar
        def _(act):
            with on_path(g, act, "dense"):
                act.sem_inc(mat_done, 2)
                act.sem_inc(y_ps)
                with act.Fori(0, NT) as dt:
                    for gr in range(NGR):
                        n = 4 * TN if gr < NGR - 1 else 2 * TN
                        if gr == 0:
                            act.wait_ge(y_ps, dt * NGR + 1)
                            act.wait_ge(x_in, dt * 16 + 16)
                            act.activation(xcur, xnext, ACT.Copy).then_inc(x_copied, 1)
                        act.wait_ge(slots_used, dt * NB_S + min(8 * gr + 8, NB_S) + OHR)
                        act.wait_ge(y_ps, dt * NGR + max(gr, 1))
                        act.activation(mat[0:TN, gr % 2, 0:n], g.ps[0:TN, gr % 2, 0:n], ACT.Copy).then_inc(mat_done, 1)


def part_tile(part, b):
    return part[0:TN, b * D:(b + 1) * D]


def split_phase(nc, g, sem, feats, dt16, n):
    tile_ps, hi_done, rest_done, mid_done, low_done = (sem(s) for s in ("tile_ps", "hi_done", "rest_done", "mid_done",
                                                                     "low_done"))
    parts = [p.bitcast(dt16) for p in g.parts]
    rest = g.S1[:, 1600:1600 + 4 * P].rearrange("p (u f) -> p u f", u=4)
    with nc.Block() as block:
        @block.tensor
        def _(pe):
            with on_path(g, pe, "dense"):
                for b in range(NT):
                    if b >= 4:
                        pe.wait_ge(low_done, b - 3)
                    pe.transpose(g.ps[0:TN, b % 4, 0:P], feats[:, b * TN:(b + 1) * TN], g.ident[:, :]).then_inc(tile_ps, 1)

        @block.scalar
        def _(act):
            with on_path(g, act, "dense"):
                for b in range(NT):
                    act.wait_ge(tile_ps, b + 1)
                    act.activation(part_tile(parts[0], b), g.ps[0:TN, b % 4, 0:P], ACT.Copy).then_inc(hi_done, 1)

        @block.vector
        def _(dve):
            with on_path(g, dve, "dense"):
                for b in range(NT):
                    dve.wait_ge(hi_done, b + 1)
                    ps = g.ps[0:TN, b % 4, 0:P]
                    if n == 2:
                        dve.tensor_tensor(part_tile(parts[1], b), ps, part_tile(parts[0], b), ALU.subtract
                                          ).then_inc(low_done, 1)
                        continue
                    r = rest[0:TN, b % 4, :]
                    if b >= 4:
                        dve.wait_ge(low_done, b - 3)
                    dve.tensor_tensor(r, ps, part_tile(parts[0], b), ALU.subtract).then_inc(rest_done, 1)
                    dve.wait_ge(rest_done, b + 1)
                    dve.tensor_copy(part_tile(parts[1], b), r).then_inc(mid_done, 1)
                    dve.wait_ge(mid_done, b + 1)
                    dve.tensor_tensor(part_tile(parts[2], b), r, part_tile(parts[1], b), ALU.subtract).then_inc(low_done, 1)


def dense_typed_phase(nc, g, sem, first):
    made, slots_used, mat_done, agg_done, sums_out, a_ps, a_taken, chain = (
        sem(s) for s in ("made", "slots_used", "mat_done", "agg_done", "sums_out", "a_ps", "a_taken", "chain"))
    KT = K * TN
    parts = [p.bitcast(F16) for p in g.parts]
    ohk = g.S1[:, 1600:2624].bitcast(F16).rearrange("p (u f) -> p u f", u=OHR)
    mat = g.S2[:, 1600:1600 + 768].bitcast(F16).rearrange("p (u f) -> p u f", u=3)
    ohs = g.S2[:, 2400:2400 + OHR * 64].bitcast(F16).rearrange("p (u f) -> p u f", u=OHR)
    sums, deg, degt = g.S3[:, 1600:1600 + KT], g.S3[:, 2112:2112 + KT], g.S3[:, 2624:2624 + TN]
    ones = g.ones16
    bias = g.rows[:, :, :].rearrange("p u f -> p (u f)")
    with nc.Block() as block:
        @block.vector
        def _(dve):
            with on_path(g, dve, "dense"):
                dve.sem_inc(sums_out)
                dve.sem_inc(a_taken)
                with dve.Fori(0, NT) as dt:
                    for t in range(NB_S):
                        u = t % OHR
                        at = bass.ds(dt * NB_S + t, 1)
                        dve.wait_ge(slots_used, dt * NB_S + t + 1)
                        dve.tensor_scalar(ohs[:, u, 0:TN], g.iotah[:, 0:TN], g.t_src[:, at], None, ALU.is_equal)
                        dve.tensor_scalar(ohk[:, u, 0:KT], g.iotah[:, 0:KT], g.t_code[:, at], None, ALU.is_equal
                                          ).then_inc(made, 1)
                    dve.wait_ge(agg_done, (dt + 1) * NBL + 1)
                    if first:
                        dve.tensor_copy(deg, g.ps[:, 4, 0:KT])
                    dve.tensor_copy(sums, g.ps[:, 3, 0:KT]).then_inc(sums_out, 1)
                    at = bass.ds(dt * TN, TN)
                    if first:
                        dve.wait_ge(sums_out, dt + 2)
                        dve.tensor_reduce(degt, deg.rearrange("p (k n) -> p n k", k=K), AX.X, ALU.add).then_inc(chain, 1)
                        dve.wait_ge(chain, dt * 2 + 1)
                        dve.tensor_scalar(g.rdeg[:, at], degt, 1.0, None, ALU.mult)
                    dve.wait_ge(a_ps, dt + 1)
                    if first:
                        dve.tensor_scalar(bias[:, at], g.ps[:, 6, 0:TN], 1.0, None, ALU.mult).then_inc(chain, 1)
                        dve.wait_ge(chain, dt * 2 + 2)
                    dve.tensor_tensor(g.acc[:, at], g.ps[:, 5, 0:TN], bias[:, at], ALU.add).then_inc(a_taken, 1)

        @block.tensor
        def _(pe):
            with on_path(g, pe, "dense"):
                pe.sem_inc(slots_used, OHR)
                with pe.Fori(0, NT) as dt:
                    def aggregate(b):
                        if b == 0:
                            pe.wait_ge(sums_out, dt + 1)
                        pe.wait_ge(mat_done, dt * NBL + b + 2)
                        m = mat[0:TN, b % 3, 0:KT]
                        for i, p in enumerate(parts[0:2]):
                            rows = part_tile(p, b) if b < NT else p[0:TN, bass.ds(dt * D, D)]
                            mm = pe.matmul(g.ps[:, 3, 0:KT], rows, m, start=(b == 0 and i == 0),
                                           stop=(b == NBL - 1 and i == 1))
                        if first:
                            mm = pe.matmul(g.ps[:, 4, 0:KT], ones[0:TN, :], m, start=(b == 0), stop=(b == NBL - 1))
                        mm.then_inc(agg_done, 1)

                    for b in range(NBL + 2):
                        if b < NBL:
                            pe.wait_ge(mat_done, dt * NBL + max(b - 1, 1))
                            ts = range(2 * b, min(2 * b + 2, NB_S))
                            for t in ts:
                                pe.wait_ge(made, dt * NB_S + t + 1)
                                pe.matmul(g.ps[0:TN, b % 3, 0:KT], ohs[:, t % OHR, 0:TN], ohk[:, t % OHR, 0:KT],
                                          start=(t == ts[0]), stop=(t == ts[-1])).then_inc(slots_used, 1)
                        if b >= 2:
                            aggregate(b - 2)
                    pe.wait_ge(sums_out, dt + 2)
                    pe.wait_ge(a_taken, dt + 1)
                    if first:
                        for k in range(K):
                            pe.matmul(g.ps[:, 6, 0:TN], g.brow[0:1, k * D:(k + 1) * D], deg[0:1, k * TN:(k + 1) * TN],
                                      start=(k == 0), stop=(k == K - 1))
                    for k in range(K):
                        mm = pe.matmul(g.ps[:, 5, 0:TN], g.wt(f"wet{k}"), sums[:, k * TN:(k + 1) * TN],
                                       start=(k == 0), stop=(k == K - 1))
                    mm.then_inc(a_ps, 1)

        @block.scalar
        def _(act):
            with on_path(g, act, "dense"):
                act.sem_inc(mat_done)
                act.sem_inc(agg_done)
                with act.Fori(0, NT) as dt:
                    for b in range(NBL):
                        act.wait_ge(slots_used, dt * NB_S + min(2 * b + 2, NB_S) + OHR)
                        act.wait_ge(agg_done, dt * NBL + max(b - 1, 1))
                        act.activation(mat[0:TN, b % 3, 0:KT], g.ps[0:TN, b % 3, 0:KT], ACT.Copy).then_inc(mat_done, 1)


def dense_plain_phase(nc, g, sem):
    made, slots_used, mat_done, agg_done, sums_out = (
        sem(s) for s in ("made", "slots_used", "mat_done", "agg_done", "sums_out"))
    parts = [p.bitcast(BF16) for p in g.parts]
    oh = [g.S1[:, lo:lo + OHR * 64].bitcast(BF16).rearrange("p (u f) -> p u f", u=OHR) for lo in (1600, 1900)]
    mat = g.S2[:, 1600:1600 + 512].bitcast(BF16).rearrange("p (u f) -> p u f", u=2)
    with nc.Block() as block:
        @block.vector
        def _(dve):
            with on_path(g, dve, "dense"):
                dve.sem_inc(sums_out)
                with dve.Fori(0, NT) as dt:
                    for t in range(NB_S):
                        u = t % OHR
                        at = bass.ds(dt * NB_S + t, 1)
                        dve.wait_ge(slots_used, dt * NB_S + t + 1)
                        dve.tensor_scalar(oh[0][:, u, 0:TN], g.iotah[:, 0:TN], g.t_src[:, at], None, ALU.is_equal)
                        dve.tensor_scalar(oh[1][:, u, 0:TN], g.iotah[:, 0:TN], g.t_dst[:, at], None, ALU.is_equal
                                          ).then_inc(made, 1)
                    dve.wait_ge(agg_done, (dt + 1) * NGR + 1)
                    dve.tensor_scalar(g.acc[:, bass.ds(dt * TN, TN)], g.ps[:, 2, 0:TN], 1.0, None, ALU.mult
                                      ).then_inc(sums_out, 1)

        @block.tensor
        def _(pe):
            with on_path(g, pe, "dense"):
                pe.sem_inc(slots_used, OHR)
                with pe.Fori(0, NT) as dt:
                    def aggregate(gr):
                        if gr == 0:
                            pe.wait_ge(sums_out, dt + 1)
                        pe.wait_ge(mat_done, dt * NGR + gr + 3)
                        for b in range(4 * gr, min(4 * gr + 4, NBL)):
                            for i, p in enumerate(parts):
                                rows = part_tile(p, b) if b < NT else p[0:TN, bass.ds(dt * D, D)]
                                mm = pe.matmul(g.ps[:, 2, 0:TN], rows, mat[0:TN, gr % 2, (b % 4) * TN:(b % 4 + 1) * TN],
                                               start=(b == 0 and i == 0), stop=(b == NBL - 1 and i == 2))
                        mm.then_inc(agg_done, 1)

                    for b in range(NBL):
                        gr, c = group_of(b)
                        if c == 0:
                            pe.wait_ge(mat_done, dt * NGR + max(gr + 1, 2))
                        ts = range(2 * b, min(2 * b + 2, NB_S))
                        for t in ts:
                            pe.wait_ge(made, dt * NB_S + t + 1)
                            pe.matmul(g.ps[0:TN, gr % 2, c * TN:(c + 1) * TN], oh[0][:, t % OHR, 0:TN],
                                      oh[1][:, t % OHR, 0:TN], start=(t == ts[0]), stop=(t == ts[-1])
                                      ).then_inc(slots_used, 1)
                        if c == 1 and gr:
                            aggregate(gr - 1)
                    aggregate(NGR - 1)

        @block.scalar
        def _(act):
            with on_path(g, act, "dense"):
                act.sem_inc(mat_done, 2)
                act.sem_inc(agg_done)
                with act.Fori(0, NT) as dt:
                    for gr in range(NGR):
                        n = 4 * TN if gr < NGR - 1 else 2 * TN
                        act.wait_ge(slots_used, dt * NB_S + min(8 * gr + 8, NB_S) + OHR)
                        act.wait_ge(agg_done, dt * NGR + max(gr, 1))
                        act.activation(mat[0:TN, gr % 2, 0:n], g.ps[0:TN, gr % 2, 0:n], ACT.Copy).then_inc(mat_done, 1)


ET = -(-E // P)
SG, SR = 26, 13
NB, BW = 7, 448
assert ET % SG == 0 and SG % SR == 0 and NB * BW == NP


def scatter_phase(nc, g, sem):
    edges_in, made, idx_now, turn, rows_used, split_done, onehot_done, tile_added, chain, taken, zeroed, zeros_added = (
        sem(s) for s in ("edges_in", "made", "idx_now", "turn", "rows_used", "split_done", "onehot_done",
                         "tile_added", "chain", "taken", "zeroed", "zeros_added"))
    src_i = g.S3[:, 0:ET].bitcast(I32)
    dst_i = g.S3[:, ET:2 * ET].bitcast(I32)
    src_f, wgt = g.S3[:, 2 * ET:3 * ET], g.H[:, 0:ET]
    nodes = g.H[:, ET:ET + NP // 2].bitcast(mybir.dt.int16)
    oh = [t[:, 0:NP // 2].bitcast(BF16) for t in (g.S1, g.S2)]
    h1, h2, h3 = (g.attr[:, 0, k * P:(k + 1) * P].bitcast(BF16).rearrange("p (u f) -> p u f", u=2) for k in range(3))
    rest = g.attr[:, 0, 3 * P:5 * P].rearrange("p (u f) -> p u f", u=2)
    zero = g.attr[:, 0, 5 * P:5 * P + BW // 2].bitcast(BF16)
    with nc.Block() as block:
        @block.sync
        def _(sp):
            with on_path(g, sp, "general"):
                sp.dma_start(dst_i, g.dst_pt).then_inc(edges_in, 16)
                sp.dma_start(src_i, g.src_pt).then_inc(edges_in, 16)
                sp.dma_start(wgt, g.ewt_pt).then_inc(edges_in, 16)

        @block.gpsimd
        def _(pool):
            with on_path(g, pool, "general"):
                pool.iota(nodes, [[1, NP]], base=0, channel_multiplier=0,
                          allow_small_or_imprecise_dtypes=True).then_inc(made, 1)
                pool.wait_ge(edges_in, 48)
                with pool.Fori(0, ET // SG) as i:
                    for h in range(SG // SR):
                        pool.wait_ge(rows_used, i * SG + h * SR + 1)
                        pool.sem_inc(turn)
                        pool.tensor_copy(g.gnow[:, h * SR:(h + 1) * SR], dst_i[:, bass.ds(i * SG + h * SR, SR)]).then_inc(idx_now, 1)
                        pool.wait_ge(idx_now, i * 2 + h + 1)
                        pool.sem_inc(turn)
                        for u in range(SR):
                            pool.wait_ge(rows_used, i * SG + h * SR + u + 2)
                            pool.sem_inc(turn)
                            pool.indirect_dma_start(g.rows[:, u, 0:D], None, g.x,
                                                    bass.IndirectOffsetOnAxis(g.gnow[:, h * SR + u:h * SR + u + 1], 0)
                                                    ).then_inc(g.rows_in[u], 16)

        @block.vector
        def _(dve):
            with on_path(g, dve, "general"):
                dve.sem_inc(rows_used, SR + 1)
                dve.memset(zero, 0.0).then_inc(zeroed, 1)
                dve.wait_ge(edges_in, 48)
                dve.tensor_copy(src_f, src_i).then_inc(chain, 1)
                dve.wait_ge(chain, 1)
                dve.wait_ge(made, 1)
                with dve.Fori(0, ET // SG) as i:
                    for u in range(SG):
                        t = i * SG + u
                        w = wgt[:, bass.ds(t, 1)]
                        b = u % 2
                        dve.wait_ge(tile_added, t + 1)
                        dve.tensor_scalar(oh[b], nodes, src_f[:, bass.ds(t, 1)], None, ALU.is_equal
                                          ).then_inc(onehot_done, 1)
                        dve.wait_ge(g.rows_in[u % SR], (i * 2 + u // SR + 1) * 16)
                        row = g.rows[:, u % SR, 0:D]
                        dve.tensor_scalar(h1[:, b, :], row, w, None, ALU.mult).then_inc(chain, 1)
                        dve.wait_ge(chain, t * 3 + 2)
                        dve.scalar_tensor_tensor(out=rest[:, b, :], in0=row, scalar=w, in1=h1[:, b, :], op0=ALU.mult,
                                                 op1=ALU.subtract).then_inc(chain, 1)
                        dve.wait_ge(chain, t * 3 + 3)
                        dve.sem_inc(rows_used)
                        dve.tensor_scalar(h2[:, b, :], rest[:, b, :], 1.0, None, ALU.mult).then_inc(chain, 1)
                        dve.wait_ge(chain, t * 3 + 4)
                        dve.tensor_tensor(h3[:, b, :], rest[:, b, :], h2[:, b, :], ALU.subtract).then_inc(split_done, 1)
                dve.wait_ge(zeros_added, 1)
                for c in range(NB):
                    dve.tensor_copy(g.acc[:, c * BW:(c + 1) * BW], g.ps[:, c, 0:BW]).then_inc(taken, 1)

        @block.tensor
        def _(pe):
            with on_path(g, pe, "general"):
                pe.sem_inc(tile_added, 2)
                pe.wait_ge(zeroed, 1)
                for c in range(NB):
                    pe.matmul(g.ps[:, c, 0:BW], zero[:, 0:P], zero, start=True, stop=False, skip_group_check=True)
                with pe.Fori(0, ET // SG) as i:
                    for u in range(SG):
                        t = i * SG + u
                        b = u % 2
                        pe.wait_ge(onehot_done, t + 1)
                        pe.wait_ge(split_done, t + 1)
                        for part in (h1, h2, h3):
                            for c in range(NB):
                                mm = pe.matmul(g.ps[:, c, 0:BW], part[:, b, :], oh[b][:, c * BW:(c + 1) * BW],
                                               start=False, stop=False, skip_group_check=True)
                        mm.then_inc(tile_added, 1)
                for c in range(NB):
                    mm = pe.matmul(g.ps[:, c, 0:BW], zero[:, 0:P], zero, start=False, stop=True, skip_group_check=True)
                mm.then_inc(zeros_added, 1)


def edge_phase(nc, g, sem, kind, table, width, before, deg=False):
    L1, L3 = kind == "L1", kind == "L3"
    raw_in, conv_done, metaT_done, idx_done = sem("raw_in"), sem("conv_done"), sem("metaT_done"), sem("idx_done")
    rows_in = g.rows_in
    attr_in = [sem(f"attr_in{i}") for i in range(2)]
    idx_now, sp_turn = sem("idx_now"), sem("sp_turn")
    turn, tile_added, onehot_done, acc_done, chain = (
        sem("turn"), sem("tile_added"), sem("onehot_done"), sem("acc_done"), sem("chain"))
    ohT_ps, ohT_done, edge_ps, pre_ps, pre_done, sig_done, msg_done = (
        sem("ohT_ps"), sem("ohT_done"), sem("edge_ps"), sem("pre_ps"), sem("pre_done"), sem("sig_done"),
        sem("msg_done"))
    CR = RING + 1
    n_meta = 3 if L1 else 2
    rows_done = msg_done if L3 else tile_added

    def old(w, ring):
        return w - ring + 1 if w >= ring else 0

    def rounds_of(eng):
        return (eng.value_load(g.rounds[0:1, 0:1], min_val=1, max_val=RMAXN),
                eng.value_load(g.path[0:1, 2:3], min_val=0, max_val=RMAXN))

    wstart = g.wstart[:, :, :].rearrange("p a b -> p (a b)")
    wfirst = g.wfirst[:, :, :].rearrange("p a b -> p (a b)")
    wnode = g.wnode[:, :, :].rearrange("p a b -> p (a b)")

    with nc.Block() as block:
        @block.sync
        def _(sp):
            with on_path(g, sp, "both" if L3 else "general"):
                rounds, _ = rounds_of(sp)

                def load_meta(gi, at):
                    def win(t):
                        return t[bass.ds(at, WIN)].rearrange("(w p) -> w p", p=P)
                    sp.wait_ge(conv_done, gi + 1)
                    sp.sem_inc(sp_turn)
                    sp.dma_start(g.rawi[0:W, :], win(g.dst)).then_inc(raw_in, 16)
                    sp.dma_start(g.rawi[W:2 * W, :], win(g.src)).then_inc(raw_in, 16)
                    if L1:
                        sp.dma_start(g.rawi[2 * W:3 * W, :], win(g.ety)).then_inc(raw_in, 16)

                with sp.Fori(0, rounds * NT) as gi:
                    at = sp.value_load(wstart[0:1, bass.ds(gi, 1)], min_val=0, max_val=E - WIN)
                    load_meta(gi, at)
                    if L3:
                        for half in range(2):
                            sp.wait_ge(edge_ps, gi * W + half * RING + 1)
                            sp.sem_inc(sp_turn)
                            sp.dma_start(g.attr[:, half, :],
                                         g.d_attrT[:, bass.ds(at + half * RING * P, RING * P)]).then_inc(attr_in[half], 16)
                last = sp.snap(rounds * NT)
                at = sp.value_load(wstart[0:1, bass.ds(last, 1)], min_val=0, max_val=E - WIN)
                load_meta(last, at)

        @block.gpsimd
        def _(pool):
            with on_path(g, pool, "both" if L3 else "general"):
                rounds, _ = rounds_of(pool)
                groups = [0, 4, 8, 12, RING, RING + 4, RING + 8, RING + 12, W]
                with pool.Fori(0, rounds * NT) as gi:
                    par = pool.snap((gi % 2) * W)
                    pool.wait_ge(idx_done, gi + 1)
                    pool.sem_inc(turn)
                    for a, b in zip(groups, groups[1:]):
                        pool.wait_ge(rows_done, gi * W + b + 1)
                        pool.sem_inc(turn)
                        if a % RING == 0:
                            half = a // RING
                            pool.tensor_copy(g.gnow[:, a:a + RING], g.gidx[:, bass.ds(par + a, RING)]).then_inc(idx_now, 1)
                            pool.wait_ge(idx_now, gi * 2 + half + 1)
                            pool.sem_inc(turn)
                        for w in range(a, b):
                            pool.indirect_dma_start(g.rows[:, w % RING, 0:width], None, table,
                                                    bass.IndirectOffsetOnAxis(g.gnow[:, w:w + 1], 0)
                                                    ).then_inc(rows_in[w % RING], 16)

        @block.tensor
        def _(pe):
            with on_path(g, pe, "both" if L3 else "general"):
                rounds, slow_rounds = rounds_of(pe)
                base = pe.snap(slow_rounds * (NT * 2 * 16 * before))
                scattered = pe.snap(pe.value_load(g.path[0:1, 0:1], min_val=0, max_val=1) * (ET // SR * 16))

                def transpose_meta(gi):
                    pe.wait_ge(conv_done, gi + 2)
                    pe.transpose(g.ps[:, 6, 0:n_meta * W], g.meta[0:n_meta * W, :],
                                 g.ident[0:n_meta * W, 0:n_meta * W]).then_inc(metaT_done, 1)

                def add_up(gi, w, rows):
                    if w == 0:
                        pe.wait_ge(acc_done, gi + 1)
                    mm = pe.matmul(g.ps[:, 0, 0:TN], rows, g.oh[:, w % RING, :], start=(w == 0), stop=(w == W - 1))
                    if deg:
                        mm = pe.matmul(g.ps[:, 1, 0:TN], g.ones[:, :], g.oh[:, w % RING, :],
                                       start=(w == 0), stop=(w == W - 1))
                    mm.then_inc(tile_added, 1)

                pe.sem_inc(metaT_done)
                pe.sem_inc(edge_ps, CR)
                pe.sem_inc(tile_added, CR)
                pe.sem_inc(pre_ps, 2)
                transpose_meta(0)
                with pe.Fori(0, rounds) as r:
                    with pe.Fori(0, NT) as dt:
                        gi = pe.snap(r * NT + dt)
                        for w in range(W + (S_LAG if L3 else 0)):
                            if w == W // 2 - 1:
                                transpose_meta(gi + 1)
                            if not L3:
                                pe.wait_ge(onehot_done, gi * W + w + 1)
                                pe.wait_ge(rows_in[w % RING], (gi * 2 + w // RING + 1) * 16 + base + (scattered if w % RING < SR else 0))
                                add_up(gi, w, g.rows[:, w % RING, 0:D])
                                continue
                            if w < W:
                                pe.wait_ge(onehot_done, gi * W + w + 1)
                                pe.wait_ge(ohT_done, gi * W + w + 1)
                                pe.transpose(g.ps[0:TN, 2 + w % 2, 0:P], g.oh[:, w % RING, :],
                                             g.ident[:, :]).then_inc(ohT_ps, 1)
                                if w % RING == 0:
                                    pe.wait_ge(attr_in[w // RING], (gi + 1) * 16)
                                pe.wait_ge(pre_done, gi * W + w + 1)
                                pe.matmul(g.ps[:, 4 + w % 2, 0:D],
                                          g.attr[:, w // RING, (w % RING) * P:(w % RING + 1) * P],
                                          g.wt("we"), start=True, stop=False).then_inc(edge_ps, 1)
                            if 1 <= w <= W:
                                u = w - 1
                                pe.wait_ge(ohT_done, gi * W + u + 3)
                                pe.matmul(g.ps[:, 4 + u % 2, 0:D], g.ohT[0:TN, u % 2, :],
                                          g.C[0:TN, bass.ds(dt * D, D)], start=False, stop=True).then_inc(pre_ps, 1)
                            if w >= S_LAG:
                                u = w - S_LAG
                                pe.wait_ge(msg_done, gi * W + u + 1 + CR)
                                add_up(gi, u, g.msg[:, u % 4, :])

        @block.vector
        def _(dve):
            with on_path(g, dve, "both" if L3 else "general"):
                rounds, slow_rounds = rounds_of(dve)
                base = dve.snap(slow_rounds * (NT * 2 * 16 * before))
                scattered = dve.snap(dve.value_load(g.path[0:1, 0:1], min_val=0, max_val=1) * (ET // SR * 16))
                links = 4 if L1 else 3

                def prepare(gi):
                    made = [0]

                    def link(ins):
                        made[0] += 1
                        ins.then_inc(chain, 1)
                        dve.wait_ge(chain, gi * links + made[0])

                    par = dve.snap((gi % 2) * W)
                    ints = 3 * W if L1 else 2 * W
                    dve.wait_ge(raw_in, (gi + 1) * 16 * n_meta)
                    dve.tensor_copy(g.meta[0:ints, :], g.rawi[0:ints, :]).then_inc(conv_done, 1)
                    link(dve.tensor_scalar(g.mask[:, :], g.eidx[:, :], wfirst[:, bass.ds(gi, 1)], None, ALU.is_ge))
                    dve.wait_ge(metaT_done, gi + 2)
                    m = g.ps[:, 6, :]
                    link(dve.scalar_tensor_tensor(out=g.dcol[:, bass.ds(par, W)], in0=m[:, 0:W],
                                                  scalar=wnode[:, bass.ds(gi, 1)], in1=g.mask[:, :],
                                                  op0=ALU.add, op1=ALU.mult))
                    if L1:
                        link(dve.tensor_scalar(g.tmpw[:, :], m[:, 2 * W:3 * W], float(N), None, ALU.mult))
                        link(dve.tensor_tensor(g.gidx[:, bass.ds(par, W)], g.tmpw[:, :], m[:, W:2 * W], ALU.add))
                    else:
                        link(dve.tensor_scalar(g.gidx[:, bass.ds(par, W)], m[:, W:2 * W], 1.0, None, ALU.mult))
                    assert made[0] == links
                    dve.sem_inc(idx_done)

                dve.sem_inc(conv_done)
                dve.sem_inc(acc_done)
                dve.sem_inc(pre_done, 2)
                dve.sem_inc(msg_done, CR)
                dve.memset(g.acc[:, :], 0.0).then_inc(acc_done, 1)
                dve.wait_ge(acc_done, 2)
                prepare(0)
                with dve.Fori(0, rounds) as r:
                    with dve.Fori(0, NT) as dt:
                        gi = dve.snap(r * NT + dt)
                        par = dve.snap((gi % 2) * W)
                        for w in range(W + (MUL_LAG if L3 else 0)):
                            if w == W // 2 - 1:
                                prepare(gi + 1)
                            if w < W:
                                dve.wait_ge(tile_added, gi * W + w + 2)
                                dc = g.dcol[:, bass.ds(par + w, 1)]
                                dve.tensor_scalar(g.oh[:, w % RING, :], g.iota1[:, :], dc, None, ALU.is_equal
                                                  ).then_inc(onehot_done, 1)
                            if L3 and PRE_LAG <= w < W + PRE_LAG:
                                u = w - PRE_LAG
                                dve.wait_ge(pre_ps, gi * W + u + 3)
                                dve.wait_ge(rows_in[u % RING], (gi * 2 + u // RING + 1) * 16 + base + (scattered if u % RING < SR else 0))
                                dve.wait_ge(sig_done, gi * W + old(u, 4) + 1)
                                dve.tensor_tensor(g.pre[:, u % 4, :], g.ps[:, 4 + u % 2, 0:D], g.rows[:, u % RING, 0:D],
                                                  ALU.add).then_inc(pre_done, 1)
                            if L3 and w >= MUL_LAG:
                                u = w - MUL_LAG
                                dve.wait_ge(sig_done, gi * W + u + 2)
                                dve.wait_ge(tile_added, gi * W + old(u, 4) + CR)
                                dve.tensor_tensor(g.msg[:, u % 4, :], g.sig[:, u % 4, :], g.rows[:, u % RING, D:2 * D],
                                                  ALU.mult).then_inc(msg_done, 1)
                        dve.wait_ge(tile_added, gi * W + W + CR)
                        dve.wait_ge(acc_done, gi + 2)
                        a = g.acc[:, bass.ds(dt * TN, TN)]
                        if deg:
                            q = g.rdeg[:, bass.ds(dt * TN, TN)]
                            dve.tensor_tensor(q, q, g.ps[:, 1, 0:TN], ALU.add)
                        dve.tensor_tensor(a, a, g.ps[:, 0, 0:TN], ALU.add).then_inc(acc_done, 1)

        @block.scalar
        def _(act):
            with on_path(g, act, "both" if L3 else "general"):
                if not L3:
                    return
                rounds, _ = rounds_of(act)
                act.sem_inc(ohT_done, 2)
                act.sem_inc(sig_done)
                with act.Fori(0, rounds * NT) as gi:
                    for w in range(W + PRE_LAG):
                        if w < W:
                            act.wait_ge(pre_ps, gi * W + w + 1)
                            act.wait_ge(ohT_ps, gi * W + w + 1)
                            act.activation(g.ohT[0:TN, w % 2, :], g.ps[0:TN, 2 + w % 2, 0:P], ACT.Copy
                                           ).then_inc(ohT_done, 1)
                        if w >= PRE_LAG:
                            u = w - PRE_LAG
                            act.wait_ge(msg_done, gi * W + old(u, 4) + CR)
                            act.wait_ge(pre_done, gi * W + u + 3)
                            act.activation(g.sig[:, u % 4, :], g.pre[:, u % 4, :], ACT.Sigmoid).then_inc(sig_done, 1)


TU = 5


def table_phase(nc, g, sem, feats, rhs, bias, M, dest, cpart=False, general=True):
    tile_copied, row_ps, rows_done, row_out = sem("tile_copied"), sem("row_ps"), sem("rows_done"), [
        sem(f"row_out{u}") for u in range(TU)]
    sp_turn = sem("sp_turn")
    MD = M - D if cpart else M
    with nc.Block() as block:
        @block.vector
        def _(dve):
            with on_path(g, dve, "general" if general else "both"):
                dve.sem_inc(rows_done, TU + 1)
                with dve.Fori(0, NT // TU) as i:
                    for u in range(TU):
                        dve.wait_ge(row_ps, i * TU + u + 1)
                        dve.tensor_scalar(g.lt[:, u, :], feats[:, bass.ds(i * TU * TN + u * TN, TN)], 1.0, None,
                                          ALU.mult).then_inc(tile_copied, 1)
                    for u in range(TU):
                        dve.wait_ge(row_ps, i * TU + u + 1 + TU)
                        dve.wait_ge(row_out[u], i * 16 + 1)
                        if cpart:
                            dve.tensor_tensor(g.C[0:TN, bass.ds(i * TU * D + u * D, D)], g.ps[0:TN, u, MD:M],
                                              bias[0:TN, MD:M], ALU.add)
                        dve.tensor_tensor(g.rowbuf[0:TN, u, 0:MD], g.ps[0:TN, u, 0:MD], bias[0:TN, 0:MD],
                                          ALU.add).then_inc(rows_done, 1)

        @block.tensor
        def _(pe):
            with on_path(g, pe, "general" if general else "both"):
                pe.sem_inc(row_ps, TU)
                with pe.Fori(0, NT // TU) as i:
                    for u in range(TU):
                        pe.wait_ge(rows_done, i * TU + u + 2)
                        pe.wait_ge(tile_copied, i * TU + u + 1)
                        pe.matmul(g.ps[0:TN, u, 0:M], g.lt[:, u, :], rhs, start=True, stop=True).then_inc(row_ps, 1)

        @block.sync
        def _(sp):
            with on_path(g, sp, "general" if general else "both"):
                for u in range(TU):
                    sp.sem_inc(row_out[u])
                with sp.Fori(0, NT // TU) as i:
                    for u in range(TU):
                        sp.wait_ge(rows_done, i * TU + u + 2 + TU)
                        sp.sem_inc(sp_turn)
                        sp.dma_start(dest(bass.ds(i * TU * TN + u * TN, TN)), g.rowbuf[0:TN, u, 0:MD]
                                     ).then_inc(row_out[u], 16)
                for u in range(TU):
                    sp.wait_ge(row_out[u], NT // TU * 16 + 1)


def cols(t, c):
    return t[:, c * CH:(c + 1) * CH]


def bank(g, b):
    return g.ps[:, b, 0:CH]


class Norm:

    def __init__(self, g, sem):
        self.g = g
        (self.ready, self.mean_ps, self.centred, self.squared, self.var_ps, self.root_done, self.recip_done,
         self.x_done) = (sem(s) for s in ("ln_ready", "ln_mean_ps", "ln_centred", "ln_squared", "ln_var_ps",
                                          "ln_root", "ln_recip", "ln_x"))

    def tensor(self, pe):
        g = self.g
        for c in range(NCH):
            pe.wait_ge(self.ready, c + 1)
            pe.matmul(bank(g, c), g.onesd[:, :], cols(g.S3, c), start=True, stop=True).then_inc(self.mean_ps, 1)
        for c in range(NCH):
            pe.wait_ge(self.squared, c + 1)
            pe.matmul(bank(g, c), g.onesd[:, :], cols(g.S2, c), start=True, stop=True).then_inc(self.var_ps, 1)

    def vector(self, dve):
        g = self.g
        for c in range(NCH):
            dve.wait_ge(self.mean_ps, c + 1)
            dve.tensor_tensor(cols(g.S3, c), cols(g.S3, c), bank(g, c), ALU.subtract).then_inc(self.centred, 1)
        for c in range(NCH):
            dve.wait_ge(self.root_done, c + 1)
            dve.reciprocal(cols(g.S1, c), cols(g.S1, c)).then_inc(self.recip_done, 1)
            if c:
                dve.wait_ge(self.recip_done, c)
                dve.tensor_tensor(cols(g.X, c - 1), cols(g.S3, c - 1), cols(g.S1, c - 1), ALU.mult
                                  ).then_inc(self.x_done, 1)
        dve.wait_ge(self.recip_done, NCH)
        dve.tensor_tensor(cols(g.X, NCH - 1), cols(g.S3, NCH - 1), cols(g.S1, NCH - 1), ALU.mult
                          ).then_inc(self.x_done, 1)

    def scalar(self, act):
        g = self.g
        for c in range(NCH):
            act.wait_ge(self.centred, c + 1)
            act.activation(cols(g.S2, c), cols(g.S3, c), ACT.Square).then_inc(self.squared, 1)
        for c in range(NCH):
            act.wait_ge(self.var_ps, c + 1)
            act.activation(cols(g.S1, c), bank(g, c), ACT.Sqrt, bias=g.epst[:, 0:1]).then_inc(self.root_done, 1)


def first_node_phase(nc, g, sem):
    y_ps, h_done = sem("y_ps"), sem("h_done")
    norm = Norm(g, sem)
    with nc.Block() as block:
        @block.tensor
        def _(pe):
            for c in range(NCH):
                pe.matmul(bank(g, c), g.wt("w0"), cols(g.acc, c), start=True, stop=True).then_inc(y_ps, 1)
            norm.tensor(pe)

        @block.vector
        def _(dve):
            for c in range(NCH):
                dve.wait_ge(y_ps, c + 1)
                dve.scalar_tensor_tensor(out=cols(g.S3, c), in0=cols(g.X, c), scalar=2.0, in1=bank(g, c),
                                         op0=ALU.mult, op1=ALU.add).then_inc(norm.ready, 1)
            norm.vector(dve)

        @block.scalar
        def _(act):
            norm.scalar(act)
            for c in range(NCH):
                act.wait_ge(norm.x_done, c + 1)
                act.activation(cols(g.H, c), cols(g.X, c), ACT.Copy).then_inc(h_done, 1)


def gru_phase(nc, g, sem):
    bias_done, gates_ps, r_done, z_done, rn_done, pre_done, n_done, diff_done, prod_done, h_done = (
        sem(s) for s in ("gru_bias", "gates_ps", "r_done", "z_done", "rn_done", "npre_done", "n_done", "diff_done",
                         "prod_done", "h_done"))
    with nc.Block() as block:
        @block.tensor
        def _(pe):
            for c in range(NCH):
                b = 4 * (c % 2)
                if c >= 2:
                    pe.wait_ge(z_done, c - 1)
                    pe.wait_ge(pre_done, c - 1)
                for k, (wi, wh) in enumerate((("ih_r", "hh_r"), ("ih_z", "hh_z"))):
                    pe.matmul(bank(g, b + k), g.wt(wi), cols(g.acc, c), start=True, stop=False)
                    pe.matmul(bank(g, b + k), g.wt(wh), cols(g.H, c), start=False, stop=True)
                pe.matmul(bank(g, b + 2), g.wt("ih_n"), cols(g.acc, c), start=True, stop=True)
                pe.matmul(bank(g, b + 3), g.wt("hh_n"), cols(g.H, c), start=True, stop=True).then_inc(gates_ps, 1)

        @block.scalar
        def _(act):
            act.wait_ge(bias_done, 2)
            for c in range(NCH + 1):
                if c < NCH:
                    b = 4 * (c % 2)
                    act.wait_ge(gates_ps, c + 1)
                    act.activation(cols(g.S1, c), bank(g, b), ACT.Sigmoid, bias=g.bsum[:, 0:1]).then_inc(r_done, 1)
                    act.activation(cols(g.S2, c), bank(g, b + 1), ACT.Sigmoid, bias=g.bsum[:, 1:2]).then_inc(z_done, 1)
                if c:
                    act.wait_ge(pre_done, c)
                    act.activation(cols(g.S3, c - 1), cols(g.S3, c - 1), ACT.Tanh).then_inc(n_done, 1)

        @block.vector
        def _(dve):
            dve.tensor_tensor(g.bsum[:, 0:1], g.bt("bih_r"), g.bt("bhh_r"), ALU.add).then_inc(bias_done, 1)
            dve.tensor_tensor(g.bsum[:, 1:2], g.bt("bih_z"), g.bt("bhh_z"), ALU.add).then_inc(bias_done, 1)
            for c in range(NCH + 1):
                if c < NCH:
                    b = 4 * (c % 2)
                    dve.wait_ge(r_done, c + 1)
                    dve.scalar_tensor_tensor(out=cols(g.S1, c), in0=bank(g, b + 3), scalar=g.bt("bhh_n"),
                                             in1=cols(g.S1, c), op0=ALU.add, op1=ALU.mult).then_inc(rn_done, 1)
                    dve.wait_ge(rn_done, c + 1)
                    dve.scalar_tensor_tensor(out=cols(g.S3, c), in0=bank(g, b + 2), scalar=g.bt("bih_n"),
                                             in1=cols(g.S1, c), op0=ALU.add, op1=ALU.add).then_inc(pre_done, 1)
                if c:
                    p = c - 1
                    dve.wait_ge(n_done, c)
                    dve.tensor_tensor(cols(g.S1, p), cols(g.H, p), cols(g.S3, p), ALU.subtract).then_inc(diff_done, 1)
                    dve.wait_ge(diff_done, c)
                    dve.wait_ge(z_done, c)
                    dve.tensor_tensor(cols(g.S2, p), cols(g.S2, p), cols(g.S1, p), ALU.mult).then_inc(prod_done, 1)
                    dve.wait_ge(prod_done, c)
                    dve.tensor_tensor(cols(g.H, p), cols(g.S3, p), cols(g.S2, p), ALU.add).then_inc(h_done, 1)


def gate_phase(nc, g, sem):
    out_ps, gate_done, prod_done = sem("out_ps"), sem("gate_done"), sem("prod_done")
    norm = Norm(g, sem)
    with nc.Block() as block:
        @block.tensor
        def _(pe):
            for c in range(NCH):
                b = 2 * (c % 4)
                if c >= 4:
                    pe.wait_ge(prod_done, c - 3)
                pe.matmul(bank(g, b), g.wt("iw_h"), cols(g.H, c), start=True, stop=False)
                pe.matmul(bank(g, b), g.wt("iw_f"), cols(g.X, c), start=False, stop=True)
                pe.matmul(bank(g, b + 1), g.wt("jw"), cols(g.H, c), start=True, stop=True).then_inc(out_ps, 1)
            pe.wait_ge(prod_done, NCH)
            norm.tensor(pe)

        @block.scalar
        def _(act):
            for c in range(NCH):
                act.wait_ge(out_ps, c + 1)
                act.activation(cols(g.S1, c), bank(g, 2 * (c % 4)), ACT.Sigmoid, bias=g.bt("ib")).then_inc(gate_done, 1)
            norm.scalar(act)

        @block.vector
        def _(dve):
            for c in range(NCH):
                dve.wait_ge(gate_done, c + 1)
                dve.scalar_tensor_tensor(out=cols(g.S2, c), in0=bank(g, 2 * (c % 4) + 1), scalar=g.bt("jb"),
                                         in1=cols(g.S1, c), op0=ALU.add, op1=ALU.mult).then_inc(prod_done, 1)
                dve.wait_ge(prod_done, c + 1)
                dve.tensor_tensor(cols(g.S3, c), cols(g.X, c), cols(g.S2, c), ALU.add).then_inc(norm.ready, 1)
            norm.vector(dve)


def gin_phase(nc, g, sem, first):
    deg_max, deg_done, mean_done, in_done, a_ps, a_done, b_ps, b_done = (
        sem(s) for s in ("deg_max", "deg_done", "mean_done", "in_done", "a_ps", "a_done", "b_ps", "b_done"))
    norm = None if first else Norm(g, sem)
    wa, wb, ba, bb = ("w1a", "w1b", "b1a", "b1b") if first else ("w2a", "w2b", "b2a", "b2b")
    f = g.X if first else g.H
    with nc.Block() as block:
        @block.tensor
        def _(pe):
            for c in range(NCH):
                pe.wait_ge(in_done, c + 1)
                pe.matmul(bank(g, c), g.wt(wa), cols(g.S1, c), start=True, stop=True).then_inc(a_ps, 1)
            for c in range(NCH):
                pe.wait_ge(a_done, c + 1)
                pe.matmul(bank(g, c), g.wt(wb), cols(g.S2, c), start=True, stop=True).then_inc(b_ps, 1)
            if not first:
                norm.tensor(pe)

        @block.scalar
        def _(act):
            for c in range(NCH):
                act.wait_ge(a_ps, c + 1)
                act.activation(cols(g.S2, c), bank(g, c), ACT.Identity, bias=g.bt(ba)).then_inc(a_done, 1)
            for c in range(NCH):
                act.wait_ge(b_ps, c + 1)
                act.activation(cols(g.H, c), bank(g, c), ACT.Relu, bias=g.bt(bb)).then_inc(b_done, 1)
            if not first:
                norm.scalar(act)

        @block.vector
        def _(dve):
            if first:
                for c in range(NCH):
                    dve.tensor_scalar(cols(g.rdeg, c), cols(g.rdeg, c), 1.0, None, ALU.max).then_inc(deg_max, 1)
                for c in range(NCH):
                    dve.wait_ge(deg_max, c + 1)
                    dve.reciprocal(cols(g.rdeg, c), cols(g.rdeg, c)).then_inc(deg_done, 1)
            for c in range(NCH):
                if first:
                    dve.wait_ge(deg_done, c + 1)
                dve.tensor_tensor(cols(g.S1, c), cols(g.acc, c), cols(g.rdeg, c), ALU.mult).then_inc(mean_done, 1)
                dve.wait_ge(mean_done, c + 1)
                dve.tensor_tensor(cols(g.S1, c), cols(g.S1, c), cols(f, c), ALU.add).then_inc(in_done, 1)
            if not first:
                for c in range(NCH):
                    dve.wait_ge(b_done, c + 1)
                    dve.tensor_tensor(cols(g.S3, c), cols(g.X, c), cols(g.H, c), ALU.add).then_inc(norm.ready, 1)
                norm.vector(dve)


def last_node_phase(nc, g, sem):
    res_ps, sum_done, relu_done, stored = sem("res_ps"), sem("sum_done"), sem("relu_done"), sem("stored")
    norm = Norm(g, sem)
    with nc.Block() as block:
        @block.tensor
        def _(pe):
            for c in range(NCH):
                pe.matmul(bank(g, c), g.wt("wres"), cols(g.X, c), start=True, stop=True).then_inc(res_ps, 1)
            norm.tensor(pe)

        @block.scalar
        def _(act):
            for c in range(NCH):
                act.wait_ge(sum_done, c + 1)
                act.activation(cols(g.S2, c), cols(g.S1, c), ACT.Relu, bias=g.bt("bres")).then_inc(relu_done, 1)
            norm.scalar(act)

        @block.vector
        def _(dve):
            for c in range(NCH):
                dve.wait_ge(res_ps, c + 1)
                dve.tensor_tensor(cols(g.S1, c), cols(g.acc, c), bank(g, c), ALU.add).then_inc(sum_done, 1)
            for c in range(NCH):
                dve.wait_ge(relu_done, c + 1)
                dve.tensor_tensor(cols(g.S3, c), cols(g.X, c), cols(g.S2, c), ALU.add).then_inc(norm.ready, 1)
            norm.vector(dve)

        @block.sync
        def _(sp):
            sp.wait_ge(norm.x_done, NCH)
            sp.dma_start(g.out, g.X[:, :]).then_inc(stored, 16)
            sp.wait_ge(stored, 16)


def build(nc, d, out):
    g = Shared()
    with ExitStack() as ctx:
        def sb(name, shape, dt=F32):
            return ctx.enter_context(nc.sbuf_tensor(name, shape, dt))

        g.x, g.src, g.dst, g.ety = d["x"], d["src"], d["dst"], d["etype"]
        g.ewt = d["eweight"]
        g.src_pt, g.dst_pt, g.ewt_pt = d["src_pt"], d["dst_pt"], d["eweight_pt"]
        g.d_attrT, g.d_w, g.d_b, g.d_brow, g.d_xT, g.out = d["attrT"], d["w"], d["b"], d["brow"], d["xT"], out
        t_types = nc.dram_tensor("t_types", (K * N, D), F32, kind="Internal").ap()
        t_feats = nc.dram_tensor("t_feats", (N, D), F32, kind="Internal").ap()
        t_gated = nc.dram_tensor("t_gated", (N, 2 * D), F32, kind="Internal").ap()

        g.X, g.H, g.acc, g.rdeg = sb("X", [P, NP]), sb("H", [P, NP]), sb("acc", [P, NP]), sb("rdeg", [P, NP])
        g.S1, g.S2, g.S3 = sb("S1", [P, NP]), sb("S2", [P, NP]), sb("S3", [P, NP])
        g.w, g.b, g.brow = sb("w", [P, len(WNAMES) * D]), sb("b", [P, len(BNAMES)]), sb("brow", [P, len(RNAMES) * D])
        g.wt = lambda n: g.w[:, WNAMES.index(n) * D:(WNAMES.index(n) + 1) * D]
        g.bt = lambda n: g.b[:, BNAMES.index(n):BNAMES.index(n) + 1]
        g.bsum, g.epst = sb("bsum", [P, 2]), sb("epst", [P, 1])
        g.ident, g.ones, g.onesd = sb("ident", [P, P]), sb("ones", [P, P]), sb("onesd", [P, P])
        g.iota1, g.eidx = sb("iota1", [P, TN]), sb("eidx", [P, W])
        shape = [P, RMAXN + 1, NT]
        g.wstart, g.wfirst, g.wnode = sb("wstart", shape, I32), sb("wfirst", shape), sb("wnode", shape)
        g.rounds = sb("rounds", [P, 1], I32)
        g.rawi, g.meta, g.mask, g.tmpw = sb("rawi", [P, P], I32), sb("meta", [P, P]), sb("mask", [P, W]), sb("tmpw", [P, W])
        g.dcol, g.gidx = sb("dcol", [P, 2 * W]), sb("gidx", [P, 2 * W], I32)
        g.gnow = sb("gnow", [P, W], I32)
        g.rows, g.oh, g.ohT = sb("rows", [P, RING, 2 * D]), sb("oh", [P, RING, TN]), sb("ohT", [P, 2, P])
        g.attr, g.C = sb("attr", [P, 2, RING * P]), sb("C", [P, NT * D])
        g.pre, g.sig, g.msg = sb("pre", [P, 4, D]), sb("sig", [P, 4, D]), sb("msg", [P, 4, D])
        g.lt = sb("lt", [P, TU, TN])
        g.rowbuf = g.rows[:, 0:2 * TU, :].rearrange("p (u h) d -> p u (h d)", h=2)
        g.dblk = sb("dblk", [P, BR * BC], I32)
        g.ov = g.S1[:, 0:NT * BR].rearrange("p (a b) -> p a b", b=BR)
        g.c2 = g.S2[:, 0:NT * BR].rearrange("p (a b) -> p a b", b=BR)
        g.c3 = g.S3[:, 0:(RMAXN + 1) * NT].rearrange("p (a b) -> p a b", b=NT)
        g.blk, g.bmin, g.bmax = sb("blk", [P, BR]), sb("bmin", [P, BR]), sb("bmax", [P, BR])
        g.dtlo, g.rnd = sb("dtlo", [P, NT]), sb("rnd", [P, RMAXN + 1])
        g.part, g.red, g.lo, g.span = sb("part", [P, 2 * NT]), sb("red", [P, 2 * NT]), sb("lo", [P, NT]), sb("span", [P, 1])
        g.raww, g.wi = sb("raww", [P, P]), sb("wi", [P, NB_S], I32)
        g.wk, g.wk2 = sb("wk", [P, 17 * W]), sb("wk2", [P, 2 * NB_S])
        g.diff, g.before, g.nbefore = sb("diff", [P, P]), sb("before", [P, P]), sb("nbefore", [P, P])
        g.iotaf, g.iotah, g.ones16 = sb("iotaf", [P, P]), sb("iotah", [P, 512], F16), sb("ones16", [P, P], F16)
        g.flags, g.path = sb("flags", [P, 7]), sb("path", [P, 3], I32)
        n = NT * NB_S
        g.t_src, g.t_code = g.C[:, 0:n], g.C[:, n:2 * n]
        g.t_dst, g.t_w = g.attr[:, 1, 0:n], g.attr[:, 0, 900:900 + n]
        g.parts = [t[:, 0:NT * D // 2] for t in (g.S1, g.S2, g.S3)]
        g.ps = ctx.enter_context(nc.psum_tensor("ps", [P, 8, 512], F32))
        g.rows_in = [ctx.enter_context(nc.semaphore(f"rows_in{i}")) for i in range(RING)]
        sem = Sems(nc, ctx)
        setup_phase(nc, g, sem)
        sem.clear()
        sort_phase(nc, g, sem)
        sem.clear()
        scatter_phase(nc, g, sem)
        sem.clear()
        dense_weighted_phase(nc, g, sem)
        sem.clear()
        first_node_phase(nc, g, sem)
        sem.clear()
        types = t_types.rearrange("(k n) f -> n k f", k=K)
        for step in range(3):
            table_phase(nc, g, sem, g.H, g.w[:, D:(1 + K) * D], g.brow, K * D, lambda n: types[n, :, :])
            sem.clear()
            edge_phase(nc, g, sem, "L1", t_types, D, step, deg=(step == 0))
            sem.clear()
            split_phase(nc, g, sem, g.H, F16, 2)
            sem.clear()
            dense_typed_phase(nc, g, sem, first=(step == 0))
            sem.clear()
            gru_phase(nc, g, sem)
            sem.clear()
        gate_phase(nc, g, sem)
        sem.clear()
        zero_row = g.brow[:, K * D:(K + 1) * D]
        for first in (True, False):
            table_phase(nc, g, sem, g.X if first else g.H, g.ident[:, :], zero_row, D, lambda n: t_feats[n, :])
            sem.clear()
            edge_phase(nc, g, sem, "L2", t_feats, D, 3 if first else 4)
            sem.clear()
            split_phase(nc, g, sem, g.X if first else g.H, BF16, 3)
            sem.clear()
            dense_plain_phase(nc, g, sem)
            sem.clear()
            gin_phase(nc, g, sem, first)
            sem.clear()
        w0 = WNAMES.index("wb") * D
        table_phase(nc, g, sem, g.X, g.w[:, w0:w0 + 3 * D], g.brow[:, K * D:(K + 3) * D], 3 * D,
                    lambda n: t_gated[n, :], cpart=True, general=False)
        sem.clear()
        edge_phase(nc, g, sem, "L3", t_gated, 2 * D, 5)
        sem.clear()
        last_node_phase(nc, g, sem)


def kernel(**inputs):
    import concourse.bacc as bacc
    from concourse.bass_utils import run_bass_kernel_spmd

    a = {k: np.asarray(v) for k, v in inputs.items()}
    wih, whh, wet, iw = a["L1_gnn_W_ih"], a["L1_gnn_W_hh"], a["L1_gnn_W_et"], a["L1_gnn_i_w"]
    blocks = [a["L0_gnn_social_weight"]] + [wet[k].T for k in range(K)]
    blocks += [wih[i * D:(i + 1) * D].T for i in range(3)] + [whh[i * D:(i + 1) * D].T for i in range(3)]
    blocks += [iw[:, :D].T, iw[:, D:].T, a["L1_gnn_j_w"].T]
    blocks += [a[f"L2_gnn_W{n}"].T for n in ("1a", "1b", "2a", "2b")]
    blocks += [a[f"L3_gnn_W{n}"] for n in ("B", "A", "C", "E", "res")]
    columns = [a["L1_gnn_b_ih"].reshape(3, D), a["L1_gnn_b_hh"].reshape(3, D), a["L1_gnn_i_b"][None],
               a["L1_gnn_j_b"][None]] + [a[f"L2_gnn_b{n}"][None] for n in ("1a", "1b", "2a", "2b")]
    columns += [a["L3_gnn_bres"][None]]
    rows = [a["L1_gnn_b_et"].reshape(-1), np.zeros(D, np.float32)] + [a[f"L3_gnn_b{n}"] for n in ("A", "B", "C", "E")]
    pad = lambda v: np.pad(v, (0, ET * P - E)).reshape(P, ET)
    xT = np.zeros((D, NP), np.float32)
    xT[:, :N] = a["x"].T
    arrays = {
        "x": a["x"], "xT": xT, "src": a["src"], "dst": a["dst"], "etype": a["edge_type_4"], "eweight": a["edge_weight"],
        "src_pt": pad(a["src"]), "dst_pt": pad(a["dst"]), "eweight_pt": pad(a["edge_weight"]),
        "attrT": np.ascontiguousarray(a["edge_attr_128"].T), "w": np.concatenate(blocks, axis=1),
        "b": np.ascontiguousarray(np.concatenate(columns, axis=0).T), "brow": np.concatenate(rows)[None],
    }
    nc = bacc.Bacc("TRN2", target_bir_lowering=False, num_devices=1)
    d = {k: nc.dram_tensor("in_" + k, v.shape, mybir.dt.from_np(v.dtype), kind="ExternalInput").ap()
         for k, v in arrays.items()}
    out = nc.dram_tensor("out_x", (D, NP), F32, kind="ExternalOutput").ap()
    build(nc, d, out)
    r = run_bass_kernel_spmd(nc, [{"in_" + k: v for k, v in arrays.items()}], core_ids=[0])
    return np.ascontiguousarray(r.results[0]["out_x"][:, :N].T)
```

```python
from contextlib import ExitStack

import numpy as np
import concourse.bass as bass
from concourse import mybir

F32 = mybir.dt.float32
I32 = mybir.dt.int32
BF16 = mybir.dt.bfloat16
F16 = mybir.dt.float16
ALU = mybir.AluOpType
ACT = mybir.ActivationFunctionType
AX = mybir.AxisListType
RMAX = bass.bass_isa.ReduceOp.max

N, D, E, K = 3125, 128, 103125, 4
P = 128
TN = 125
NT = N // TN
W = 34
WIN = W * P
RMAXN = -(-E // WIN)
NTAB = (RMAXN + 1) * NT
RING = W // 2
NCH = 8
CH = 392
NP = NCH * CH
BR, BC = 33, 25
BIG = float(E + 1)
EPS = 1e-5
PRE_LAG, MUL_LAG, S_LAG = 2, 3, 5

WNAMES = ["w0"] + [f"wet{k}" for k in range(K)] + ["ih_r", "ih_z", "ih_n", "hh_r", "hh_z", "hh_n", "iw_h", "iw_f", "jw",
          "w1a", "w1b", "w2a", "w2b", "wb", "wa", "wc", "we", "wres"]
BNAMES = ["bih_r", "bih_z", "bih_n", "bhh_r", "bhh_z", "bhh_n", "ib", "jb", "b1a", "b1b", "b2a", "b2b", "bres"]
RNAMES = [f"bet{k}" for k in range(K)] + ["zero", "ba", "bb", "bc", "be"]


class Shared:
    pass


class Sems:

    def __init__(self, nc, ctx):
        self.nc, self.ctx, self.by_name = nc, ctx, {}

    def __call__(self, name):
        if name not in self.by_name:
            self.by_name[name] = self.ctx.enter_context(self.nc.semaphore(name))
        return self.by_name[name]

    def clear(self):
        nums = [s.num for s in self.by_name.values()]
        self.nc.sync.sem_clear(range(min(nums), max(nums) + 1))
        self.nc.all_engine_barrier()


def setup_phase(nc, g, sem):
    loaded, blocks_in = sem("loaded"), sem("blocks_in")
    made, chain, reduced = sem("made"), sem("chain"), sem("reduced")
    n_iota = 6
    with nc.Block() as block:
        @block.sync
        def _(sp):
            sp.dma_start(g.dblk[0:TN, :], g.dst.rearrange("(p f) -> p f", p=TN)).then_inc(blocks_in, 16)
            sp.dma_start(g.w[:, :], g.d_w).then_inc(loaded, 16)
            sp.dma_start(g.b[:, :], g.d_b).then_inc(loaded, 16)
            sp.dma_start(g.brow[:, :], g.d_brow.broadcast_to((P, len(RNAMES) * D))).then_inc(loaded, 16)
            sp.dma_start(g.X[:, :], g.d_xT).then_inc(loaded, 16)
            sp.wait_ge(loaded, 64)

        @block.gpsimd
        def _(pool):
            io = dict(allow_small_or_imprecise_dtypes=True)
            pool.iota(g.iota1[:, :], [[1, TN]], base=1, channel_multiplier=0, **io).then_inc(made, 1)
            pool.iota(g.eidx[:, :], [[P, W]], base=0, channel_multiplier=1, **io).then_inc(made, 1)
            pool.iota(g.ident[:, :], [[1, P]], base=0, channel_multiplier=-1, **io).then_inc(made, 1)
            pool.iota(g.blk[:, :], [[BC, BR]], base=0, channel_multiplier=BR * BC, **io).then_inc(made, 1)
            pool.iota(g.dtlo[:, :], [[TN, NT]], base=0, channel_multiplier=0, **io).then_inc(made, 1)
            pool.iota(g.rnd[:, :], [[WIN, RMAXN + 1]], base=0, channel_multiplier=0, **io).then_inc(made, 1)
            pool.wait_ge(reduced, 1)
            pool.partition_all_reduce(g.red[:, :], g.part[:, :], P, RMAX).then_inc(reduced, 1)

        @block.vector
        def _(dve):
            n = [0]

            def link(ins):
                n[0] += 1
                ins.then_inc(chain, 1)
                dve.wait_ge(chain, n[0])

            dve.memset(g.onesd[:, :], 1.0 / D)
            dve.memset(g.ones[:, :], 1.0)
            dve.memset(g.ones16[:, :], 1.0)
            dve.memset(g.epst[:, :], EPS)
            dve.memset(g.rdeg[:, :], 0.0)
            link(dve.memset(g.part[:, :], 0.0))
            dve.wait_ge(loaded, 64)
            bsum = g.brow[:, (K + 2) * D:(K + 3) * D]
            link(dve.tensor_tensor(bsum, bsum, g.brow[:, (K + 3) * D:(K + 4) * D], ALU.add))
            link(dve.tensor_tensor(bsum, bsum, g.brow[:, (K + 4) * D:(K + 5) * D], ALU.add))
            dve.wait_ge(made, n_iota)
            link(dve.tensor_scalar(g.ident[:, :], g.ident[:, :], 0.0, None, ALU.is_equal))
            dve.wait_ge(blocks_in, 16)
            dv = g.dblk[0:TN, :].rearrange("p (a b) -> p a b", b=BC)
            dve.tensor_reduce(g.bmax[0:TN, :], dv, AX.X, ALU.max)
            link(dve.tensor_reduce(g.bmin[0:TN, :], dv, AX.X, ALU.min))
            shape = [TN, NT, BR]
            lo = g.dtlo[0:TN, :].unsqueeze(2).broadcast_to(shape)
            bmin = g.bmin[0:TN, :].unsqueeze(1).broadcast_to(shape)
            bmax = g.bmax[0:TN, :].unsqueeze(1).broadcast_to(shape)
            blk = g.blk[0:TN, :].unsqueeze(1).broadcast_to(shape)
            ov, c2 = g.ov[0:TN, :, :], g.c2[0:TN, :, :]
            link(dve.tensor_scalar(g.bmin[0:TN, :], g.bmin[0:TN, :], float(TN - 1), None, ALU.subtract))
            link(dve.tensor_tensor(ov, bmin, lo, ALU.is_le))
            link(dve.tensor_tensor(c2, bmax, lo, ALU.is_ge))
            link(dve.tensor_tensor(ov, ov, c2, ALU.mult))
            link(dve.tensor_tensor(c2, ov, blk, ALU.mult))
            link(dve.scalar_tensor_tensor(out=ov, in0=ov, scalar=BIG, in1=c2, op0=ALU.mult, op1=ALU.subtract))
            link(dve.tensor_reduce(g.part[0:TN, 0:NT], ov, AX.X, ALU.max))
            link(dve.tensor_scalar(ov, ov, 0.0, float(BC), ALU.is_gt, ALU.mult))
            link(dve.tensor_tensor(c2, c2, ov, ALU.add))
            dve.tensor_reduce(g.part[0:TN, NT:2 * NT], c2, AX.X, ALU.max).then_inc(reduced, 1)
            dve.wait_ge(reduced, 2)
            neg, hi = g.red[:, 0:NT], g.red[:, NT:2 * NT]
            link(dve.tensor_scalar(g.lo[:, :], neg, -1.0, BIG, ALU.mult, ALU.add))
            link(dve.tensor_tensor(hi, hi, g.lo[:, :], ALU.subtract))
            link(dve.tensor_reduce(g.span[:, :], hi, AX.X, ALU.max))
            link(dve.tensor_scalar(g.span[:, :], g.span[:, :], 0.5, 1.0 / WIN, ALU.subtract, ALU.mult))
            link(dve.tensor_scalar(g.span[:, :], g.span[:, :], 0.5, 1.0, ALU.add, ALU.max))
            link(dve.tensor_copy(g.rounds[:, :], g.span[:, :]))
            sh = [P, RMAXN + 1, NT]
            link(dve.tensor_tensor(g.wfirst[:, :, :], g.lo[:, :].unsqueeze(1).broadcast_to(sh),
                                   g.rnd[:, :].unsqueeze(2).broadcast_to(sh), ALU.add))
            link(dve.tensor_scalar(g.c3[:, :, :], g.wfirst[:, :, :], float(E - WIN), None, ALU.min))
            link(dve.tensor_tensor(g.wfirst[:, :, :], g.wfirst[:, :, :], g.c3[:, :, :], ALU.subtract))
            link(dve.tensor_copy(g.wstart[:, :, :], g.c3[:, :, :]))
            link(dve.tensor_scalar(g.c3[:, 0, :], g.dtlo[:, :], -1.0, 1.0, ALU.mult, ALU.add))
            link(dve.tensor_copy(g.wnode[:, :, :], g.c3[:, 0, :].unsqueeze(1).broadcast_to(sh)))


NB_S = 2 * NT + 1
OHR = 17
assert NB_S % OHR == 0


def sort_phase(nc, g, sem):
    made, raw_in, conv_done, metaT_done, chain, unpack_chain, ends_done, offs_ps, lo_done, perm_ps, unpacked, reduced = (
        sem(s) for s in ("made", "raw_in", "conv_done", "metaT_done", "chain", "unpack_chain", "ends_done", "offs_ps", "lo_done",
                         "perm_ps", "unpacked", "reduced"))
    sp_turn = sem("sp_turn")
    wstart = g.wstart[:, :, :].rearrange("p a b -> p (a b)")
    wfirst, wnode = g.wfirst[:, 0, :], g.wnode[:, 0, :]
    oh = g.S1[:, 0:NT * W // 2].bitcast(BF16).rearrange("p (b w) -> p b w", w=W)
    pos = g.S2[:, 0:NT * W + 1]
    val = g.S3[:, 0:NT * W].rearrange("p (b w) -> p b w", w=W)
    ohlo = [t.rearrange("p (u f) -> p u f", u=RING) for t in (g.S1[:, 512:512 + RING * P], g.acc[:, 0:RING * P])]
    rhs = [t[:, 900:900 + RING * 2 * NB_S].rearrange("p (u f) -> p u f", u=RING) for t in (g.S2, g.S3)]
    names = ["mask", "dc", "valid", "code", "stile", "sloc", "packed", "weight", "bucket", "rank", "q", "low", "own",
             "slot", "third", "over", "overmax"]
    f = {n: g.wk[:, i * W:(i + 1) * W] for i, n in enumerate(names)}
    with nc.Block() as block:
        @block.sync
        def _(sp):
            with sp.Fori(0, NT + 1) as gi:
                at = sp.value_load(wstart[0:1, bass.ds(gi, 1)], min_val=0, max_val=E - WIN)
                sp.wait_ge(conv_done, gi + 1)
                sp.sem_inc(sp_turn)
                sp.wait_ge(metaT_done, gi + 1)
                sp.sem_inc(sp_turn)
                for i, t in enumerate((g.dst, g.src, g.ety)):
                    sp.dma_start(g.rawi[i * W:(i + 1) * W, :],
                                 t[bass.ds(at, WIN)].rearrange("(w p) -> w p", p=P)).then_inc(raw_in, 16)
                sp.dma_start(g.raww[0:W, :], g.ewt[bass.ds(at, WIN)].rearrange("(w p) -> w p", p=P)).then_inc(raw_in, 16)

        @block.gpsimd
        def _(pool):
            io = dict(allow_small_or_imprecise_dtypes=True)
            pool.iota(g.diff[:, :], [[1, P]], base=0, channel_multiplier=-1, **io).then_inc(made, 1)
            pool.iota(g.iotaf[:, :], [[1, P]], base=1, channel_multiplier=0, **io).then_inc(made, 1)
            pool.iota(g.iotah[:, :], [[1, 512]], base=1, channel_multiplier=0, **io).then_inc(made, 1)
            pool.wait_ge(reduced, 1)
            pool.partition_all_reduce(g.flags[:, 1:2], g.flags[:, 0:1], P, RMAX).then_inc(reduced, 1)

        @block.tensor
        def _(pe):
            pe.sem_inc(metaT_done)
            pe.wait_ge(made, 8)

            def transpose_meta(gi):
                pe.wait_ge(raw_in, (gi + 1) * 64)
                pe.wait_ge(conv_done, gi + 2)
                pe.transpose(g.ps[:, 5, 0:3 * W], g.raww[0:3 * W, :], g.ident[0:3 * W, 0:3 * W])
                pe.transpose(g.ps[:, 6, 0:3 * W], g.meta[0:3 * W, :], g.ident[0:3 * W, 0:3 * W]).then_inc(metaT_done, 1)

            transpose_meta(0)
            with pe.Fori(0, NT) as gi:
                pe.wait_ge(ends_done, gi + 1)
                pe.matmul(g.ps[:, 7, 0:NT], g.before[:, :], pos[:, W:NT * W + 1:W], start=True, stop=False)
                pe.matmul(g.ps[:, 7, 0:NT], g.nbefore[:, :], pos[:, 0:NT * W:W], start=False, stop=True).then_inc(offs_ps, 1)
                transpose_meta(gi + 1)
                for w in range(W):
                    if w == 0:
                        pe.wait_ge(unpacked, gi + 1)
                    pe.wait_ge(lo_done, gi * 2 + w // RING + 1)
                    pe.matmul(g.ps[:, 0, 0:2 * NB_S], ohlo[w // RING][:, w % RING, :], rhs[w // RING][:, w % RING, :],
                              start=(w == 0), stop=(w == W - 1)).then_inc(perm_ps, 1)

        @block.vector
        def _(dve):
            links, unpack_links = 22, 7
            n = [0]

            def link0(ins):
                n[0] += 1
                ins.then_inc(reduced, 1)
                dve.wait_ge(reduced, n[0])

            dve.sem_inc(unpacked)
            dve.wait_ge(made, 3)
            dve.tensor_scalar(g.before[:, :], g.diff[:, :], 0.0, None, ALU.is_gt).then_inc(made, 1)
            dve.tensor_scalar(g.nbefore[:, :], g.diff[:, :], 0.0, -1.0, ALU.is_ge, ALU.mult).then_inc(made, 1)
            dve.memset(g.raww[:, :], 0.0).then_inc(made, 1)
            dve.memset(pos[:, 0:1], 0.0).then_inc(made, 1)
            dve.memset(f["overmax"], 0.0).then_inc(made, 1)
            dve.wait_ge(made, 8)
            dve.sem_inc(conv_done)

            def convert(gi):
                dve.wait_ge(raw_in, (gi + 1) * 64)
                dve.tensor_copy(g.meta[0:3 * W, :], g.rawi[0:3 * W, :]).then_inc(conv_done, 1)

            def unpack(gi):
                made_n = [0]

                def link(ins):
                    made_n[0] += 1
                    ins.then_inc(unpack_chain, 1)
                    dve.wait_ge(unpack_chain, gi * unpack_links + made_n[0])

                dve.wait_ge(perm_ps, gi * W + W)
                pk, at = g.ps[:, 0, 0:NB_S], bass.ds(gi * NB_S, NB_S)
                wi, t1, t2 = g.wi[:, 0:NB_S], g.wk2[:, 0:NB_S], g.wk2[:, NB_S:2 * NB_S]
                dve.tensor_scalar(g.t_w[:, at], g.ps[:, 0, NB_S:2 * NB_S], 1.0, None, ALU.mult)
                link(dve.tensor_scalar(wi, pk, 255.5, 1.0 / 512, ALU.subtract, ALU.mult))
                link(dve.tensor_copy(t1, wi))
                link(dve.tensor_scalar(g.t_src[:, at], t1, 1.0, None, ALU.mult))
                link(dve.scalar_tensor_tensor(out=t2, in0=t1, scalar=-512.0, in1=pk, op0=ALU.mult, op1=ALU.add))
                dve.tensor_scalar(g.t_code[:, at], t2, 1.0, None, ALU.mult)
                dve.sem_inc(unpacked)
                link(dve.tensor_scalar(wi, t2, 63.0, 1.0 / TN, ALU.subtract, ALU.mult))
                link(dve.tensor_copy(t1, wi))
                link(dve.scalar_tensor_tensor(out=g.t_dst[:, at], in0=t1, scalar=-float(TN), in1=t2,
                                              op0=ALU.mult, op1=ALU.add))
                assert made_n[0] == unpack_links

            def body(gi, finish):
                made_n = [0]

                def link(ins):
                    made_n[0] += 1
                    ins.then_inc(chain, 1)
                    dve.wait_ge(chain, gi * links + made_n[0])

                link(dve.tensor_scalar(f["mask"], g.eidx[:, :], wfirst[:, bass.ds(gi, 1)], None, ALU.is_ge))
                dve.wait_ge(metaT_done, gi + 2)
                m = g.ps[:, 6, :]
                m_dst, m_src, m_type = m[:, 0:W], m[:, W:2 * W], m[:, 2 * W:3 * W]
                link(dve.scalar_tensor_tensor(out=f["dc"], in0=m_dst, scalar=wnode[:, bass.ds(gi, 1)], in1=f["mask"],
                                              op0=ALU.add, op1=ALU.mult))
                dve.tensor_copy(f["weight"], g.ps[:, 5, 0:W])
                dve.tensor_scalar(g.wi[:, 0:W], m_src, float(TN // 2), 1.0 / TN, ALU.subtract, ALU.mult)
                dve.scalar_tensor_tensor(out=f["code"], in0=m_type, scalar=float(TN), in1=f["dc"], op0=ALU.mult, op1=ALU.add)
                link(dve.tensor_scalar(f["valid"], f["dc"], 1.0, None, ALU.is_ge))
                link(dve.scalar_tensor_tensor(out=f["valid"], in0=f["dc"], scalar=float(TN), in1=f["valid"],
                                              op0=ALU.is_le, op1=ALU.mult))
                link(dve.tensor_copy(f["stile"], g.wi[:, 0:W]))
                dve.scalar_tensor_tensor(out=f["bucket"], in0=f["stile"], scalar=1.0, in1=f["valid"], op0=ALU.add, op1=ALU.mult)
                link(dve.scalar_tensor_tensor(out=f["sloc"], in0=f["stile"], scalar=-float(TN), in1=m_src,
                                              op0=ALU.mult, op1=ALU.add))
                link(dve.scalar_tensor_tensor(out=f["packed"], in0=f["sloc"], scalar=512.0, in1=f["code"],
                                              op0=ALU.mult, op1=ALU.add))
                link(dve.tensor_scalar(f["packed"], f["packed"], 512.0, None, ALU.add))
                sh = [P, NT, W]
                link(dve.tensor_tensor(oh, f["bucket"].unsqueeze(1).broadcast_to(sh),
                                       g.iotaf[:, 0:NT].unsqueeze(2).broadcast_to(sh), ALU.is_equal))
                ohf = g.S1[:, 0:NT * W // 2].bitcast(BF16)
                link(dve.tensor_tensor_scan(pos[:, 1:NT * W + 1], ohf, ohf, 0.0, ALU.add, ALU.max))
                dve.sem_inc(ends_done)
                if finish:
                    unpack(gi - 1)
                dve.wait_ge(offs_ps, gi + 1)
                posv = pos[:, 1:NT * W + 1].rearrange("p (b w) -> p b w", w=W)
                link(dve.tensor_tensor(val, posv, g.ps[:, 7, 0:NT].unsqueeze(2).broadcast_to(sh), ALU.add))
                link(dve.tensor_tensor(val, val, oh, ALU.mult))
                link(dve.tensor_reduce(f["rank"], val.rearrange("p b w -> p w b"), AX.X, ALU.add))
                link(dve.tensor_scalar(g.wi[:, 0:W], f["rank"], 64.5, 1.0 / P, ALU.subtract, ALU.mult))
                link(dve.tensor_copy(f["q"], g.wi[:, 0:W]))
                dve.scalar_tensor_tensor(out=f["low"], in0=f["q"], scalar=-float(P), in1=f["rank"], op0=ALU.mult, op1=ALU.add)
                dve.tensor_scalar(f["own"], f["bucket"], g.iotaf[:, bass.ds(gi, 1)], None, ALU.is_equal)
                link(dve.scalar_tensor_tensor(out=f["slot"], in0=f["stile"], scalar=2.0, in1=f["q"], op0=ALU.mult, op1=ALU.add))
                dve.scalar_tensor_tensor(out=f["third"], in0=f["q"], scalar=2.0, in1=f["own"], op0=ALU.is_ge, op1=ALU.mult)
                dve.tensor_tensor(f["over"], f["q"], f["own"], ALU.subtract)
                link(dve.scalar_tensor_tensor(out=f["slot"], in0=f["slot"], scalar=1.0, in1=f["valid"], op0=ALU.add, op1=ALU.mult))
                link(dve.tensor_tensor(f["overmax"], f["overmax"], f["over"], ALU.max))
                link(dve.scalar_tensor_tensor(out=f["over"], in0=f["slot"], scalar=float(NB_S), in1=f["third"],
                                              op0=ALU.subtract, op1=ALU.mult))
                link(dve.tensor_tensor(f["slot"], f["slot"], f["over"], ALU.subtract))
                convert(gi + 1)
                for half in range(2):
                    def edges(what, n):
                        return f[what][:, half * RING:(half + 1) * RING].unsqueeze(2).broadcast_to([P, RING, n])

                    packed, weight = rhs[half][:, :, 0:NB_S], rhs[half][:, :, NB_S:2 * NB_S]
                    link(dve.tensor_tensor(packed, edges("slot", NB_S),
                                           g.iotaf[:, 0:NB_S].unsqueeze(1).broadcast_to([P, RING, NB_S]), ALU.is_equal))
                    dve.tensor_tensor(ohlo[half], edges("low", P), g.iotaf[:, :].unsqueeze(1).broadcast_to([P, RING, P]),
                                      ALU.is_equal)
                    dve.tensor_tensor(weight, packed, edges("weight", NB_S), ALU.mult)
                    dve.tensor_tensor(packed, packed, edges("packed", NB_S), ALU.mult).then_inc(lo_done, 1)
                assert made_n[0] == links, made_n

            convert(0)
            over_windows(dve, body, lambda: unpack(NT - 1))
            link0(dve.tensor_reduce(g.flags[:, 0:1], f["overmax"], AX.X, ALU.max))
            dve.wait_ge(reduced, 2)
            n[0] += 1
            link0(dve.tensor_copy(g.flags[:, 2:3], g.rounds[:, :]))
            link0(dve.tensor_scalar(g.flags[:, 3:4], g.flags[:, 1:2], 1.5, None, ALU.is_ge))
            link0(dve.scalar_tensor_tensor(out=g.flags[:, 4:5], in0=g.flags[:, 2:3], scalar=1.5, in1=g.flags[:, 3:4],
                                           op0=ALU.is_ge, op1=ALU.max))
            link0(dve.tensor_scalar(g.flags[:, 5:6], g.flags[:, 4:5], -1.0, 1.0, ALU.mult, ALU.add))
            link0(dve.tensor_tensor(g.flags[:, 6:7], g.flags[:, 4:5], g.flags[:, 2:3], ALU.mult))
            link0(dve.tensor_copy(g.path[:, :], g.flags[:, 4:7]))


def on_path(g, eng, path):
    if path == "both":
        return ExitStack()
    at = 1 if path == "dense" else 0
    return eng.If(eng.value_load(g.path[0:1, at:at + 1], min_val=0, max_val=1))


def group_of(b):
    return b // 4, b % 4


NBL = NT + 1
NGR = -(-NBL // 4)
RGR = 4


def before_reuse(gr):
    if gr >= RGR:
        return gr - RGR + 1
    last = max(x for x in range(NGR) if x % RGR == gr)
    return last + 1 - NGR


def window_tables(dve, g, dt, finish, tables, made, copied):
    if finish:
        dve.wait_ge(made, dt * NB_S)
    cur = [g.cur[:, i * NB_S:(i + 1) * NB_S] for i in range(len(tables))]
    for c, t in zip(cur, tables):
        dve.tensor_scalar(c, t[:, bass.ds(dt * NB_S, NB_S)], 1.0, None, ALU.mult).then_inc(copied, 1)
    dve.wait_ge(copied, dt * len(tables) + len(tables))
    return cur


def over_windows(eng, body, last):
    body(0, False)
    with eng.Fori(1, NT) as dt:
        body(dt, True)
    last()


def dense_weighted_phase(nc, g, sem):
    made, slots_used, mat_done, y_ps, added, x_in, x_copied, sp_turn, copied, y_out, turn = (
        sem(s) for s in ("made", "slots_used", "mat_done", "y_ps", "added", "x_in", "x_copied", "sp_turn",
                         "copied", "y_out", "turn"))
    MC, YC, OC, AC = 4, 3, 3, 3
    ohd = g.S1[:, 0:OHR * P].rearrange("p (u f) -> p u f", u=OHR)
    ohs = g.oh
    mat = g.S2[:, 0:4 * 512].rearrange("p (u f) -> p u f", u=RGR)
    xnext, xcur = g.S3[0:TN, 0:P], g.S3[0:TN, P:2 * P]
    ys = g.S3[:, 2 * P:2 * P + RGR * 512].rearrange("p (u f) -> p u f", u=RGR)
    cols_of = lambda gr: 4 * TN if gr < NGR - 1 else 2 * TN
    with nc.Block() as block:
        @block.sync
        def _(sp):
            with on_path(g, sp, "dense"):
                sp.sem_inc(x_copied)
                with sp.Fori(0, NT) as dt:
                    sp.wait_ge(x_copied, dt + 1)
                    sp.sem_inc(sp_turn)
                    sp.dma_start(xnext, g.x[bass.ds(dt * TN, TN), :]).then_inc(x_in, 16)

        @block.vector
        def _(dve):
            with on_path(g, dve, "dense"):
                dve.memset(g.acc[:, :], 0.0).then_inc(added, 1)
                dve.wait_ge(added, 1)
                dve.sem_inc(added, AC - 1)

                def body(dt, finish):
                    src, dst, weight = window_tables(dve, g, dt, finish, (g.t_src, g.t_dst, g.t_w), made, copied)
                    for t in range(NB_S):
                        u = t % OHR
                        if t % 3 == 0:
                            dve.wait_ge(slots_used, dt * NB_S + t + 3)
                        dve.tensor_scalar(ohd[:, u, 0:TN], g.iotaf[:, 0:TN], dst[:, t:t + 1], None, ALU.is_equal)
                        dve.tensor_scalar(ohs[:, u, 0:TN], g.iotaf[:, 0:TN], src[:, t:t + 1], weight[:, t:t + 1],
                                          ALU.is_equal, ALU.mult).then_inc(made, 1)

                over_windows(dve, body, lambda: None)

        @block.gpsimd
        def _(pool):
            with on_path(g, pool, "dense"):
                def add(dt, n, to, what):
                    pool.wait_ge(added, dt * (NGR + 1) + n + AC)
                    pool.sem_inc(turn)
                    pool.tensor_tensor(to, to, what, ALU.add).then_inc(added, 1)

                with pool.Fori(0, NT) as dt:
                    for gr in range(NGR):
                        pool.wait_ge(y_out, dt * NGR + gr + 1 + OC)
                        pool.sem_inc(turn)
                        y = ys[:, gr % RGR, :]
                        if gr < NGR - 1:
                            add(dt, gr, g.acc[:, gr * 4 * TN:(gr + 1) * 4 * TN], y[:, 0:4 * TN])
                        else:
                            add(dt, gr, g.acc[:, (NT - 1) * TN:NT * TN], y[:, 0:TN])
                            add(dt, gr + 1, g.acc[:, bass.ds(dt * TN, TN)], y[:, TN:2 * TN])

        @block.tensor
        def _(pe):
            with on_path(g, pe, "dense"):
                pe.sem_inc(slots_used, OHR)

                def times_x(dt, gr):
                    if gr == 0:
                        pe.wait_ge(x_copied, dt + 2)
                    pe.wait_ge(mat_done, dt * NGR + gr + 1 + MC)
                    pe.wait_ge(y_out, dt * NGR + before_reuse(gr) + OC)
                    n = cols_of(gr)
                    pe.matmul(g.ps[:, 4 + gr % RGR, 0:n], xcur, mat[0:TN, gr % RGR, 0:n], start=True, stop=True
                              ).then_inc(y_ps, 1)

                def body(dt, finish):
                    for b in range(NBL):
                        gr, c = b // 4, b % 4
                        if c == 0:
                            pe.wait_ge(mat_done, dt * NGR + before_reuse(gr) + MC)
                        ts = range(2 * b, min(2 * b + 2, NB_S))
                        pe.wait_ge(made, dt * NB_S + ts[-1] + 1)
                        for t in ts:
                            pe.matmul(g.ps[0:TN, gr % RGR, c * TN:(c + 1) * TN], ohd[:, t % OHR, 0:TN],
                                      ohs[:, t % OHR, 0:TN], start=(t == ts[0]), stop=(t == ts[-1])
                                      ).then_inc(slots_used, 1)
                        if c == 1 and gr:
                            times_x(dt, gr - 1)
                        elif c == 1 and finish:
                            times_x(dt - 1, NGR - 1)

                over_windows(pe, body, lambda: times_x(NT - 1, NGR - 1))

        @block.scalar
        def _(act):
            with on_path(g, act, "dense"):
                act.sem_inc(mat_done, MC)
                act.sem_inc(y_ps, YC)
                act.sem_inc(y_out, OC)

                def copy_sums(dt, gr):
                    n = cols_of(gr)
                    act.wait_ge(y_ps, dt * NGR + gr + 1 + YC)
                    act.wait_ge(added, dt * (NGR + 1) + (gr if gr >= RGR else (1, 1, 3, 3)[gr]))
                    act.activation(ys[:, gr % RGR, 0:n], g.ps[:, 4 + gr % RGR, 0:n], ACT.Copy).then_inc(y_out, 1)

                def body(dt, finish):
                    for gr in range(NGR):
                        n = cols_of(gr)
                        act.wait_ge(slots_used, dt * NB_S + min(8 * gr + 8, NB_S) + OHR)
                        act.wait_ge(y_ps, dt * NGR + before_reuse(gr) + YC)
                        act.activation(mat[0:TN, gr % RGR, 0:n], g.ps[0:TN, gr % RGR, 0:n], ACT.Copy
                                       ).then_inc(mat_done, 1)
                        if gr == 0:
                            act.wait_ge(y_ps, dt * NGR + YC)
                            act.wait_ge(x_in, dt * 16 + 16)
                            act.activation(xcur, xnext, ACT.Copy).then_inc(x_copied, 1)
                            if finish:
                                copy_sums(dt - 1, NGR - 1)
                        else:
                            copy_sums(dt, gr - 1)

                over_windows(act, body, lambda: copy_sums(NT - 1, NGR - 1))


def part_tile(part, b):
    return part[0:TN, b * D:(b + 1) * D]


def split_phase(nc, g, sem, feats, dt16, n):
    tile_ps, hi_done, rest_done, mid_done, low_done = (sem(s) for s in ("tile_ps", "hi_done", "rest_done", "mid_done",
                                                                     "low_done"))
    parts = [p.bitcast(dt16) for p in g.parts]
    rest = g.S1[:, 1600:1600 + 4 * P].rearrange("p (u f) -> p u f", u=4)
    with nc.Block() as block:
        @block.tensor
        def _(pe):
            with on_path(g, pe, "dense"):
                for b in range(NT):
                    if b >= 4:
                        pe.wait_ge(low_done, b - 3)
                    pe.transpose(g.ps[0:TN, b % 4, 0:P], feats[:, b * TN:(b + 1) * TN], g.ident[:, :]).then_inc(tile_ps, 1)

        @block.scalar
        def _(act):
            with on_path(g, act, "dense"):
                for b in range(NT):
                    act.wait_ge(tile_ps, b + 1)
                    act.activation(part_tile(parts[0], b), g.ps[0:TN, b % 4, 0:P], ACT.Copy).then_inc(hi_done, 1)

        @block.vector
        def _(dve):
            with on_path(g, dve, "dense"):
                for b in range(NT):
                    dve.wait_ge(hi_done, b + 1)
                    ps = g.ps[0:TN, b % 4, 0:P]
                    if n == 2:
                        dve.tensor_tensor(part_tile(parts[1], b), ps, part_tile(parts[0], b), ALU.subtract
                                          ).then_inc(low_done, 1)
                        continue
                    r = rest[0:TN, b % 4, :]
                    if b >= 4:
                        dve.wait_ge(low_done, b - 3)
                    dve.tensor_tensor(r, ps, part_tile(parts[0], b), ALU.subtract).then_inc(rest_done, 1)
                    dve.wait_ge(rest_done, b + 1)
                    dve.tensor_copy(part_tile(parts[1], b), r).then_inc(mid_done, 1)
                    dve.wait_ge(mid_done, b + 1)
                    dve.tensor_tensor(part_tile(parts[2], b), r, part_tile(parts[1], b), ALU.subtract).then_inc(low_done, 1)


def dense_typed_phase(nc, g, sem):
    made, slots_used, mat_done, agg_done, sums_out, a_ps, chain, copied = (
        sem(s) for s in ("made", "slots_used", "mat_done", "agg_done", "sums_out", "a_ps", "chain", "copied"))
    KT = K * TN
    LAG = 2
    SUMS_AT, FINAL_AT, ACC_AT = 6, 8, 30
    GR = 5
    parts = [p.bitcast(F16) for p in g.parts]
    ohk = [g.S3[:, i * 256:(i + 1) * 256] for i in range(12)] + [g.S1[:, 1600 + i * 256:1856 + i * 256] for i in range(5)]
    ohk = [t.bitcast(F16) for t in ohk]
    stored, sp_turn = [sem(f"stored{j}") for j in range(GR)], sem("sp_turn")
    ohs = g.oh[:, :, :].rearrange("p u f -> p (u f)")[:, 0:OHR * 64].bitcast(F16).rearrange("p (u f) -> p u f", u=OHR)
    sums, deg, degt = (t[:, :, :].rearrange("p u f -> p (u f)") for t in (g.msg, g.sig, g.pre))
    sums, deg, degt = sums[:, 0:KT], deg[:, 0:KT], degt[:, 0:TN]
    bias = g.rows[:, :, :].rearrange("p u f -> p (u f)")
    pairs = [g.S2[:, 1600 + j * KT:1600 + (j + 1) * KT] for j in range(3)] + [
        bias[:, NT * TN + j * KT:NT * TN + (j + 1) * KT] for j in range(2)]
    pairs = [t.bitcast(F16) for t in pairs]
    NPR = NBL // 2
    half_sums = [g.C[:, 2 * NT * NB_S + j * 250:2 * NT * NB_S + (j + 1) * 250].bitcast(F16) for j in range(2)] + [
        g.lt[:, :, :].rearrange("p u f -> p (u f)")[:, 0:250].bitcast(F16)]
    part_pairs = (0, 7, NPR)
    totals = [g.attr[:, 0, 0:7 * TN].bitcast(BF16), g.attr[:, 1, NT * NB_S:NT * NB_S + 6 * TN].bitcast(BF16)]
    half_done, summed, turn, t_stored = sem("half_done"), sem("summed"), sem("turn"), [sem("t_stored0"), sem("t_stored1")]
    SC = 3
    mat = lambda b: pairs[b // 2 % GR][0:TN, b % 2 * KT:(b % 2 + 1) * KT]

    def reuse(dt, b, ring):
        return dt * NBL + (b - ring + 3 if b >= ring else min(b + 1, 2))

    def stores(j):
        return len(range(j, NBL // 2, GR))

    with nc.Block() as block:
        @block.sync
        def _(sp):
            with on_path(g, sp, "dense"):
                with sp.Fori(0, NT) as dt:
                    for b in range(0, NBL, 2):
                        sp.wait_ge(mat_done, dt * NBL + b + 4)
                        sp.sem_inc(sp_turn)
                        j = b // 2 % GR
                        sp.dma_start(g.t_tmats[bass.ds(dt * TN, TN), b * KT:(b + 2) * KT], pairs[j][0:TN, :]
                                     ).then_inc(stored[j], 16)
                        if b // 2 in (10, NPR - 1):
                            i = 0 if b // 2 == 10 else 1
                            sp.wait_ge(summed, dt * NPR + part_pairs[i + 1] + SC)
                            sp.sem_inc(sp_turn)
                            x, y = part_pairs[i] * 2 * TN, part_pairs[i + 1] * 2 * TN
                            sp.dma_start(g.t_mats[bass.ds(dt * TN, TN), x:y], totals[i][0:TN, 0:y - x]
                                         ).then_inc(t_stored[i], 16)
                for j in range(GR):
                    sp.wait_ge(stored[j], NT * 16 * stores(j) + 1)
                for i in range(2):
                    sp.wait_ge(t_stored[i], NT * 16 + 1)

        @block.gpsimd
        def _(pool):
            with on_path(g, pool, "dense"):
                with pool.Fori(0, NT) as dt:
                    for q in range(NPR):
                        i = 0 if q < part_pairs[1] else 1
                        if q == part_pairs[i]:
                            pool.wait_ge(t_stored[i], dt * 16 + 1)
                            pool.sem_inc(turn)
                        pool.wait_ge(mat_done, dt * NBL + 2 * q + 4)
                        pool.sem_inc(turn)
                        m = pairs[q % GR][0:TN, :].rearrange("p (b f) -> p b f", b=2)
                        h = half_sums[q % 2 if q < NPR - 1 else 2][0:TN, :].rearrange("p (b f) -> p b f", b=2)
                        t = totals[i][0:TN, (q - part_pairs[i]) * 2 * TN:(q - part_pairs[i] + 1) * 2 * TN]
                        pool.tensor_tensor(h, m[:, :, 0:2 * TN], m[:, :, 2 * TN:4 * TN], ALU.add).then_inc(half_done, 1)
                        pool.wait_ge(half_done, dt * NPR + q + 1)
                        pool.sem_inc(turn)
                        pool.tensor_tensor(t.rearrange("p (b f) -> p b f", b=2), h[:, :, 0:TN], h[:, :, TN:2 * TN],
                                           ALU.add).then_inc(summed, 1)

        @block.vector
        def _(dve):
            with on_path(g, dve, "dense"):
                dve.sem_inc(sums_out, 2)

                def take_sums(dt):
                    dve.wait_ge(agg_done, dt * NBL + NBL + 2)
                    dve.tensor_scalar(deg, g.ps[:, 4, 0:KT], 1.0, None, ALU.mult)
                    dve.tensor_scalar(sums, g.ps[:, 3, 0:KT], 1.0, None, ALU.mult).then_inc(sums_out, 1)
                    dve.wait_ge(sums_out, dt + 3)
                    dve.tensor_reduce(degt, deg.rearrange("p (k n) -> p n k", k=K), AX.X, ALU.add).then_inc(chain, 1)
                    dve.wait_ge(chain, dt * 2 + 1)
                    dve.tensor_scalar(g.rdeg[:, bass.ds(dt * TN, TN)], degt, 1.0, None, ALU.mult)

                def finish_sums(dt):
                    at = bass.ds(dt * TN, TN)
                    dve.wait_ge(a_ps, dt + 1)
                    dve.tensor_scalar(bias[:, at], g.ps[:, 6, 0:TN], 1.0, None, ALU.mult).then_inc(chain, 1)
                    dve.wait_ge(chain, dt * 2 + 2)
                    dve.tensor_tensor(g.acc[:, at], g.ps[:, 5, 0:TN], bias[:, at], ALU.add)

                def body(dt, finish):
                    src, code = window_tables(dve, g, dt, finish, (g.t_src, g.t_code), made, copied)
                    for t in range(NB_S):
                        if finish and t == SUMS_AT:
                            take_sums(dt - 1)
                        if finish and t == ACC_AT:
                            finish_sums(dt - 1)
                        u = t % OHR
                        if t % 3 == 0:
                            dve.wait_ge(slots_used, dt * NB_S + t + 3)
                        dve.tensor_scalar(ohs[:, u, 0:TN], g.iotah[:, 0:TN], src[:, t:t + 1], None, ALU.is_equal)
                        dve.tensor_scalar(ohk[u][:, 0:KT], g.iotah[:, 0:KT], code[:, t:t + 1], None, ALU.is_equal
                                          ).then_inc(made, 1)

                def last():
                    take_sums(NT - 1)
                    finish_sums(NT - 1)

                over_windows(dve, body, last)

        @block.tensor
        def _(pe):
            with on_path(g, pe, "dense"):
                pe.sem_inc(slots_used, OHR)

                def aggregate(dt, b):
                    if b == 0:
                        pe.wait_ge(sums_out, dt + 2)
                    pe.wait_ge(mat_done, dt * NBL + b + 3)
                    m = mat(b)
                    for i, p in enumerate(parts[0:2]):
                        rows = part_tile(p, b) if b < NT else p[0:TN, bass.ds(dt * D, D)]
                        mm = pe.matmul(g.ps[:, 3, 0:KT], rows, m, start=(b == 0 and i == 0), stop=(b == NBL - 1 and i == 1))
                    mm = pe.matmul(g.ps[:, 4, 0:KT], g.ones16[0:TN, :], m, start=(b == 0), stop=(b == NBL - 1))
                    mm.then_inc(agg_done, 1)

                def types(dt):
                    pe.wait_ge(sums_out, dt + 3)
                    for k in range(K):
                        pe.matmul(g.ps[:, 6, 0:TN], g.brow[0:1, k * D:(k + 1) * D], deg[0:1, k * TN:(k + 1) * TN],
                                  start=(k == 0), stop=(k == K - 1))
                    for k in range(K):
                        mm = pe.matmul(g.ps[:, 5, 0:TN], g.wt(f"wet{k}"), sums[:, k * TN:(k + 1) * TN],
                                       start=(k == 0), stop=(k == K - 1))
                    mm.then_inc(a_ps, 1)

                def body(dt, finish):
                    for b in range(NBL):
                        pe.wait_ge(mat_done, reuse(dt, b, 3))
                        ts = range(2 * b, min(2 * b + 2, NB_S))
                        pe.wait_ge(made, dt * NB_S + ts[-1] + 1)
                        for t in ts:
                            pe.matmul(g.ps[0:TN, b % 3, 0:KT], ohs[:, t % OHR, 0:TN], ohk[t % OHR][:, 0:KT],
                                      start=(t == ts[0]), stop=(t == ts[-1])).then_inc(slots_used, 1)
                        if b >= LAG:
                            aggregate(dt, b - LAG)
                        elif finish:
                            aggregate(dt - 1, NBL + b - LAG)
                        if finish and b == FINAL_AT:
                            types(dt - 1)

                def last():
                    for b in range(NBL - LAG, NBL):
                        aggregate(NT - 1, b)
                    types(NT - 1)

                over_windows(pe, body, last)

        @block.scalar
        def _(act):
            with on_path(g, act, "dense"):
                act.sem_inc(mat_done, 2)
                act.sem_inc(agg_done, 2)
                act.sem_inc(summed, SC)
                act.sem_inc(t_stored[0])
                act.sem_inc(t_stored[1])
                for j in range(GR):
                    act.sem_inc(stored[j])
                with act.Fori(0, NT) as dt:
                    for b in range(NBL):
                        act.wait_ge(slots_used, dt * NB_S + min(2 * b + 2, NB_S) + OHR)
                        act.wait_ge(agg_done, reuse(dt, b, 2 * GR))
                        j = b // 2 % GR
                        if b % 2 == 0:
                            act.wait_ge(summed, dt * NPR + ((1, 2, 3, 1, 1)[j] if b < 2 * GR else b // 2 - GR + 1 + SC))
                        act.wait_ge(stored[j], dt * (16 * stores(j)) + b // 2 // GR * 16 + 1)
                        act.activation(mat(b), g.ps[0:TN, b % 3, 0:KT], ACT.Copy).then_inc(mat_done, 1)


def dense_typed_stored_phase(nc, g, sem):
    KT = K * TN
    TYPES_AT = 8
    mats_in = [sem(f"mats_in{j}") for j in range(7)]
    agg_done, sums_out, a_ps, a_taken, sp_turn = (
        sem(s) for s in ("agg_done", "sums_out", "a_ps", "a_taken", "sp_turn"))
    parts = [p.bitcast(F16) for p in g.parts]
    bias = g.rows[:, :, :].rearrange("p u f -> p (u f)")
    sums = g.msg[:, :, :].rearrange("p u f -> p (u f)")[:, 0:KT]
    ps = g.ps[:, :, :].rearrange("p b f -> p (b f)")
    h = KT // 2
    pieces = [g.S3[:, 0:4 * h], g.S3[:, 4 * h:8 * h], g.S3[:, 8 * h:12 * h], g.S1[:, 1600:1600 + 4 * h],
              g.S1[:, 1600 + 4 * h:1600 + 6 * h], g.S2[:, 1600:1600 + 4 * h],
              g.oh[:, :, :].rearrange("p u f -> p (u f)")[:, 0:4 * h]]
    pieces = [t.bitcast(F16) for t in pieces]
    first_block = [0, 4, 8, 12, 16, 18, 22, NBL]

    def bank_of(eng, dt):
        par = dt % 2 if isinstance(dt, int) else eng.snap(dt % 2)
        return ps[:, bass.ds(par * 512, KT)]

    with nc.Block() as block:
        @block.sync
        def _(sp):
            with on_path(g, sp, "dense"):
                with sp.Fori(0, NT) as dt:
                    for j, piece in enumerate(pieces):
                        a, b = first_block[j:j + 2]
                        sp.wait_ge(agg_done, dt * 7 + j + 1)
                        sp.sem_inc(sp_turn)
                        sp.dma_start(piece[0:TN, :], g.t_tmats[bass.ds(dt * TN, TN), a * KT:b * KT]
                                     ).then_inc(mats_in[j], 16)

        @block.tensor
        def _(pe):
            with on_path(g, pe, "dense"):
                pe.sem_inc(agg_done, 7)

                def types(dt):
                    pe.wait_ge(sums_out, dt + 3)
                    pe.wait_ge(a_taken, dt + 1)
                    for k in range(K):
                        mm = pe.matmul(g.ps[:, 5, 0:TN], g.wt(f"wet{k}"), sums[:, k * TN:(k + 1) * TN],
                                       start=(k == 0), stop=(k == K - 1))
                    mm.then_inc(a_ps, 1)

                def body(dt, finish):
                    pe.wait_ge(sums_out, dt + 1)
                    to = bank_of(pe, dt)
                    for j, piece in enumerate(pieces):
                        pe.wait_ge(mats_in[j], dt * 16 + 16)
                        for b in range(*first_block[j:j + 2]):
                            for k, p in enumerate(parts[0:2]):
                                rows = part_tile(p, b) if b < NT else p[0:TN, bass.ds(dt * D, D)]
                                u = b - first_block[j]
                                mm = pe.matmul(to, rows, piece[0:TN, u * KT:(u + 1) * KT],
                                               start=(b == 0 and k == 0), stop=(b == NBL - 1 and k == 1))
                            if finish and b == TYPES_AT:
                                types(dt - 1)
                        mm.then_inc(agg_done, 1)

                over_windows(pe, body, lambda: types(NT - 1))

        @block.vector
        def _(dve):
            with on_path(g, dve, "dense"):
                dve.sem_inc(sums_out, 2)
                dve.sem_inc(a_taken)
                with dve.Fori(0, NT) as dt:
                    dve.wait_ge(agg_done, dt * 7 + 14)
                    dve.tensor_scalar(sums, bank_of(dve, dt), 1.0, None, ALU.mult).then_inc(sums_out, 1)
                    dve.wait_ge(a_ps, dt + 1)
                    at = bass.ds(dt * TN, TN)
                    dve.tensor_tensor(g.acc[:, at], g.ps[:, 5, 0:TN], bias[:, at], ALU.add).then_inc(a_taken, 1)


def whole_window(words):
    return words.bitcast(BF16)


def dense_stored_phase(nc, g, sem):
    U = 5
    mats_in = [sem(f"mats_in{u}") for u in range(U)]
    agg_done, sums_out, sp_turn = sem("agg_done"), sem("sums_out"), sem("sp_turn")
    parts = [p.bitcast(BF16) for p in g.parts]
    n = NBL * TN // 2
    rows, attr = g.rows[:, :, :].rearrange("p u f -> p (u f)"), g.attr[:, :, :].rearrange("p u f -> p (u f)")
    mats = [whole_window(t) for t in (rows[:, 0:n], rows[:, n:2 * n], attr[:, 0:n], attr[:, n:2 * n], g.C[:, 0:n])]
    with nc.Block() as block:
        @block.sync
        def _(sp):
            with on_path(g, sp, "dense"):
                with sp.Fori(0, NT // U) as i:
                    for u in range(U):
                        sp.wait_ge(agg_done, i * U + u + 1)
                        sp.sem_inc(sp_turn)
                        sp.dma_start(mats[u][0:TN, :], g.t_mats[bass.ds(i * U * TN + u * TN, TN), :]
                                     ).then_inc(mats_in[u], 16)

        @block.tensor
        def _(pe):
            with on_path(g, pe, "dense"):
                pe.sem_inc(agg_done, U)
                with pe.Fori(0, NT // U) as i:
                    for u in range(U):
                        pe.wait_ge(mats_in[u], i * 16 + 16)
                        pe.wait_ge(sums_out, i * U + u + 1)
                        for b in range(NBL):
                            for k, p in enumerate(parts):
                                rows = part_tile(p, b) if b < NT else p[0:TN, bass.ds(i * U * D + u * D, D)]
                                mm = pe.matmul(g.ps[:, u, 0:TN], rows, mats[u][0:TN, b * TN:(b + 1) * TN],
                                               start=(b == 0 and k == 0), stop=(b == NBL - 1 and k == 2))
                        mm.then_inc(agg_done, 1)

        @block.vector
        def _(dve):
            with on_path(g, dve, "dense"):
                dve.sem_inc(sums_out, U)
                with dve.Fori(0, NT // U) as i:
                    for u in range(U):
                        dve.wait_ge(agg_done, i * U + u + 1 + U)
                        dve.tensor_scalar(g.acc[:, bass.ds(i * U * TN + u * TN, TN)], g.ps[:, u, 0:TN], 1.0, None,
                                          ALU.mult).then_inc(sums_out, 1)


ET = -(-E // P)
SG, SR = 26, 13
NB, BW = 7, 448
assert ET % SG == 0 and SG % SR == 0 and NB * BW == NP


def scatter_phase(nc, g, sem):
    edges_in, made, idx_now, turn, rows_used, split_done, onehot_done, tile_added, chain, taken, zeroed, zeros_added = (
        sem(s) for s in ("edges_in", "made", "idx_now", "turn", "rows_used", "split_done", "onehot_done",
                         "tile_added", "chain", "taken", "zeroed", "zeros_added"))
    src_i = g.S3[:, 0:ET].bitcast(I32)
    dst_i = g.S3[:, ET:2 * ET].bitcast(I32)
    src_f, wgt = g.S3[:, 2 * ET:3 * ET], g.H[:, 0:ET]
    nodes = g.H[:, ET:ET + NP // 2].bitcast(mybir.dt.int16)
    oh = [t[:, 0:NP // 2].bitcast(BF16) for t in (g.S1, g.S2)]
    h1, h2, h3 = (g.attr[:, 0, k * P:(k + 1) * P].bitcast(BF16).rearrange("p (u f) -> p u f", u=2) for k in range(3))
    rest = g.attr[:, 0, 3 * P:5 * P].rearrange("p (u f) -> p u f", u=2)
    zero = g.attr[:, 0, 5 * P:5 * P + BW // 2].bitcast(BF16)
    with nc.Block() as block:
        @block.sync
        def _(sp):
            with on_path(g, sp, "general"):
                sp.dma_start(dst_i, g.dst_pt).then_inc(edges_in, 16)
                sp.dma_start(src_i, g.src_pt).then_inc(edges_in, 16)
                sp.dma_start(wgt, g.ewt_pt).then_inc(edges_in, 16)

        @block.gpsimd
        def _(pool):
            with on_path(g, pool, "general"):
                pool.iota(nodes, [[1, NP]], base=0, channel_multiplier=0,
                          allow_small_or_imprecise_dtypes=True).then_inc(made, 1)
                pool.wait_ge(edges_in, 48)
                with pool.Fori(0, ET // SG) as i:
                    for h in range(SG // SR):
                        pool.wait_ge(rows_used, i * SG + h * SR + 1)
                        pool.sem_inc(turn)
                        pool.tensor_copy(g.gnow[:, h * SR:(h + 1) * SR], dst_i[:, bass.ds(i * SG + h * SR, SR)]).then_inc(idx_now, 1)
                        pool.wait_ge(idx_now, i * 2 + h + 1)
                        pool.sem_inc(turn)
                        for u in range(SR):
                            pool.wait_ge(rows_used, i * SG + h * SR + u + 2)
                            pool.sem_inc(turn)
                            pool.indirect_dma_start(g.rows[:, u, 0:D], None, g.x,
                                                    bass.IndirectOffsetOnAxis(g.gnow[:, h * SR + u:h * SR + u + 1], 0)
                                                    ).then_inc(g.rows_in[u], 16)

        @block.vector
        def _(dve):
            with on_path(g, dve, "general"):
                dve.sem_inc(rows_used, SR + 1)
                dve.memset(zero, 0.0).then_inc(zeroed, 1)
                dve.wait_ge(edges_in, 48)
                dve.tensor_copy(src_f, src_i).then_inc(chain, 1)
                dve.wait_ge(chain, 1)
                dve.wait_ge(made, 1)
                with dve.Fori(0, ET // SG) as i:
                    for u in range(SG):
                        t = i * SG + u
                        w = wgt[:, bass.ds(t, 1)]
                        b = u % 2
                        dve.wait_ge(tile_added, t + 1)
                        dve.tensor_scalar(oh[b], nodes, src_f[:, bass.ds(t, 1)], None, ALU.is_equal
                                          ).then_inc(onehot_done, 1)
                        dve.wait_ge(g.rows_in[u % SR], (i * 2 + u // SR + 1) * 16)
                        row = g.rows[:, u % SR, 0:D]
                        dve.tensor_scalar(h1[:, b, :], row, w, None, ALU.mult).then_inc(chain, 1)
                        dve.wait_ge(chain, t * 3 + 2)
                        dve.scalar_tensor_tensor(out=rest[:, b, :], in0=row, scalar=w, in1=h1[:, b, :], op0=ALU.mult,
                                                 op1=ALU.subtract).then_inc(chain, 1)
                        dve.wait_ge(chain, t * 3 + 3)
                        dve.sem_inc(rows_used)
                        dve.tensor_scalar(h2[:, b, :], rest[:, b, :], 1.0, None, ALU.mult).then_inc(chain, 1)
                        dve.wait_ge(chain, t * 3 + 4)
                        dve.tensor_tensor(h3[:, b, :], rest[:, b, :], h2[:, b, :], ALU.subtract).then_inc(split_done, 1)
                dve.wait_ge(zeros_added, 1)
                for c in range(NB):
                    dve.tensor_copy(g.acc[:, c * BW:(c + 1) * BW], g.ps[:, c, 0:BW]).then_inc(taken, 1)

        @block.tensor
        def _(pe):
            with on_path(g, pe, "general"):
                pe.sem_inc(tile_added, 2)
                pe.wait_ge(zeroed, 1)
                for c in range(NB):
                    pe.matmul(g.ps[:, c, 0:BW], zero[:, 0:P], zero, start=True, stop=False, skip_group_check=True)
                with pe.Fori(0, ET // SG) as i:
                    for u in range(SG):
                        t = i * SG + u
                        b = u % 2
                        pe.wait_ge(onehot_done, t + 1)
                        pe.wait_ge(split_done, t + 1)
                        for part in (h1, h2, h3):
                            for c in range(NB):
                                mm = pe.matmul(g.ps[:, c, 0:BW], part[:, b, :], oh[b][:, c * BW:(c + 1) * BW],
                                               start=False, stop=False, skip_group_check=True)
                        mm.then_inc(tile_added, 1)
                for c in range(NB):
                    mm = pe.matmul(g.ps[:, c, 0:BW], zero[:, 0:P], zero, start=False, stop=True, skip_group_check=True)
                mm.then_inc(zeros_added, 1)


def edge_phase(nc, g, sem, kind, table, width, before, deg=False):
    L1, L3 = kind == "L1", kind == "L3"
    raw_in, conv_done, metaT_done, idx_done = sem("raw_in"), sem("conv_done"), sem("metaT_done"), sem("idx_done")
    rows_in = g.rows_in
    attr_in = [sem(f"attr_in{i}") for i in range(2)]
    idx_now, sp_turn = sem("idx_now"), sem("sp_turn")
    turn, tile_added, onehot_done, acc_done, chain = (
        sem("turn"), sem("tile_added"), sem("onehot_done"), sem("acc_done"), sem("chain"))
    ohT_ps, ohT_done, edge_ps, pre_ps, pre_done, sig_done, msg_done = (
        sem("ohT_ps"), sem("ohT_done"), sem("edge_ps"), sem("pre_ps"), sem("pre_done"), sem("sig_done"),
        sem("msg_done"))
    CR = RING + 1
    n_meta = 3 if L1 else 2
    rows_done = msg_done if L3 else tile_added

    def old(w, ring, carry):
        if w >= ring:
            return w - ring + 1
        return max(t for t in range(W) if t % ring == w) + 1 - W if carry else 0

    def windows(eng, rounds, body, last):
        with eng.Fori(0, rounds) as r:
            if not L3:
                with eng.Fori(0, NT) as dt:
                    body(eng.snap(r * NT + dt), dt, False)
                return
            body(eng.snap(r * NT), 0, False)
            with eng.Fori(1, NT) as dt:
                body(eng.snap(r * NT + dt), dt, True)
            last(eng.snap(r * NT + NT))

    def rounds_of(eng):
        return (eng.value_load(g.rounds[0:1, 0:1], min_val=1, max_val=RMAXN),
                eng.value_load(g.path[0:1, 2:3], min_val=0, max_val=RMAXN))

    wstart = g.wstart[:, :, :].rearrange("p a b -> p (a b)")
    wfirst = g.wfirst[:, :, :].rearrange("p a b -> p (a b)")
    wnode = g.wnode[:, :, :].rearrange("p a b -> p (a b)")

    with nc.Block() as block:
        @block.sync
        def _(sp):
            with on_path(g, sp, "both" if L3 else "general"):
                rounds, _ = rounds_of(sp)

                def load_meta(gi, at):
                    def win(t):
                        return t[bass.ds(at, WIN)].rearrange("(w p) -> w p", p=P)
                    sp.wait_ge(conv_done, gi + 1)
                    sp.sem_inc(sp_turn)
                    sp.dma_start(g.rawi[0:W, :], win(g.dst)).then_inc(raw_in, 16)
                    sp.dma_start(g.rawi[W:2 * W, :], win(g.src)).then_inc(raw_in, 16)
                    if L1:
                        sp.dma_start(g.rawi[2 * W:3 * W, :], win(g.ety)).then_inc(raw_in, 16)

                with sp.Fori(0, rounds * NT) as gi:
                    at = sp.value_load(wstart[0:1, bass.ds(gi, 1)], min_val=0, max_val=E - WIN)
                    load_meta(gi, at)
                    if L3:
                        for half in range(2):
                            sp.wait_ge(edge_ps, gi * W + half * RING + 1)
                            sp.sem_inc(sp_turn)
                            sp.dma_start(g.attr[:, half, :],
                                         g.d_attrT[:, bass.ds(at + half * RING * P, RING * P)]).then_inc(attr_in[half], 16)
                last = sp.snap(rounds * NT)
                at = sp.value_load(wstart[0:1, bass.ds(last, 1)], min_val=0, max_val=E - WIN)
                load_meta(last, at)

        @block.gpsimd
        def _(pool):
            with on_path(g, pool, "both" if L3 else "general"):
                rounds, _ = rounds_of(pool)
                groups = [0, 4, 8, 12, RING, RING + 4, RING + 8, RING + 12, W]
                with pool.Fori(0, rounds * NT) as gi:
                    par = pool.snap((gi % 2) * W)
                    pool.wait_ge(idx_done, gi + 1)
                    pool.sem_inc(turn)
                    for a, b in zip(groups, groups[1:]):
                        pool.wait_ge(rows_done, gi * W + b + 1)
                        pool.sem_inc(turn)
                        if a % RING == 0:
                            half = a // RING
                            pool.tensor_copy(g.gnow[:, a:a + RING], g.gidx[:, bass.ds(par + a, RING)]).then_inc(idx_now, 1)
                            pool.wait_ge(idx_now, gi * 2 + half + 1)
                            pool.sem_inc(turn)
                        for w in range(a, b):
                            pool.indirect_dma_start(g.rows[:, w % RING, 0:width], None, table,
                                                    bass.IndirectOffsetOnAxis(g.gnow[:, w:w + 1], 0)
                                                    ).then_inc(rows_in[w % RING], 16)

        @block.tensor
        def _(pe):
            with on_path(g, pe, "both" if L3 else "general"):
                rounds, slow_rounds = rounds_of(pe)
                base = pe.snap(slow_rounds * (NT * 2 * 16 * before))
                scattered = pe.snap(pe.value_load(g.path[0:1, 0:1], min_val=0, max_val=1) * (ET // SR * 16))

                def transpose_meta(gi):
                    pe.wait_ge(conv_done, gi + 2)
                    pe.transpose(g.ps[:, 6, 0:n_meta * W], g.meta[0:n_meta * W, :],
                                 g.ident[0:n_meta * W, 0:n_meta * W]).then_inc(metaT_done, 1)

                def add_up(gi, w, rows):
                    if w == 0:
                        pe.wait_ge(acc_done, gi + 2)
                    mm = pe.matmul(g.ps[:, 0, 0:TN], rows, g.oh[:, w % RING, :], start=(w == 0), stop=(w == W - 1))
                    if deg:
                        mm = pe.matmul(g.ps[:, 1, 0:TN], g.ones[:, :], g.oh[:, w % RING, :],
                                       start=(w == 0), stop=(w == W - 1))
                    mm.then_inc(tile_added, 1)

                pe.sem_inc(metaT_done)
                pe.sem_inc(edge_ps, CR)
                pe.sem_inc(tile_added, CR)
                pe.sem_inc(pre_ps, 2)
                transpose_meta(0)

                def add_destinations(gi, dt, u):
                    pe.wait_ge(ohT_done, gi * W + u + 3)
                    pe.matmul(g.ps[:, 4 + u % 2, 0:D], g.ohT[0:TN, u % 2, :],
                              g.C[0:TN, bass.ds(dt * D, D)], start=False, stop=True).then_inc(pre_ps, 1)

                def add_messages(gi, u):
                    pe.wait_ge(msg_done, gi * W + u + 1 + CR)
                    add_up(gi, u, g.msg[:, u % 4, :])

                def body(gi, dt, carry):
                    for w in range(W):
                        if w == W // 2 - 1:
                            transpose_meta(gi + 1)
                        if not L3:
                            pe.wait_ge(onehot_done, gi * W + w + 1)
                            pe.wait_ge(rows_in[w % RING], (gi * 2 + w // RING + 1) * 16 + base + (scattered if w % RING < SR else 0))
                            add_up(gi, w, g.rows[:, w % RING, 0:D])
                            continue
                        pe.wait_ge(onehot_done, gi * W + w + 1)
                        pe.wait_ge(ohT_done, gi * W + w + 1)
                        pe.transpose(g.ps[0:TN, 2 + w % 2, 0:P], g.oh[:, w % RING, :],
                                     g.ident[:, :]).then_inc(ohT_ps, 1)
                        if w % RING == 0:
                            pe.wait_ge(attr_in[w // RING], (gi + 1) * 16)
                        pe.wait_ge(pre_done, gi * W + w + 1)
                        pe.matmul(g.ps[:, 4 + w % 2, 0:D],
                                  g.attr[:, w // RING, (w % RING) * P:(w % RING + 1) * P],
                                  g.wt("we"), start=True, stop=False).then_inc(edge_ps, 1)
                        if w >= 1:
                            add_destinations(gi, dt, w - 1)
                        elif carry:
                            add_destinations(gi - 1, dt - 1, W - 1)
                        if w >= S_LAG:
                            add_messages(gi, w - S_LAG)
                        elif carry:
                            add_messages(gi - 1, W + w - S_LAG)

                def last(end):
                    add_destinations(end - 1, NT - 1, W - 1)
                    for u in range(W - S_LAG, W):
                        add_messages(end - 1, u)

                windows(pe, rounds, body, last)

        @block.vector
        def _(dve):
            with on_path(g, dve, "both" if L3 else "general"):
                rounds, slow_rounds = rounds_of(dve)
                base = dve.snap(slow_rounds * (NT * 2 * 16 * before))
                scattered = dve.snap(dve.value_load(g.path[0:1, 0:1], min_val=0, max_val=1) * (ET // SR * 16))
                links = 4 if L1 else 3

                def prepare(gi):
                    made = [0]

                    def link(ins):
                        made[0] += 1
                        ins.then_inc(chain, 1)
                        dve.wait_ge(chain, gi * links + made[0])

                    par = dve.snap((gi % 2) * W)
                    ints = 3 * W if L1 else 2 * W
                    dve.wait_ge(raw_in, (gi + 1) * 16 * n_meta)
                    dve.tensor_copy(g.meta[0:ints, :], g.rawi[0:ints, :]).then_inc(conv_done, 1)
                    link(dve.tensor_scalar(g.mask[:, :], g.eidx[:, :], wfirst[:, bass.ds(gi, 1)], None, ALU.is_ge))
                    dve.wait_ge(metaT_done, gi + 2)
                    m = g.ps[:, 6, :]
                    link(dve.scalar_tensor_tensor(out=g.dcol[:, bass.ds(par, W)], in0=m[:, 0:W],
                                                  scalar=wnode[:, bass.ds(gi, 1)], in1=g.mask[:, :],
                                                  op0=ALU.add, op1=ALU.mult))
                    if L1:
                        link(dve.tensor_scalar(g.tmpw[:, :], m[:, 2 * W:3 * W], float(N), None, ALU.mult))
                        link(dve.tensor_tensor(g.gidx[:, bass.ds(par, W)], g.tmpw[:, :], m[:, W:2 * W], ALU.add))
                    else:
                        link(dve.tensor_scalar(g.gidx[:, bass.ds(par, W)], m[:, W:2 * W], 1.0, None, ALU.mult))
                    assert made[0] == links
                    dve.sem_inc(idx_done)

                dve.sem_inc(conv_done)
                dve.sem_inc(acc_done)
                dve.sem_inc(pre_done, 2)
                dve.sem_inc(msg_done, CR)
                dve.memset(g.acc[:, :], 0.0).then_inc(acc_done, 1)
                dve.wait_ge(acc_done, 2)
                prepare(0)

                def add_sources(gi, u, carry):
                    dve.wait_ge(pre_ps, gi * W + u + 3)
                    dve.wait_ge(rows_in[u % RING], (gi * 2 + u // RING + 1) * 16 + base + (scattered if u % RING < SR else 0))
                    dve.wait_ge(sig_done, gi * W + old(u, 4, carry) + 1)
                    dve.tensor_tensor(g.pre[:, u % 4, :], g.ps[:, 4 + u % 2, 0:D], g.rows[:, u % RING, 0:D],
                                      ALU.add).then_inc(pre_done, 1)

                def gate_sources(gi, u, carry):
                    dve.wait_ge(sig_done, gi * W + u + 2)
                    dve.wait_ge(tile_added, gi * W + old(u, 4, carry) + CR)
                    dve.tensor_tensor(g.msg[:, u % 4, :], g.sig[:, u % 4, :], g.rows[:, u % RING, D:2 * D],
                                      ALU.mult).then_inc(msg_done, 1)

                def take_sums(gi, dt):
                    dve.wait_ge(tile_added, gi * W + W + CR)
                    dve.wait_ge(acc_done, gi + 2)
                    a = g.acc[:, bass.ds(dt * TN, TN)]
                    if deg:
                        q = g.rdeg[:, bass.ds(dt * TN, TN)]
                        dve.tensor_tensor(q, q, g.ps[:, 1, 0:TN], ALU.add)
                    dve.tensor_tensor(a, a, g.ps[:, 0, 0:TN], ALU.add).then_inc(acc_done, 1)

                def body(gi, dt, carry):
                    par = dve.snap((gi % 2) * W)
                    for w in range(W):
                        if w == W // 2 - 1:
                            prepare(gi + 1)
                        dve.wait_ge(tile_added, gi * W + w + 2)
                        dc = g.dcol[:, bass.ds(par + w, 1)]
                        dve.tensor_scalar(g.oh[:, w % RING, :], g.iota1[:, :], dc, None, ALU.is_equal
                                          ).then_inc(onehot_done, 1)
                        if not L3:
                            continue
                        if w >= PRE_LAG:
                            add_sources(gi, w - PRE_LAG, carry)
                        elif carry:
                            add_sources(gi - 1, W + w - PRE_LAG, True)
                        if w >= MUL_LAG:
                            gate_sources(gi, w - MUL_LAG, carry)
                        elif carry:
                            gate_sources(gi - 1, W + w - MUL_LAG, True)
                        if carry and w == S_LAG:
                            take_sums(gi - 1, dt - 1)
                    if not L3:
                        take_sums(gi, dt)

                def last(end):
                    for w in range(W, W + MUL_LAG):
                        if w < W + PRE_LAG:
                            add_sources(end - 1, w - PRE_LAG, True)
                        gate_sources(end - 1, w - MUL_LAG, True)
                    take_sums(end - 1, NT - 1)

                windows(dve, rounds, body, last)

        @block.scalar
        def _(act):
            with on_path(g, act, "both" if L3 else "general"):
                if not L3:
                    return
                rounds, _ = rounds_of(act)
                act.sem_inc(ohT_done, 2)
                act.sem_inc(sig_done)

                def gate(gi, u, carry):
                    act.wait_ge(msg_done, gi * W + old(u, 4, carry) + CR)
                    act.wait_ge(pre_done, gi * W + u + 3)
                    act.activation(g.sig[:, u % 4, :], g.pre[:, u % 4, :], ACT.Sigmoid).then_inc(sig_done, 1)

                def body(gi, dt, carry):
                    for w in range(W):
                        act.wait_ge(pre_ps, gi * W + w + 1)
                        act.wait_ge(ohT_ps, gi * W + w + 1)
                        act.activation(g.ohT[0:TN, w % 2, :], g.ps[0:TN, 2 + w % 2, 0:P], ACT.Copy
                                       ).then_inc(ohT_done, 1)
                        if w >= PRE_LAG:
                            gate(gi, w - PRE_LAG, carry)
                        elif carry:
                            gate(gi - 1, W + w - PRE_LAG, True)

                def last(end):
                    for u in range(W - PRE_LAG, W):
                        gate(end - 1, u, True)

                windows(act, rounds, body, last)


TU = 5


def table_phase(nc, g, sem, feats, rhs, bias, M, dest, cpart=False, general=True):
    tile_copied, row_ps, rows_done, row_out = sem("tile_copied"), sem("row_ps"), sem("rows_done"), [
        sem(f"row_out{u}") for u in range(TU)]
    sp_turn = sem("sp_turn")
    MD = M - D if cpart else M
    with nc.Block() as block:
        @block.vector
        def _(dve):
            with on_path(g, dve, "general" if general else "both"):
                dve.sem_inc(rows_done, TU + 1)
                with dve.Fori(0, NT // TU) as i:
                    for u in range(TU):
                        dve.wait_ge(row_ps, i * TU + u + 1)
                        dve.tensor_scalar(g.lt[:, u, :], feats[:, bass.ds(i * TU * TN + u * TN, TN)], 1.0, None,
                                          ALU.mult).then_inc(tile_copied, 1)
                    for u in range(TU):
                        dve.wait_ge(row_ps, i * TU + u + 1 + TU)
                        dve.wait_ge(row_out[u], i * 16 + 1)
                        if cpart:
                            dve.tensor_tensor(g.C[0:TN, bass.ds(i * TU * D + u * D, D)], g.ps[0:TN, u, MD:M],
                                              bias[0:TN, MD:M], ALU.add)
                        dve.tensor_tensor(g.rowbuf[0:TN, u, 0:MD], g.ps[0:TN, u, 0:MD], bias[0:TN, 0:MD],
                                          ALU.add).then_inc(rows_done, 1)

        @block.tensor
        def _(pe):
            with on_path(g, pe, "general" if general else "both"):
                pe.sem_inc(row_ps, TU)
                with pe.Fori(0, NT // TU) as i:
                    for u in range(TU):
                        pe.wait_ge(rows_done, i * TU + u + 2)
                        pe.wait_ge(tile_copied, i * TU + u + 1)
                        pe.matmul(g.ps[0:TN, u, 0:M], g.lt[:, u, :], rhs, start=True, stop=True).then_inc(row_ps, 1)

        @block.sync
        def _(sp):
            with on_path(g, sp, "general" if general else "both"):
                for u in range(TU):
                    sp.sem_inc(row_out[u])
                with sp.Fori(0, NT // TU) as i:
                    for u in range(TU):
                        sp.wait_ge(rows_done, i * TU + u + 2 + TU)
                        sp.sem_inc(sp_turn)
                        sp.dma_start(dest(bass.ds(i * TU * TN + u * TN, TN)), g.rowbuf[0:TN, u, 0:MD]
                                     ).then_inc(row_out[u], 16)
                for u in range(TU):
                    sp.wait_ge(row_out[u], NT // TU * 16 + 1)


def cols(t, c):
    return t[:, c * CH:(c + 1) * CH]


def bank(g, b):
    return g.ps[:, b, 0:CH]


class Norm:

    def __init__(self, g, sem):
        self.g = g
        (self.ready, self.mean_ps, self.centred, self.squared, self.var_ps, self.root_done, self.recip_done,
         self.x_done) = (sem(s) for s in ("ln_ready", "ln_mean_ps", "ln_centred", "ln_squared", "ln_var_ps",
                                          "ln_root", "ln_recip", "ln_x"))

    def tensor(self, pe):
        g = self.g
        for c in range(NCH):
            pe.wait_ge(self.ready, c + 1)
            pe.matmul(bank(g, c), g.onesd[:, :], cols(g.S3, c), start=True, stop=True).then_inc(self.mean_ps, 1)
        for c in range(NCH):
            pe.wait_ge(self.squared, c + 1)
            pe.matmul(bank(g, c), g.onesd[:, :], cols(g.S2, c), start=True, stop=True).then_inc(self.var_ps, 1)

    def vector(self, dve):
        g = self.g
        for c in range(NCH):
            dve.wait_ge(self.mean_ps, c + 1)
            dve.tensor_tensor(cols(g.S3, c), cols(g.S3, c), bank(g, c), ALU.subtract).then_inc(self.centred, 1)
        for c in range(NCH):
            dve.wait_ge(self.root_done, c + 1)
            dve.reciprocal(cols(g.S1, c), cols(g.S1, c)).then_inc(self.recip_done, 1)
            if c:
                dve.wait_ge(self.recip_done, c)
                dve.tensor_tensor(cols(g.X, c - 1), cols(g.S3, c - 1), cols(g.S1, c - 1), ALU.mult
                                  ).then_inc(self.x_done, 1)
        dve.wait_ge(self.recip_done, NCH)
        dve.tensor_tensor(cols(g.X, NCH - 1), cols(g.S3, NCH - 1), cols(g.S1, NCH - 1), ALU.mult
                          ).then_inc(self.x_done, 1)

    def scalar(self, act):
        g = self.g
        for c in range(NCH):
            act.wait_ge(self.centred, c + 1)
            act.activation(cols(g.S2, c), cols(g.S3, c), ACT.Square).then_inc(self.squared, 1)
        for c in range(NCH):
            act.wait_ge(self.var_ps, c + 1)
            act.activation(cols(g.S1, c), bank(g, c), ACT.Sqrt, bias=g.epst[:, 0:1]).then_inc(self.root_done, 1)


def first_node_phase(nc, g, sem):
    y_ps, h_done = sem("y_ps"), sem("h_done")
    norm = Norm(g, sem)
    with nc.Block() as block:
        @block.tensor
        def _(pe):
            for c in range(NCH):
                pe.matmul(bank(g, c), g.wt("w0"), cols(g.acc, c), start=True, stop=True).then_inc(y_ps, 1)
            norm.tensor(pe)

        @block.vector
        def _(dve):
            for c in range(NCH):
                dve.wait_ge(y_ps, c + 1)
                dve.scalar_tensor_tensor(out=cols(g.S3, c), in0=cols(g.X, c), scalar=2.0, in1=bank(g, c),
                                         op0=ALU.mult, op1=ALU.add).then_inc(norm.ready, 1)
            norm.vector(dve)

        @block.scalar
        def _(act):
            norm.scalar(act)
            for c in range(NCH):
                act.wait_ge(norm.x_done, c + 1)
                act.activation(cols(g.H, c), cols(g.X, c), ACT.Copy).then_inc(h_done, 1)


def gru_phase(nc, g, sem):
    bias_done, gates_ps, r_done, z_done, rn_done, pre_done, n_done, diff_done, prod_done, h_done = (
        sem(s) for s in ("gru_bias", "gates_ps", "r_done", "z_done", "rn_done", "npre_done", "n_done", "diff_done",
                         "prod_done", "h_done"))
    with nc.Block() as block:
        @block.tensor
        def _(pe):
            for c in range(NCH):
                b = 4 * (c % 2)
                if c >= 2:
                    pe.wait_ge(z_done, c - 1)
                    pe.wait_ge(pre_done, c - 1)
                for k, (wi, wh) in enumerate((("ih_r", "hh_r"), ("ih_z", "hh_z"))):
                    pe.matmul(bank(g, b + k), g.wt(wi), cols(g.acc, c), start=True, stop=False)
                    pe.matmul(bank(g, b + k), g.wt(wh), cols(g.H, c), start=False, stop=True)
                pe.matmul(bank(g, b + 2), g.wt("ih_n"), cols(g.acc, c), start=True, stop=True)
                pe.matmul(bank(g, b + 3), g.wt("hh_n"), cols(g.H, c), start=True, stop=True).then_inc(gates_ps, 1)

        @block.scalar
        def _(act):
            act.wait_ge(bias_done, 2)
            for c in range(NCH + 1):
                if c < NCH:
                    b = 4 * (c % 2)
                    act.wait_ge(gates_ps, c + 1)
                    act.activation(cols(g.S1, c), bank(g, b), ACT.Sigmoid, bias=g.bsum[:, 0:1]).then_inc(r_done, 1)
                    act.activation(cols(g.S2, c), bank(g, b + 1), ACT.Sigmoid, bias=g.bsum[:, 1:2]).then_inc(z_done, 1)
                if c:
                    act.wait_ge(pre_done, c)
                    act.activation(cols(g.S3, c - 1), cols(g.S3, c - 1), ACT.Tanh).then_inc(n_done, 1)

        @block.vector
        def _(dve):
            dve.tensor_tensor(g.bsum[:, 0:1], g.bt("bih_r"), g.bt("bhh_r"), ALU.add).then_inc(bias_done, 1)
            dve.tensor_tensor(g.bsum[:, 1:2], g.bt("bih_z"), g.bt("bhh_z"), ALU.add).then_inc(bias_done, 1)
            for c in range(NCH + 1):
                if c < NCH:
                    b = 4 * (c % 2)
                    dve.wait_ge(r_done, c + 1)
                    dve.scalar_tensor_tensor(out=cols(g.S1, c), in0=bank(g, b + 3), scalar=g.bt("bhh_n"),
                                             in1=cols(g.S1, c), op0=ALU.add, op1=ALU.mult).then_inc(rn_done, 1)
                    dve.wait_ge(rn_done, c + 1)
                    dve.scalar_tensor_tensor(out=cols(g.S3, c), in0=bank(g, b + 2), scalar=g.bt("bih_n"),
                                             in1=cols(g.S1, c), op0=ALU.add, op1=ALU.add).then_inc(pre_done, 1)
                if c:
                    p = c - 1
                    dve.wait_ge(n_done, c)
                    dve.tensor_tensor(cols(g.S1, p), cols(g.H, p), cols(g.S3, p), ALU.subtract).then_inc(diff_done, 1)
                    dve.wait_ge(diff_done, c)
                    dve.wait_ge(z_done, c)
                    dve.tensor_tensor(cols(g.S2, p), cols(g.S2, p), cols(g.S1, p), ALU.mult).then_inc(prod_done, 1)
                    dve.wait_ge(prod_done, c)
                    dve.tensor_tensor(cols(g.H, p), cols(g.S3, p), cols(g.S2, p), ALU.add).then_inc(h_done, 1)


def gate_phase(nc, g, sem):
    out_ps, gate_done, prod_done = sem("out_ps"), sem("gate_done"), sem("prod_done")
    norm = Norm(g, sem)
    with nc.Block() as block:
        @block.tensor
        def _(pe):
            for c in range(NCH):
                b = 2 * (c % 4)
                if c >= 4:
                    pe.wait_ge(prod_done, c - 3)
                pe.matmul(bank(g, b), g.wt("iw_h"), cols(g.H, c), start=True, stop=False)
                pe.matmul(bank(g, b), g.wt("iw_f"), cols(g.X, c), start=False, stop=True)
                pe.matmul(bank(g, b + 1), g.wt("jw"), cols(g.H, c), start=True, stop=True).then_inc(out_ps, 1)
            pe.wait_ge(prod_done, NCH)
            norm.tensor(pe)

        @block.scalar
        def _(act):
            for c in range(NCH):
                act.wait_ge(out_ps, c + 1)
                act.activation(cols(g.S1, c), bank(g, 2 * (c % 4)), ACT.Sigmoid, bias=g.bt("ib")).then_inc(gate_done, 1)
            norm.scalar(act)

        @block.vector
        def _(dve):
            for c in range(NCH):
                dve.wait_ge(gate_done, c + 1)
                dve.scalar_tensor_tensor(out=cols(g.S2, c), in0=bank(g, 2 * (c % 4) + 1), scalar=g.bt("jb"),
                                         in1=cols(g.S1, c), op0=ALU.add, op1=ALU.mult).then_inc(prod_done, 1)
                dve.wait_ge(prod_done, c + 1)
                dve.tensor_tensor(cols(g.S3, c), cols(g.X, c), cols(g.S2, c), ALU.add).then_inc(norm.ready, 1)
            norm.vector(dve)


def gin_phase(nc, g, sem, first):
    deg_max, deg_done, mean_done, in_done, a_ps, a_done, b_ps, b_done = (
        sem(s) for s in ("deg_max", "deg_done", "mean_done", "in_done", "a_ps", "a_done", "b_ps", "b_done"))
    norm = None if first else Norm(g, sem)
    wa, wb, ba, bb = ("w1a", "w1b", "b1a", "b1b") if first else ("w2a", "w2b", "b2a", "b2b")
    f = g.X if first else g.H
    with nc.Block() as block:
        @block.tensor
        def _(pe):
            for c in range(NCH):
                pe.wait_ge(in_done, c + 1)
                pe.matmul(bank(g, c), g.wt(wa), cols(g.S1, c), start=True, stop=True).then_inc(a_ps, 1)
            for c in range(NCH):
                pe.wait_ge(a_done, c + 1)
                pe.matmul(bank(g, c), g.wt(wb), cols(g.S2, c), start=True, stop=True).then_inc(b_ps, 1)
            if not first:
                norm.tensor(pe)

        @block.scalar
        def _(act):
            for c in range(NCH):
                act.wait_ge(a_ps, c + 1)
                act.activation(cols(g.S2, c), bank(g, c), ACT.Identity, bias=g.bt(ba)).then_inc(a_done, 1)
            for c in range(NCH):
                act.wait_ge(b_ps, c + 1)
                act.activation(cols(g.H, c), bank(g, c), ACT.Relu, bias=g.bt(bb)).then_inc(b_done, 1)
            if not first:
                norm.scalar(act)

        @block.vector
        def _(dve):
            if first:
                for c in range(NCH):
                    dve.tensor_scalar(cols(g.rdeg, c), cols(g.rdeg, c), 1.0, None, ALU.max).then_inc(deg_max, 1)
                for c in range(NCH):
                    dve.wait_ge(deg_max, c + 1)
                    dve.reciprocal(cols(g.rdeg, c), cols(g.rdeg, c)).then_inc(deg_done, 1)
            for c in range(NCH):
                if first:
                    dve.wait_ge(deg_done, c + 1)
                dve.tensor_tensor(cols(g.S1, c), cols(g.acc, c), cols(g.rdeg, c), ALU.mult).then_inc(mean_done, 1)
                dve.wait_ge(mean_done, c + 1)
                dve.tensor_tensor(cols(g.S1, c), cols(g.S1, c), cols(f, c), ALU.add).then_inc(in_done, 1)
            if not first:
                for c in range(NCH):
                    dve.wait_ge(b_done, c + 1)
                    dve.tensor_tensor(cols(g.S3, c), cols(g.X, c), cols(g.H, c), ALU.add).then_inc(norm.ready, 1)
                norm.vector(dve)


def last_node_phase(nc, g, sem):
    res_ps, sum_done, relu_done, stored = sem("res_ps"), sem("sum_done"), sem("relu_done"), sem("stored")
    norm = Norm(g, sem)
    with nc.Block() as block:
        @block.tensor
        def _(pe):
            for c in range(NCH):
                pe.matmul(bank(g, c), g.wt("wres"), cols(g.X, c), start=True, stop=True).then_inc(res_ps, 1)
            norm.tensor(pe)

        @block.scalar
        def _(act):
            for c in range(NCH):
                act.wait_ge(sum_done, c + 1)
                act.activation(cols(g.S2, c), cols(g.S1, c), ACT.Relu, bias=g.bt("bres")).then_inc(relu_done, 1)
            norm.scalar(act)

        @block.vector
        def _(dve):
            for c in range(NCH):
                dve.wait_ge(res_ps, c + 1)
                dve.tensor_tensor(cols(g.S1, c), cols(g.acc, c), bank(g, c), ALU.add).then_inc(sum_done, 1)
            for c in range(NCH):
                dve.wait_ge(relu_done, c + 1)
                dve.tensor_tensor(cols(g.S3, c), cols(g.X, c), cols(g.S2, c), ALU.add).then_inc(norm.ready, 1)
            norm.vector(dve)

        @block.sync
        def _(sp):
            sp.wait_ge(norm.x_done, NCH)
            sp.dma_start(g.out, g.X[:, :]).then_inc(stored, 16)
            sp.wait_ge(stored, 16)


def build(nc, d, out):
    g = Shared()
    with ExitStack() as ctx:
        def sb(name, shape, dt=F32):
            return ctx.enter_context(nc.sbuf_tensor(name, shape, dt))

        g.x, g.src, g.dst, g.ety = d["x"], d["src"], d["dst"], d["etype"]
        g.ewt = d["eweight"]
        g.src_pt, g.dst_pt, g.ewt_pt = d["src_pt"], d["dst_pt"], d["eweight_pt"]
        g.d_attrT, g.d_w, g.d_b, g.d_brow, g.d_xT, g.out = d["attrT"], d["w"], d["b"], d["brow"], d["xT"], out
        t_types = nc.dram_tensor("t_types", (K * N, D), F32, kind="Internal").ap()
        t_feats = nc.dram_tensor("t_feats", (N, D), F32, kind="Internal").ap()
        g.t_mats = nc.dram_tensor("t_mats", (NT * TN, NBL * TN), BF16, kind="Internal").ap()
        g.t_tmats = nc.dram_tensor("t_tmats", (NT * TN, NBL * K * TN), F16, kind="Internal").ap()
        t_gated = nc.dram_tensor("t_gated", (N, 2 * D), F32, kind="Internal").ap()

        g.X, g.H, g.acc, g.rdeg = sb("X", [P, NP]), sb("H", [P, NP]), sb("acc", [P, NP]), sb("rdeg", [P, NP])
        g.S1, g.S2, g.S3 = sb("S1", [P, NP]), sb("S2", [P, NP]), sb("S3", [P, NP])
        g.w, g.b, g.brow = sb("w", [P, len(WNAMES) * D]), sb("b", [P, len(BNAMES)]), sb("brow", [P, len(RNAMES) * D])
        g.wt = lambda n: g.w[:, WNAMES.index(n) * D:(WNAMES.index(n) + 1) * D]
        g.bt = lambda n: g.b[:, BNAMES.index(n):BNAMES.index(n) + 1]
        g.bsum, g.epst = sb("bsum", [P, 2]), sb("epst", [P, 1])
        g.ident, g.ones, g.onesd = sb("ident", [P, P]), sb("ones", [P, P]), sb("onesd", [P, P])
        g.iota1, g.eidx = sb("iota1", [P, TN]), sb("eidx", [P, W])
        shape = [P, RMAXN + 1, NT]
        g.wstart, g.wfirst, g.wnode = sb("wstart", shape, I32), sb("wfirst", shape), sb("wnode", shape)
        g.rounds = sb("rounds", [P, 1], I32)
        g.rawi, g.meta, g.mask, g.tmpw = sb("rawi", [P, P], I32), sb("meta", [P, P]), sb("mask", [P, W]), sb("tmpw", [P, W])
        g.dcol, g.gidx = sb("dcol", [P, 2 * W]), sb("gidx", [P, 2 * W], I32)
        g.gnow = sb("gnow", [P, W], I32)
        g.rows, g.oh, g.ohT = sb("rows", [P, RING, 2 * D]), sb("oh", [P, RING, TN]), sb("ohT", [P, 2, P])
        g.attr, g.C = sb("attr", [P, 2, RING * P]), sb("C", [P, NT * D])
        g.pre, g.sig, g.msg = sb("pre", [P, 4, D]), sb("sig", [P, 4, D]), sb("msg", [P, 4, D])
        g.lt = sb("lt", [P, TU, TN])
        g.rowbuf = g.rows[:, 0:2 * TU, :].rearrange("p (u h) d -> p u (h d)", h=2)
        g.dblk = sb("dblk", [P, BR * BC], I32)
        g.ov = g.S1[:, 0:NT * BR].rearrange("p (a b) -> p a b", b=BR)
        g.c2 = g.S2[:, 0:NT * BR].rearrange("p (a b) -> p a b", b=BR)
        g.c3 = g.S3[:, 0:(RMAXN + 1) * NT].rearrange("p (a b) -> p a b", b=NT)
        g.blk, g.bmin, g.bmax = sb("blk", [P, BR]), sb("bmin", [P, BR]), sb("bmax", [P, BR])
        g.dtlo, g.rnd = sb("dtlo", [P, NT]), sb("rnd", [P, RMAXN + 1])
        g.part, g.red, g.lo, g.span = sb("part", [P, 2 * NT]), sb("red", [P, 2 * NT]), sb("lo", [P, NT]), sb("span", [P, 1])
        g.raww, g.wi = sb("raww", [P, P]), sb("wi", [P, NB_S], I32)
        g.wk, g.wk2 = sb("wk", [P, 17 * W]), sb("wk2", [P, 2 * NB_S])
        g.cur = sb("cur", [P, 3 * NB_S])
        g.diff, g.before, g.nbefore = sb("diff", [P, P]), sb("before", [P, P]), sb("nbefore", [P, P])
        g.iotaf, g.iotah, g.ones16 = sb("iotaf", [P, P]), sb("iotah", [P, 512], F16), sb("ones16", [P, P], F16)
        g.flags, g.path = sb("flags", [P, 7]), sb("path", [P, 3], I32)
        n = NT * NB_S
        g.t_src, g.t_code = g.C[:, 0:n], g.C[:, n:2 * n]
        g.t_dst, g.t_w = g.attr[:, 1, 0:n], g.attr[:, 0, 900:900 + n]
        g.parts = [t[:, 0:NT * D // 2] for t in (g.S1, g.S2, g.S3)]
        g.ps = ctx.enter_context(nc.psum_tensor("ps", [P, 8, 512], F32))
        g.rows_in = [ctx.enter_context(nc.semaphore(f"rows_in{i}")) for i in range(RING)]
        sem = Sems(nc, ctx)
        setup_phase(nc, g, sem)
        sem.clear()
        sort_phase(nc, g, sem)
        sem.clear()
        scatter_phase(nc, g, sem)
        sem.clear()
        dense_weighted_phase(nc, g, sem)
        sem.clear()
        first_node_phase(nc, g, sem)
        sem.clear()
        types = t_types.rearrange("(k n) f -> n k f", k=K)
        for step in range(3):
            table_phase(nc, g, sem, g.H, g.w[:, D:(1 + K) * D], g.brow, K * D, lambda n: types[n, :, :])
            sem.clear()
            edge_phase(nc, g, sem, "L1", t_types, D, step, deg=(step == 0))
            sem.clear()
            split_phase(nc, g, sem, g.H, F16, 2)
            sem.clear()
            (dense_typed_stored_phase if step else dense_typed_phase)(nc, g, sem)
            sem.clear()
            gru_phase(nc, g, sem)
            sem.clear()
        gate_phase(nc, g, sem)
        sem.clear()
        zero_row = g.brow[:, K * D:(K + 1) * D]
        for first in (True, False):
            table_phase(nc, g, sem, g.X if first else g.H, g.ident[:, :], zero_row, D, lambda n: t_feats[n, :])
            sem.clear()
            edge_phase(nc, g, sem, "L2", t_feats, D, 3 if first else 4)
            sem.clear()
            split_phase(nc, g, sem, g.X if first else g.H, BF16, 3)
            sem.clear()
            dense_stored_phase(nc, g, sem)
            sem.clear()
            gin_phase(nc, g, sem, first)
            sem.clear()
        w0 = WNAMES.index("wb") * D
        table_phase(nc, g, sem, g.X, g.w[:, w0:w0 + 3 * D], g.brow[:, K * D:(K + 3) * D], 3 * D,
                    lambda n: t_gated[n, :], cpart=True, general=False)
        sem.clear()
        edge_phase(nc, g, sem, "L3", t_gated, 2 * D, 5)
        sem.clear()
        last_node_phase(nc, g, sem)


def kernel(**inputs):
    import concourse.bacc as bacc
    from concourse.bass_utils import run_bass_kernel_spmd

    a = {k: np.asarray(v) for k, v in inputs.items()}
    wih, whh, wet, iw = a["L1_gnn_W_ih"], a["L1_gnn_W_hh"], a["L1_gnn_W_et"], a["L1_gnn_i_w"]
    blocks = [a["L0_gnn_social_weight"]] + [wet[k].T for k in range(K)]
    blocks += [wih[i * D:(i + 1) * D].T for i in range(3)] + [whh[i * D:(i + 1) * D].T for i in range(3)]
    blocks += [iw[:, :D].T, iw[:, D:].T, a["L1_gnn_j_w"].T]
    blocks += [a[f"L2_gnn_W{n}"].T for n in ("1a", "1b", "2a", "2b")]
    blocks += [a[f"L3_gnn_W{n}"] for n in ("B", "A", "C", "E", "res")]
    columns = [a["L1_gnn_b_ih"].reshape(3, D), a["L1_gnn_b_hh"].reshape(3, D), a["L1_gnn_i_b"][None],
               a["L1_gnn_j_b"][None]] + [a[f"L2_gnn_b{n}"][None] for n in ("1a", "1b", "2a", "2b")]
    columns += [a["L3_gnn_bres"][None]]
    rows = [a["L1_gnn_b_et"].reshape(-1), np.zeros(D, np.float32)] + [a[f"L3_gnn_b{n}"] for n in ("A", "B", "C", "E")]
    pad = lambda v: np.pad(v, (0, ET * P - E)).reshape(P, ET)
    xT = np.zeros((D, NP), np.float32)
    xT[:, :N] = a["x"].T
    arrays = {
        "x": a["x"], "xT": xT, "src": a["src"], "dst": a["dst"], "etype": a["edge_type_4"], "eweight": a["edge_weight"],
        "src_pt": pad(a["src"]), "dst_pt": pad(a["dst"]), "eweight_pt": pad(a["edge_weight"]),
        "attrT": np.ascontiguousarray(a["edge_attr_128"].T), "w": np.concatenate(blocks, axis=1),
        "b": np.ascontiguousarray(np.concatenate(columns, axis=0).T), "brow": np.concatenate(rows)[None],
    }
    nc = bacc.Bacc("TRN2", target_bir_lowering=False, num_devices=1)
    d = {k: nc.dram_tensor("in_" + k, v.shape, mybir.dt.from_np(v.dtype), kind="ExternalInput").ap()
         for k, v in arrays.items()}
    out = nc.dram_tensor("out_x", (D, NP), F32, kind="ExternalOutput").ap()
    build(nc, d, out)
    r = run_bass_kernel_spmd(nc, [{"in_" + k: v for k, v in arrays.items()}], core_ids=[0])
    return np.ascontiguousarray(r.results[0]["out_x"][:, :N].T)
```
